# Optimizing a Trainium2 kernel written in Bass

```python
import numpy as np
import jax
import jax.numpy as jnp

def _softmax(x, axis=-1):
    return jax.nn.softmax(x, axis=axis)

def _gelu(x):
    return jax.nn.gelu(x, approximate=True)

def _silu(x):
    return jax.nn.silu(x)

def _sigmoid(x):
    return jax.nn.sigmoid(x)

def _layernorm(x, axis=-1, eps=1e-05):
    m = jnp.mean(x, axis=axis, keepdims=True)
    v = jnp.var(x, axis=axis, keepdims=True)
    return (x - m) / jnp.sqrt(v + eps)

def _scatter_add(tgt, idx, src, axis=0):
    return tgt.at[idx].add(src)

def _segment_sum(src, seg, n):
    return jax.ops.segment_sum(src, seg, n)
kernel_name = 'mk_xattn_ffn_d2_seqx_r4_cfa015'

def setup_inputs(seed: int=0):
    np.random.seed(seed)
    _w = jnp.asarray

    def _rec_inputs():
        import jax
        import jax.numpy as jnp
        _rk = jax.random.key(seed)
        x = -0.0002928 + 1 * jax.random.normal(jax.random.fold_in(_rk, 1), (4, 512, 256), jnp.float32)
        _lenS = 512 - jax.random.randint(jax.random.fold_in(_rk, 7), (4,), 0, max(1, 512 // 4) + 1, jnp.int32)
        _lenS2 = 512 - jax.random.randint(jax.random.fold_in(_rk, 8), (4,), 0, max(1, 512 // 4) + 1, jnp.int32)
        _ctx_1024P = jax.random.normal(jax.random.fold_in(_rk, 11), (4, 16, 256), jnp.float32)
        _ctx_1024c = jax.random.dirichlet(jax.random.fold_in(_rk, 511), 0.3 * jnp.ones((16,), jnp.float32), (4, 512))
        _ctx_1024t = jnp.einsum('bsk,bkd->bsd', _ctx_1024c, _ctx_1024P)
        _ctx_1024t = _ctx_1024t * jax.lax.rsqrt(jnp.mean(jnp.square(_ctx_1024t)) + 1e-12) * 0.953939
        ctx_1024 = -1.39393e-06 + 0.999914 * (_ctx_1024t + 0.3 * jax.random.normal(jax.random.fold_in(_rk, 611), (4, 512, 256), jnp.float32))
        _validS = jnp.arange(512)[None, :] < _lenS[:, None]
        _validS2 = jnp.arange(512)[None, :] < _lenS2[:, None]
        _causal = jnp.tril(jnp.ones((512, 512), dtype=bool))
        mask_SxS2_bk1 = jnp.broadcast_to(_validS2[0:1, :], (512, 512))
        return (x, ctx_1024, mask_SxS2_bk1)
    x, ctx_1024, mask_SxS2_bk1 = _rec_inputs()

    def _L0_xattn_setup():
        import jax, jax.numpy as jnp
        import numpy as np
        D_MODEL = 256
        NHEAD = 16
        HEAD_DIM = D_MODEL // NHEAD
        B, SQ, SK = (2, 512, 512)
        key = jax.random.key(seed)
        ks = jax.random.split(key, 12)
        s = 0.02
        inp = {'q': jax.random.normal(ks[0], (B, SQ, D_MODEL), jnp.float32), 'k': jax.random.normal(ks[1], (B, SK, D_MODEL), jnp.float32), 'v': jax.random.normal(ks[2], (B, SK, D_MODEL), jnp.float32), 'causal_mask': jnp.triu(jnp.ones((SQ, SK), jnp.bool_), k=1), 'Wq': jax.random.normal(ks[3], (D_MODEL, D_MODEL), jnp.float32) * s, 'bq': jnp.zeros((D_MODEL,), jnp.float32), 'Wk': jax.random.normal(ks[4], (D_MODEL, D_MODEL), jnp.float32) * s, 'bk': jnp.zeros((D_MODEL,), jnp.float32), 'Wv': jax.random.normal(ks[5], (D_MODEL, D_MODEL), jnp.float32) * s, 'bv': jnp.zeros((D_MODEL,), jnp.float32), 'Wo': jax.random.normal(ks[6], (D_MODEL, D_MODEL), jnp.float32) * s, 'bo': jnp.zeros((D_MODEL,), jnp.float32)}
        return inp
    _L0_xattn_all = _L0_xattn_setup()
    _L0_xattn_in = {k: v for k, v in _L0_xattn_all.items() if k in ('Wq', 'bq', 'Wk', 'bk', 'Wv', 'bv', 'Wo', 'bo')}
    del _L0_xattn_all

    def _L0_ffn_setup():
        import jax, jax.numpy as jnp
        import numpy as np
        B, S, D, F, E = (4, 512, 256, 1024, 8)
        key = jax.random.key(seed)
        ks = jax.random.split(key, 7)
        s1 = 1.0 / np.sqrt(D)
        s2 = 1.0 / np.sqrt(F)
        x = jax.random.normal(ks[0], (B, S, D), dtype=jnp.float32)
        W1 = jax.random.uniform(ks[1], (E, D, F), jnp.float32, -s1, s1)
        b1 = jax.random.uniform(ks[2], (E, F), jnp.float32, -s1, s1)
        W2 = jax.random.uniform(ks[3], (E, F, D), jnp.float32, -s2, s2)
        b2 = jax.random.uniform(ks[4], (E, D), jnp.float32, -s2, s2)
        Wr = jax.random.uniform(ks[5], (D, E), jnp.float32, -s1, s1)
        br = jax.random.uniform(ks[6], (E,), jnp.float32, -s1, s1)
        return {'x': x, 'W1': W1, 'b1': b1, 'W2': W2, 'b2': b2, 'Wr': Wr, 'br': br}
    _L0_ffn_all = _L0_ffn_setup()
    _L0_ffn_in = {k: v for k, v in _L0_ffn_all.items() if k in ('W1', 'b1', 'W2', 'b2', 'Wr', 'br')}
    del _L0_ffn_all

    def _L1_xattn_setup():
        import jax, jax.numpy as jnp
        import numpy as np
        H, DK, DV = (16, 64, 64)
        MEM = 128
        D_MODEL = 256
        OUT_DIM = 256
        key = jax.random.key(seed)
        ks = jax.random.split(key, 12)
        B, S = (2, 512)
        scale = 1.0 / np.sqrt(D_MODEL)
        inp = {'queries': jax.random.normal(ks[0], (B, S, D_MODEL), jnp.float32), 'keys': jax.random.normal(ks[1], (B, S, D_MODEL), jnp.float32), 'values': jax.random.normal(ks[2], (B, S, D_MODEL), jnp.float32), 'wq_w': jax.random.normal(ks[3], (D_MODEL, H * DK), jnp.float32) * scale, 'wq_b': jnp.zeros((H * DK,), jnp.float32), 'wk_w': jax.random.normal(ks[4], (D_MODEL, H * DK), jnp.float32) * scale, 'wk_b': jnp.zeros((H * DK,), jnp.float32), 'wv_w': jax.random.normal(ks[5], (D_MODEL, H * DV), jnp.float32) * scale, 'wv_b': jnp.zeros((H * DV,), jnp.float32), 'mk': jax.random.normal(ks[6], (1, MEM, H * DK), jnp.float32) * (0.1 / DK), 'mv': jax.random.normal(ks[7], (1, MEM, H * DV), jnp.float32) * (0.1 / MEM), 'wo_w': jax.random.normal(ks[8], (H * DV, OUT_DIM), jnp.float32) * (1.0 / np.sqrt(H * DV)), 'wo_b': jnp.zeros((OUT_DIM,), jnp.float32)}
        return inp
    _L1_xattn_all = _L1_xattn_setup()
    _L1_xattn_in = {k: v for k, v in _L1_xattn_all.items() if k in ('wq_w', 'wq_b', 'wk_w', 'wk_b', 'wv_w', 'wv_b', 'mk', 'mv', 'wo_w', 'wo_b')}
    del _L1_xattn_all

    def _L1_ffn_setup():
        import jax, jax.numpy as jnp
        import numpy as np
        GROUP = 16
        EPS = 1e-05

        def _dequant(q, scale):
            w = q.astype(jnp.float32) / 7.5 - 1.0
            return w * jnp.repeat(scale, GROUP, axis=1)

        def _qlora_linear(x, q, scale, bias, la, lb):
            w = _dequant(q, scale)
            base = jnp.einsum('btd,od->bto', x, w) + bias
            lora = jnp.einsum('btr,or->bto', jnp.einsum('btd,rd->btr', x, la), lb)
            return base + lora

        def _layernorm(x, g, b):
            mu = jnp.mean(x, axis=-1, keepdims=True)
            var = jnp.mean(jnp.square(x - mu), axis=-1, keepdims=True)
            return (x - mu) * jax.lax.rsqrt(var + EPS) * g + b
        key = jax.random.key(seed)
        ks = jax.random.split(key, 6)
        D, R, B, T = (256, 32, 8, 1024)
        x = jax.random.normal(ks[0], (B, T, D), dtype=jnp.float32)
        qweights = jax.random.randint(ks[1], (6, D, D), 0, 16, dtype=jnp.int32)
        scales = jax.random.uniform(ks[2], (6, D, D // GROUP), dtype=jnp.float32)
        biases = jax.random.normal(ks[3], (6, D), dtype=jnp.float32) * 0.02
        lora_a = jax.random.normal(ks[4], (6, R, D), dtype=jnp.float32) * 0.02
        lora_b = jax.random.normal(ks[5], (6, D, R), dtype=jnp.float32) * 0.02
        ln_gamma = jnp.ones((3, D), dtype=jnp.float32)
        ln_beta = jnp.zeros((3, D), dtype=jnp.float32)
        return {'x': x, 'qweights': qweights, 'scales': scales, 'biases': biases, 'lora_a': lora_a, 'lora_b': lora_b, 'ln_gamma': ln_gamma, 'ln_beta': ln_beta}
    _L1_ffn_all = _L1_ffn_setup()
    _L1_ffn_in = {k: v for k, v in _L1_ffn_all.items() if k in ('qweights', 'scales', 'biases', 'lora_a', 'lora_b', 'ln_gamma', 'ln_beta')}
    del _L1_ffn_all
    return {'x': x, 'ctx_1024': ctx_1024, 'mask_SxS2_bk1': mask_SxS2_bk1, 'L0_xattn_Wq': _L0_xattn_in['Wq'], 'L0_xattn_bq': _L0_xattn_in['bq'], 'L0_xattn_Wk': _L0_xattn_in['Wk'], 'L0_xattn_bk': _L0_xattn_in['bk'], 'L0_xattn_Wv': _L0_xattn_in['Wv'], 'L0_xattn_bv': _L0_xattn_in['bv'], 'L0_xattn_Wo': _L0_xattn_in['Wo'], 'L0_xattn_bo': _L0_xattn_in['bo'], 'L0_ffn_W1': _L0_ffn_in['W1'], 'L0_ffn_b1': _L0_ffn_in['b1'], 'L0_ffn_W2': _L0_ffn_in['W2'], 'L0_ffn_b2': _L0_ffn_in['b2'], 'L0_ffn_Wr': _L0_ffn_in['Wr'], 'L0_ffn_br': _L0_ffn_in['br'], 'L1_xattn_wq_w': _L1_xattn_in['wq_w'], 'L1_xattn_wq_b': _L1_xattn_in['wq_b'], 'L1_xattn_wk_w': _L1_xattn_in['wk_w'], 'L1_xattn_wk_b': _L1_xattn_in['wk_b'], 'L1_xattn_wv_w': _L1_xattn_in['wv_w'], 'L1_xattn_wv_b': _L1_xattn_in['wv_b'], 'L1_xattn_mk': _L1_xattn_in['mk'], 'L1_xattn_mv': _L1_xattn_in['mv'], 'L1_xattn_wo_w': _L1_xattn_in['wo_w'], 'L1_xattn_wo_b': _L1_xattn_in['wo_b'], 'L1_ffn_qweights': _L1_ffn_in['qweights'], 'L1_ffn_scales': _L1_ffn_in['scales'], 'L1_ffn_biases': _L1_ffn_in['biases'], 'L1_ffn_lora_a': _L1_ffn_in['lora_a'], 'L1_ffn_lora_b': _L1_ffn_in['lora_b'], 'L1_ffn_ln_gamma': _L1_ffn_in['ln_gamma'], 'L1_ffn_ln_beta': _L1_ffn_in['ln_beta']}

def reference(x, ctx_1024, mask_SxS2_bk1, L0_xattn_Wq, L0_xattn_bq, L0_xattn_Wk, L0_xattn_bk, L0_xattn_Wv, L0_xattn_bv, L0_xattn_Wo, L0_xattn_bo, L0_ffn_W1, L0_ffn_b1, L0_ffn_W2, L0_ffn_b2, L0_ffn_Wr, L0_ffn_br, L1_xattn_wq_w, L1_xattn_wq_b, L1_xattn_wk_w, L1_xattn_wk_b, L1_xattn_wv_w, L1_xattn_wv_b, L1_xattn_mk, L1_xattn_mv, L1_xattn_wo_w, L1_xattn_wo_b, L1_ffn_qweights, L1_ffn_scales, L1_ffn_biases, L1_ffn_lora_a, L1_ffn_lora_b, L1_ffn_ln_gamma, L1_ffn_ln_beta):
    import jax
    import jax.numpy as jnp

    def _L0_xattn_ref(q, k, v, causal_mask, Wq, bq, Wk, bk, Wv, bv, Wo, bo):
        import jax, jax.numpy as jnp
        import numpy as np
        D_MODEL = 256
        NHEAD = 16
        HEAD_DIM = D_MODEL // NHEAD
        B, SQ, SK = (2, 512, 512)
        Bq, Sq, D = q.shape
        Sk = k.shape[1]
        H, Dh = (NHEAD, HEAD_DIM)
        scale = Dh ** (-0.5)
        qh = (q @ Wq.T + bq).reshape(Bq, Sq, H, Dh).transpose(0, 2, 1, 3)
        kh = (k @ Wk.T + bk).reshape(Bq, Sk, H, Dh).transpose(0, 2, 1, 3)
        vh = (v @ Wv.T + bv).reshape(Bq, Sk, H, Dh).transpose(0, 2, 1, 3)
        attn = jnp.einsum('bhqd,bhkd->bhqk', qh, kh) * scale
        attn = jnp.where(causal_mask[None, None, :, :], -jnp.inf, attn)
        attn = jax.nn.softmax(attn, axis=-1)
        out = jnp.einsum('bhqk,bhkd->bhqd', attn, vh)
        out = out.transpose(0, 2, 1, 3).reshape(Bq, Sq, D)
        return out @ Wo.T + bo

    def _L0_ffn_ref(x, W1, b1, W2, b2, Wr, br):
        import jax, jax.numpy as jnp
        import numpy as np
        B, S, D, F, E = (4, 512, 256, 1024, 8)
        b, s, d = x.shape
        e = Wr.shape[1]
        logits = x @ Wr + br
        idx = jnp.argmax(logits, axis=-1)
        probs = jax.nn.softmax(logits, axis=-1)
        gates = jnp.take_along_axis(probs, idx[..., None], axis=-1)[..., 0]
        xf = x.reshape(-1, d)
        idxf = idx.reshape(-1)
        gf = gates.reshape(-1)
        out = jnp.zeros_like(xf)
        for ei in range(e):
            h = jax.nn.gelu(xf @ W1[ei] + b1[ei], approximate=False)
            y = h @ W2[ei] + b2[ei]
            mask = (idxf == ei).astype(xf.dtype)
            out = out + y * (gf * mask)[:, None]
        return out.reshape(b, s, d)

    def _L1_xattn_ref(queries, keys, values, wq_w, wq_b, wk_w, wk_b, wv_w, wv_b, mk, mv, wo_w, wo_b):
        import jax, jax.numpy as jnp
        import numpy as np
        H, DK, DV = (16, 64, 64)
        MEM = 128
        D_MODEL = 256
        OUT_DIM = 256
        B, S, _ = queries.shape
        q = (queries @ wq_w + wq_b).reshape(B, S, H, DK).transpose(0, 2, 1, 3)
        k_proj = keys @ wk_w + wk_b
        v_proj = values @ wv_w + wv_b
        k_ext = jnp.concatenate([k_proj, jnp.broadcast_to(mk, (B, MEM, H * DK))], axis=1)
        v_ext = jnp.concatenate([v_proj, jnp.broadcast_to(mv, (B, MEM, H * DV))], axis=1)
        T = S + MEM
        k = k_ext.reshape(B, T, H, DK).transpose(0, 2, 1, 3)
        v = v_ext.reshape(B, T, H, DV).transpose(0, 2, 1, 3)
        scores = jnp.einsum('bhsd,bhtd->bhst', q, k) / jnp.sqrt(jnp.float32(DK))
        attn = jax.nn.softmax(scores, axis=-1)
        out = jnp.einsum('bhst,bhtd->bhsd', attn, v)
        out = out.transpose(0, 2, 1, 3).reshape(B, S, H * DV)
        return out @ wo_w + wo_b

    def _L1_ffn_ref(x, qweights, scales, biases, lora_a, lora_b, ln_gamma, ln_beta):
        import jax, jax.numpy as jnp
        import numpy as np
        GROUP = 16
        EPS = 1e-05

        def _dequant(q, scale):
            w = q.astype(jnp.float32) / 7.5 - 1.0
            return w * jnp.repeat(scale, GROUP, axis=1)

        def _qlora_linear(x, q, scale, bias, la, lb):
            w = _dequant(q, scale)
            base = jnp.einsum('btd,od->bto', x, w) + bias
            lora = jnp.einsum('btr,or->bto', jnp.einsum('btd,rd->btr', x, la), lb)
            return base + lora

        def _layernorm(x, g, b):
            mu = jnp.mean(x, axis=-1, keepdims=True)
            var = jnp.mean(jnp.square(x - mu), axis=-1, keepdims=True)
            return (x - mu) * jax.lax.rsqrt(var + EPS) * g + b
        h = x
        for blk in range(3):
            i0, i1 = (2 * blk, 2 * blk + 1)
            y = _qlora_linear(h, qweights[i0], scales[i0], biases[i0], lora_a[i0], lora_b[i0])
            y = _layernorm(y, ln_gamma[blk], ln_beta[blk])
            y = jax.nn.gelu(y, approximate=False)
            y = _qlora_linear(y, qweights[i1], scales[i1], biases[i1], lora_a[i1], lora_b[i1])
            h = y + h
        return h
    x = x + _L0_xattn_ref(_layernorm(x, axis=-1), ctx_1024, ctx_1024, mask_SxS2_bk1, L0_xattn_Wq, L0_xattn_bq, L0_xattn_Wk, L0_xattn_bk, L0_xattn_Wv, L0_xattn_bv, L0_xattn_Wo, L0_xattn_bo)
    x = x + _L0_ffn_ref(_layernorm(x, axis=-1), L0_ffn_W1, L0_ffn_b1, L0_ffn_W2, L0_ffn_b2, L0_ffn_Wr, L0_ffn_br)
    x = x + _L1_xattn_ref(_layernorm(x, axis=-1), ctx_1024, ctx_1024, L1_xattn_wq_w, L1_xattn_wq_b, L1_xattn_wk_w, L1_xattn_wk_b, L1_xattn_wv_w, L1_xattn_wv_b, L1_xattn_mk, L1_xattn_mv, L1_xattn_wo_w, L1_xattn_wo_b)
    x = x + _L1_ffn_ref(_layernorm(x, axis=-1), L1_ffn_qweights, L1_ffn_scales, L1_ffn_biases, L1_ffn_lora_a, L1_ffn_lora_b, L1_ffn_ln_gamma, L1_ffn_ln_beta)
    return x

_drawn_inputs = setup_inputs


def setup_inputs(seed=0):
    import zlib

    import numpy as np

    out = dict(_drawn_inputs(seed))
    spreads = {'L0_xattn_bq': (0.0, 0.8),
     'L0_xattn_bk': (0.0, 0.8),
     'L0_xattn_bv': (0.0, 0.1),
     'L0_xattn_bo': (0.0, 0.1),
     'L1_xattn_wq_b': (0.0, 0.448),
     'L1_xattn_wk_b': (0.0, 0.8),
     'L1_xattn_wv_b': (0.0, 0.1),
     'L1_xattn_wo_b': (0.0, 0.1),
     'L1_ffn_ln_gamma': (1.0, 0.2),
     'L1_ffn_ln_beta': (0.0, 0.1)}
    factors = {'L0_xattn_Wq': 8.0,
     'L0_xattn_Wk': 8.0,
     'L0_ffn_b1': 8.0,
     'L0_ffn_b2': 8.0,
     'L0_ffn_br': 4.438,
     'L1_xattn_mk': 8.0,
     'L1_xattn_mv': 8.0,
     'L1_ffn_biases': 7.918,
     'L1_ffn_lora_a': 4.787,
     'L1_ffn_lora_b': 4.796}
    for name, (base, spread) in spreads.items():
        noise = np.random.default_rng([zlib.crc32(name.encode()), seed]).standard_normal(out[name].shape)
        drawn = base * np.exp(spread * noise) if base else spread * noise
        out[name] = jnp.asarray(drawn.astype(out[name].dtype))
    for name, factor in factors.items():
        out[name] = (out[name] * factor).astype(out[name].dtype)
    return out
```

```python
from contextlib import ExitStack

import concourse.bass as bass
from concourse import mybir

F32 = mybir.dt.float32
F32R = mybir.dt.float32r
BF16 = mybir.dt.bfloat16
I32 = mybir.dt.int32
U32 = mybir.dt.uint32
U8 = mybir.dt.uint8
ALU = mybir.AluOpType
ACT = mybir.ActivationFunctionType
AX = mybir.AxisListType.X

P = 128
B, S, D = 4, 512, 256
NT = S // P
DC = D // P
N_TILES = B * NT
EPS = 1e-5

H0, DH0 = 16, 16
SLOT = 32
G0 = P // SLOT
NG0 = H0 // G0
ROWS0 = 3 * DH0 + 1
MASKED = 2.0 ** 120


H1, DK = 16, 64
MEM = P
PAIRS = H1 // 2
KT1 = NT + 1

NLIN, LR, GROUP = 6, 32, 16

E, FF = 8, 1024
FC = FF // P
CT = 256
TT = CT // P
TILES = B * S // CT + E - 1
RING = 3
assert TILES % RING == 0


class Count:

    def __init__(self, sem, per):
        self.sem, self.per = sem, per

    def wait(self, eng, b, n):
        assert n > 0
        eng.wait_ge(self.sem, b * self.per + n)

    def value(self, eng, b, n):
        assert n > 0
        return eng.to_reg(b * self.per + n)

    def wait_apart(self, eng, b, n, met, at):
        value = eng.to_reg(b * self.per + n)
        eng.wait_ge(met, at)
        eng.wait_ge(self.sem, value)


def attention0(nc, x_all, A):
    with ExitStack() as ctx:
        def sb(name, shape, dt=F32):
            return ctx.enter_context(nc.sbuf_tensor("a0_" + name, shape, dt))

        def ps(name, shape, dt=F32):
            return ctx.enter_context(nc.psum_tensor("a0_" + name, shape, dt))

        def sem(name):
            return ctx.enter_context(nc.semaphore("a0_" + name))

        wq, wk = sb("wq", [P, DC, D]), sb("wk", [P, DC, D])
        wv = sb("wv", [P, DC, H0 * SLOT])
        wo = sb("wo", [P, NG0, D])
        bv = sb("bv", [P, H0 * SLOT])
        bo = sb("bo", [P, D])
        bqk = sb("bqk", [P, 2, 2])
        ident = sb("ident", [P, P])
        ident_b = sb("ident_b", [P, P], BF16)
        spread = sb("spread", [P, P])
        mask_in = sb("mask_in", [P, 2, NT, S], U8)
        bias_q = sb("bias_q", [P, NT, S], BF16)
        bias_k = sb("bias_k", [P, NT, S], BF16)
        least_masked = sb("least_masked", [P, NT])
        nan_row = sb("nan_row", [P, NT])
        ctx_t = sb("ctx_t", [P, DC, S])
        xn = sb("xn", [P, NT, D])
        xn_t = sb("xn_t", [P, DC, S])
        stats = sb("stats", [P, NT, 6])
        mean_var = sb("mean_var", [P, NT, 2])
        rstd = sb("rstd", [P, NT])
        minus_half = sb("minus_half", [P, NT])
        full = sb("full", [P, 2, S])
        hi = sb("hi", [P, 4, S], F32R)
        lo = sb("lo", [P, 4, S], F32R)
        q_stack = sb("q_stack", [ROWS0, H0, S], F32R)
        k_stack = sb("k_stack", [ROWS0, H0, S], F32R)
        v = sb("v", [P, NT, H0 * SLOT])
        probs = sb("probs", [P, 4, 2, S])
        scratch = sb("scratch", [P, 2, S], BF16)
        mx = sb("mx", [P, G0 * NT])
        neg_max = sb("neg_max", [G0 * NT, P], F32R)
        o_raw = sb("o_raw", [P, S])
        recip = sb("recip", [P, S])
        o_norm = sb("o_norm", [P, NG0, S])

        p_s = ps("p_s", [P, 2, 2, S])
        p_m = ps("p_m", [P, 2, S])
        p_o = ps("p_o", [P, S])

        M_USES = NT + 4 + NT + H0 * NT + NG0 + NG0 + NT
        assert M_USES % 2 == 0
        loaded = sem("loaded")
        consts = sem("consts")
        prep = sem("prep")
        ctx_in = Count(sem("ctx_in"), 16)
        stats_done = Count(sem("stats_done"), 3)
        rstd_ready = Count(sem("rstd_ready"), 1)
        xn_ready = Count(sem("xn_ready"), 1)
        m_full = Count(sem("m_full"), M_USES)
        m_free = Count(sem("m_free"), M_USES)
        hi_ready = Count(sem("hi_ready"), 4)
        split_ready = Count(sem("split_ready"), 4)
        stacked = Count(sem("stacked"), 16 * 12)
        nm_ready = Count(sem("nm_ready"), NG0)
        nm_in = Count(sem("nm_in"), 16 * NG0)
        s_full = Count(sem("s_full"), NG0 * 8)
        exp_done = Count(sem("exp_done"), NG0 * 8)
        pv_done = Count(sem("pv_done"), NG0 * NT)
        o_free = Count(sem("o_free"), NG0)
        recip_ready = Count(sem("recip_ready"), NG0)
        norm_ready = Count(sem("norm_ready"), NG0)
        added = Count(sem("added"), NT)

        N_LOADS = 8 + B
        block = ctx.enter_context(nc.Block())

        @block.sync
        def _(sp):
            for dst, src in ((wq[:], A["L0_wq"]), (wk[:], A["L0_wk"]), (wv[:], A["L0_wv"]), (wo[:], A["L0_wo"]),
                             (bv[:], A["L0_bv"].partition_broadcast(P)), (bo[:], A["L0_bo"].partition_broadcast(P)),
                             (bqk[:], A["L0_bqk"]), (mask_in[:], A["mask"])):
                sp.dma_start(dst, src).then_inc(loaded, 16)
            for i in range(B):
                sp.dma_start(x_all[:, i * NT:(i + 1) * NT, :],
                             A["x"][i].rearrange("(t p) d -> p t d", p=P)).then_inc(loaded, 16)
            with sp.Fori(0, B) as b:
                sp.dma_start(ctx_t[:], A["ctx_t"][b]).then_inc(ctx_in.sem, 16)
                for n in range(4):
                    split_ready.wait(sp, b, n + 1)
                    stack, parts = ((q_stack, (hi, hi, lo)), (k_stack, (hi, lo, hi)))[n // 2]
                    for k, part in enumerate(parts):
                        sp.dma_start(stack[DH0 * k:DH0 * (k + 1), 8 * (n % 2):8 * (n % 2 + 1), :].bitcast(F32),
                                     part[:, n, :].bitcast(F32)).then_inc(stacked.sem, 16)
                for g in range(NG0):
                    nm_ready.wait(sp, b, g + 1)
                    sp.dma_start(q_stack[3 * DH0:ROWS0, G0 * g:G0 * (g + 1), :].bitcast(F32), neg_max[:].bitcast(F32))\
                      .then_inc(nm_in.sem, 16)
                m_full.wait_apart(sp, b, 2 * NT + 4, loaded, 16 * N_LOADS)

        @block.gpsimd
        def _(pool):
            pool.memset(ident[:], 0.0)
            pool.memset(ident_b[:], 0.0)
            pool.memset(minus_half[:], -0.5)
            pool.memset(spread[:], 1.0)
            pool.memset(k_stack[:].bitcast(F32), 1.0).then_inc(consts, 1)
            pool.wait_ge(consts, 1)
            for m in (ident, ident_b):
                pool.affine_select(out=m[:], in_=m[:], compare_op=ALU.not_equal, fill=1.0, base=0,
                                   pattern=[[-1, P]], channel_multiplier=1)
            spread_v = spread[:].rearrange("p (g m) -> p g m", g=G0)
            pool.affine_select(out=spread_v, in_=spread_v, compare_op=ALU.is_equal, fill=0.0, base=-DH0,
                               pattern=[[-SLOT, G0], [0, SLOT]], channel_multiplier=1).then_inc(consts, 1)
            with pool.Fori(0, B) as b:
                stats_done.wait(pool, b, 3)
                pool.tensor_tensor(rstd[:], rstd[:], minus_half[:], ALU.pow).then_inc(rstd_ready.sem, 1)

        @block.scalar
        def _(act):
            with act.Fori(0, B) as b:
                for g in range(NG0):
                    for j in range(8):
                        s_full.wait(act, b, 8 * g + j + 1)
                        if g or j >= 4:
                            pv_done.wait(act, b, NT * g + j // 2 - 1)
                        act.activation(probs[:, j % 4, :, :], p_s[:, j % 2, :, :], ACT.Exp)\
                           .then_inc(exp_done.sem, 1)

        @block.vector
        def _(dve):
            dve.wait_ge(loaded, 16 * N_LOADS)
            dve.tensor_scalar(bqk[:, 0, :], bqk[:, 0, :], DH0 ** -0.5, None, ALU.mult)
            dve.tensor_scalar(bias_k[:], mask_in[:, 1, :, :], -MASKED, None, ALU.mult)
            dve.tensor_scalar(bias_q[:], mask_in[:, 0, :, :], -MASKED, None, ALU.mult).then_inc(prep, 1)
            dve.wait_ge(prep, 1)
            dve.tensor_reduce(least_masked[:], bias_q[:], AX, ALU.max).then_inc(prep, 1)
            dve.wait_ge(prep, 2)
            dve.tensor_scalar(nan_row[:], least_masked[:], MASKED, MASKED, ALU.mult, ALU.mult).then_inc(prep, 1)
            dve.wait_ge(prep, 3)
            dve.tensor_tensor(nan_row[:], nan_row[:], nan_row[:], ALU.subtract).then_inc(prep, 1)
            dve.wait_ge(prep, 4)
            with dve.Fori(0, B) as b:
                xb = x_all[:, bass.ds(b * NT, NT), :]
                use = [0]

                def filled(apart=False):
                    use[0] += 1
                    if apart:
                        m_full.wait_apart(dve, b, use[0], prep, 4)
                    else:
                        m_full.wait(dve, b, use[0])
                    return p_m[:, (use[0] - 1) % 2, :]

                for t in range(NT):
                    last = dve.bn_stats(stats[:, t, :], xb[:, t, :])
                last.then_inc(stats_done.sem, 1)
                stats_done.wait_apart(dve, b, 1, prep, 4)
                for t in range(NT):
                    last = dve.bn_aggr(mean_var[:, t, :], stats[:, t, :])
                last.then_inc(stats_done.sem, 1)
                stats_done.wait(dve, b, 2)
                dve.tensor_scalar(rstd[:], mean_var[:, :, 1], EPS, None, ALU.add).then_inc(stats_done.sem, 1)
                rstd_ready.wait(dve, b, 1)
                for t in range(NT):
                    last = dve.tensor_scalar(xn[:, t, :], xb[:, t, :], mean_var[:, t, 0:1], rstd[:, t:t + 1],
                                             ALU.subtract, ALU.mult)
                last.then_inc(xn_ready.sem, 1)
                for t in range(NT):
                    m = filled()
                    dve.tensor_copy(xn_t[:, :, P * t:P * (t + 1)],
                                    m[:, 0:D].rearrange("p (c n) -> p c n", c=DC)).then_inc(m_free.sem, 1)
                for n in range(4):
                    m = filled()
                    if n < 2:
                        dve.tensor_scalar(full[:, n % 2, :], m, DH0 ** -0.5, bqk[:, 0, n:n + 1], ALU.mult,
                                          ALU.add).then_inc(m_free.sem, 1)
                    else:
                        dve.tensor_scalar(full[:, n % 2, :], m, bqk[:, 1, n - 2:n - 1], None,
                                          ALU.add).then_inc(m_free.sem, 1)
                    m_free.wait(dve, b, use[0])
                    dve.tensor_copy(hi[:, n, :], full[:, n % 2, :]).then_inc(hi_ready.sem, 1)
                    hi_ready.wait(dve, b, n + 1)
                    dve.tensor_tensor(lo[:, n, :], full[:, n % 2, :], hi[:, n, :].bitcast(F32),
                                      ALU.subtract).then_inc(split_ready.sem, 1)
                for t in range(NT):
                    m = filled()
                    dve.tensor_tensor(v[:, t, :], m, bv[:], ALU.add).then_inc(m_free.sem, 1)

                def maxima(n):
                    for i in range(n, min(n + 3, G0 * NT)):
                        m = filled(apart=True)
                        dve.tensor_tensor_reduce(scratch[:, use[0] % 2, :], m, bias_q[:, i % NT, :], 1.0, -3.0e38, ALU.add,
                                                 ALU.max, mx[:, i:i + 1]).then_inc(m_free.sem, 1)

                def turn_maxima(g):
                    m = filled()
                    if g:
                        nm_in.wait(dve, b, 16 * g)
                    dve.tensor_scalar(neg_max[:], m[0:G0 * NT, 0:P], -1.0, None, ALU.mult)\
                       .then_inc(nm_ready.sem, 1)
                    nm_ready.wait_apart(dve, b, g + 1, prep, 4)
                    dve.engine_nop().then_inc(m_free.sem, 1)

                def normalize(g):
                    m = filled()
                    dve.reciprocal(recip[:], m).then_inc(recip_ready.sem, 1)
                    recip_ready.wait(dve, b, g + 1)
                    dve.tensor_tensor(o_norm[:, g, :], o_raw[:], recip[:], ALU.mult).then_inc(m_free.sem, 1)

                for i in range(0, G0 * NT, 3):
                    maxima(i)
                turn_maxima(0)
                for g in range(NG0):
                    for j in range(8):
                        if j == 2 and g:
                            normalize(g - 1)
                        if g + 1 < NG0:
                            maxima(3 * j)
                            if j == 5:
                                turn_maxima(g + 1)
                    pv_done.wait(dve, b, NT * (g + 1))
                    m_free.wait(dve, b, use[0])
                    dve.tensor_copy(o_raw[:], p_o[:]).then_inc(o_free.sem, 1)
                normalize(NG0 - 1)
                for t in range(NT):
                    m = filled()
                    dve.scalar_tensor_tensor(out=xn[:, t, :], in0=m[:, 0:D], scalar=nan_row[:, t:t + 1], in1=bo[:],
                                             op0=ALU.add, op1=ALU.add).then_inc(m_free.sem, 1)
                    m_free.wait(dve, b, use[0])
                    dve.tensor_tensor(xb[:, t, :], xb[:, t, :], xn[:, t, :], ALU.add).then_inc(added.sem, 1)
                added.wait(dve, b, NT)
                stacked.wait(dve, b, 16 * 12)
                assert use[0] == M_USES

        @block.tensor
        def _(pe):
            pe.wait_ge(loaded, 16 * N_LOADS)
            pe.wait_ge(consts, 2)
            pe.wait_ge(prep, 4)
            with pe.Fori(0, B) as b:
                use = [0]

                def free():
                    if use[0] >= 2:
                        m_free.wait(pe, b, use[0] - 1)
                    use[0] += 1
                    return p_m[:, (use[0] - 1) % 2, :]

                def done(mm):
                    mm.then_inc(m_full.sem, 1)

                xn_ready.wait(pe, b, 1)
                for t in range(NT):
                    m = free()
                    for c in range(DC):
                        mm = pe.transpose(m[:, c * P:(c + 1) * P], xn[:, t, c * P:(c + 1) * P], ident[:])
                    done(mm)
                ctx_in.wait(pe, b, 16)
                for n in range(4):
                    m = free()
                    if n == 0:
                        m_free.wait(pe, b, NT)
                    w, src = ((wq, xn_t), (wk, ctx_t))[n // 2]
                    for c in range(DC):
                        mm = pe.matmul(m, w[:, c, P * (n % 2):P * (n % 2 + 1)], src[:, c, :],
                                       start=(c == 0), stop=(c == DC - 1))
                    done(mm)
                for t in range(NT):
                    m = free()
                    for c in range(DC):
                        mm = pe.matmul(m, ctx_t[:, c, P * t:P * (t + 1)], wv[:, c, :],
                                       start=(c == 0), stop=(c == DC - 1))
                    done(mm)

                def maxima(g, n):
                    for i in range(n, min(n + 3, G0 * NT)):
                        h, t = G0 * g + i // NT, i % NT
                        m = free()
                        if g == 0 and i == 0:
                            stacked.wait(pe, b, 16 * 12)
                        done(pe.matmul(m, q_stack[0:3 * DH0, h, P * t:P * (t + 1)], k_stack[0:3 * DH0, h, :],
                                       start=True, stop=True))

                def turn_maxima():
                    m = free()
                    m_free.wait(pe, b, use[0] - 1)
                    done(pe.transpose(m[0:G0 * NT, 0:P], mx[:], ident[:]))

                def spread_sums(g):
                    m = free()
                    o_free.wait(pe, b, g + 1)
                    done(pe.matmul(m, spread[:], o_raw[:], start=True, stop=True))

                def scores(g, j):
                    kt, slot = j // 2, j % 2
                    if j == 0:
                        nm_in.wait(pe, b, 16 * (g + 1))
                    n = 8 * g + j
                    if n >= 2:
                        exp_done.wait(pe, b, n - 1)
                    for i in range(2):
                        h = G0 * g + 2 * slot + i
                        pe.matmul(p_s[:, slot, i, :], k_stack[:, h, P * kt:P * (kt + 1)], q_stack[:, h, :],
                                  start=True, stop=False)
                        mm = pe.matmul(p_s[:, slot, i, :], ident_b[:], bias_k[:, kt, :], start=False, stop=True)
                    mm.then_inc(s_full.sem, 1)

                def times_v(g, kt):
                    exp_done.wait(pe, b, 8 * g + 2 * kt + 2)
                    if kt == 0 and g:
                        o_free.wait(pe, b, g)
                    for i in range(G0):
                        h = G0 * g + i
                        mm = pe.matmul(p_o[SLOT * i:SLOT * (i + 1), :], v[:, kt, SLOT * h:SLOT * (h + 1)],
                                       probs[:, (2 * kt + i // 2) % 4, i % 2, :], start=(kt == 0),
                                       stop=(kt == NT - 1))
                    mm.then_inc(pv_done.sem, 1)

                for i in range(0, G0 * NT, 3):
                    maxima(0, i)
                turn_maxima()
                for g in range(NG0):
                    for j in range(8):
                        scores(g, j)
                        if j == 2 and g:
                            spread_sums(g - 1)
                        if g + 1 < NG0:
                            maxima(g + 1, 3 * j)
                            if j == 5:
                                turn_maxima()
                        if j % 2 == 0 and j:
                            times_v(g, j // 2 - 1)
                    times_v(g, NT - 1)
                spread_sums(NG0 - 1)
                for t in range(NT):
                    m = free()
                    if t == 0:
                        m_free.wait(pe, b, use[0] - 1)
                    for g in range(NG0):
                        mm = pe.matmul(m[:, 0:D], o_norm[:, g, P * t:P * (t + 1)], wo[:, g, :],
                                       start=(g == 0), stop=(g == NG0 - 1))
                    done(mm)
                m_free.wait(pe, b, use[0])
                assert use[0] == M_USES


def route(nc, x_all, xn_all, slot, gate, owner, A):
    with ExitStack() as ctx:
        def sb(name, shape, dt=F32):
            return ctx.enter_context(nc.sbuf_tensor("r_" + name, shape, dt))

        def ps(name, shape, dt=F32):
            return ctx.enter_context(nc.psum_tensor("r_" + name, shape, dt))

        def sem(name):
            return ctx.enter_context(nc.semaphore("r_" + name))

        wr = sb("wr", [P, DC, E])
        br = sb("br", [P, E])
        zeros = sb("zeros", [P, 6 * D])
        ident = sb("ident", [P, P])
        before = sb("before", [P, P])
        ones = sb("ones", [P, P])
        expert_id = sb("expert_id", [P, N_TILES, E])
        steps_of = sb("steps_of", [P, E, B * S // CT])
        tile_id = sb("tile_id", [P, TILES, E])
        xn = sb("xn", [P, NT, D])
        xn_t = sb("xn_t", [P, DC, S])
        stats = sb("stats", [P, NT, 6])
        mean_var = sb("mean_var", [P, NT, 2])
        rstd = sb("rstd", [P, NT])
        minus_half = sb("minus_half", [P, NT])
        logits = sb("logits", [P, N_TILES, E])
        top = sb("top", [P, N_TILES])
        shifted = sb("shifted", [P, N_TILES, E])
        exps = sb("exps", [P, N_TILES, E])
        total = sb("total", [P, N_TILES])
        chosen = sb("chosen", [P, N_TILES])
        one_hot = sb("one_hot", [P, N_TILES, E])
        prior = sb("prior", [P, N_TILES, E])
        count = sb("count", [P, E])
        over = sb("over", [P, E, B * S // CT])
        tiles = sb("tiles", [P, E])
        start = sb("start", [P, E])
        end = sb("end", [P, E])
        past = sb("past", [P, TILES, E])
        slot_f = sb("slot_f", [P, N_TILES])
        owner_f = sb("owner_f", [P, TILES])

        p_t = ps("p_t", [P, 2, S])
        p_l = ps("p_l", [P, NT, E])
        p_rank = ps("p_rank", [P, N_TILES * E])
        p_sum = ps("p_sum", [P, N_TILES * E])

        consts, filled = sem("consts"), sem("filled")
        loaded, cleared = sem("loaded"), sem("cleared")
        stats_done = Count(sem("stats_done"), 3)
        rstd_ready = Count(sem("rstd_ready"), 1)
        xn_ready = Count(sem("xn_ready"), 1)
        kept = Count(sem("kept"), 1)
        turned = Count(sem("turned"), NT)
        copied = Count(sem("copied"), NT)
        l_full = Count(sem("l_full"), 1)
        l_read = Count(sem("l_read"), 1)
        shifted_ready, exps_ready, hot_ready = sem("shifted_ready"), sem("exps_ready"), sem("hot_ready")
        ranked, step_done, slots_ready, scattered = sem("ranked"), sem("step_done"), sem("slots_ready"), sem("scattered")
        block = ctx.enter_context(nc.Block())

        @block.sync
        def _(sp):
            sp.dma_start(wr[:], A["L0_wr"]).then_inc(loaded, 16)
            sp.dma_start(br[:], A["L0_br"].partition_broadcast(P)).then_inc(loaded, 16)
            sp.wait_ge(filled, 1)
            rows = TILES * CT // 5
            for i in range(5):
                sp.dma_start(A["x_slots"][i * rows:(i + 1) * rows, :].rearrange("(p r) d -> p (r d)", p=P),
                             zeros[:]).then_inc(cleared, 16)

        @block.gpsimd
        def _(pool):
            pool.memset(zeros[:], 0.0).then_inc(filled, 1)
            pool.memset(ident[:], 0.0)
            pool.memset(before[:], 1.0)
            pool.memset(ones[:], 1.0)
            pool.memset(minus_half[:], -0.5)
            pool.iota(expert_id[:], pattern=[[0, N_TILES], [1, E]], base=-E, channel_multiplier=0,
                      allow_small_or_imprecise_dtypes=True)
            pool.iota(steps_of[:], pattern=[[0, E], [CT, B * S // CT]], base=0, channel_multiplier=0,
                      allow_small_or_imprecise_dtypes=True)
            pool.iota(tile_id[:], pattern=[[1, TILES], [0, E]], base=0, channel_multiplier=0,
                      allow_small_or_imprecise_dtypes=True).then_inc(filled, 1)
            pool.wait_ge(filled, 2)
            pool.affine_select(out=ident[:], in_=ident[:], compare_op=ALU.not_equal, fill=1.0, base=0,
                               pattern=[[-1, P]], channel_multiplier=1)
            pool.affine_select(out=before[:], in_=before[:], compare_op=ALU.is_gt, fill=0.0, base=0,
                               pattern=[[1, P]], channel_multiplier=-1).then_inc(consts, 1)
            with pool.Fori(0, B) as b:
                stats_done.wait(pool, b, 3)
                pool.tensor_tensor(rstd[:], rstd[:], minus_half[:], ALU.pow).then_inc(rstd_ready.sem, 1)
                xn_ready.wait(pool, b, 1)
                pool.tensor_copy(xn_all[:, bass.ds(b * NT, NT), :], xn[:]).then_inc(kept.sem, 1)
            pool.wait_ge(kept.sem, B)
            pool.wait_ge(cleared, 16 * 5)
            pool.wait_ge(slots_ready, 1)
            for t in range(N_TILES):
                pool.indirect_dma_start(out=A["x_slots"], out_offset=bass.IndirectOffsetOnAxis(ap=slot[:, t:t + 1], axis=0),
                                        in_=xn_all[:, t, :], in_offset=None).then_inc(scattered, 16)
            pool.wait_ge(scattered, 16 * N_TILES)

        @block.scalar
        def _(act):
            act.wait_ge(shifted_ready, 1)
            act.activation(exps[:], shifted[:], ACT.Exp).then_inc(exps_ready, 1)

        @block.vector
        def _(dve):
            dve.wait_ge(loaded, 32)
            with dve.Fori(0, B) as b:
                xb = x_all[:, bass.ds(b * NT, NT), :]
                for t in range(NT):
                    last = dve.bn_stats(stats[:, t, :], xb[:, t, :])
                last.then_inc(stats_done.sem, 1)
                stats_done.wait_apart(dve, b, 1, loaded, 32)
                for t in range(NT):
                    last = dve.bn_aggr(mean_var[:, t, :], stats[:, t, :])
                last.then_inc(stats_done.sem, 1)
                stats_done.wait(dve, b, 2)
                dve.tensor_scalar(rstd[:], mean_var[:, :, 1], EPS, None, ALU.add).then_inc(stats_done.sem, 1)
                rstd_ready.wait(dve, b, 1)
                for t in range(NT):
                    last = dve.tensor_scalar(xn[:, t, :], xb[:, t, :], mean_var[:, t, 0:1], rstd[:, t:t + 1],
                                             ALU.subtract, ALU.mult)
                last.then_inc(xn_ready.sem, 1)
                for t in range(NT):
                    turned.wait(dve, b, t + 1)
                    dve.tensor_copy(xn_t[:, :, P * t:P * (t + 1)],
                                    p_t[:, t % 2, 0:D].rearrange("p (c n) -> p c n", c=DC)).then_inc(copied.sem, 1)
                l_full.wait(dve, b, 1)
                dve.tensor_tensor(logits[:, bass.ds(b * NT, NT), :], p_l[:],
                                  br[:].unsqueeze(1).broadcast_to([P, NT, E]), ALU.add).then_inc(l_read.sem, 1)
                kept.wait(dve, b, 1)
            dve.wait_ge(l_read.sem, B)
            dve.wait_ge(consts, 1)
            n = [0]

            def step(ins):
                n[0] += 1
                ins.then_inc(step_done, 1)
                dve.wait_ge(step_done, n[0])

            def over_tiles(v):
                return v.unsqueeze(2).broadcast_to([P, N_TILES, E])

            step(dve.tensor_reduce(top[:], logits[:], AX, ALU.max))
            dve.tensor_tensor(shifted[:], logits[:], over_tiles(top[:]), ALU.subtract).then_inc(shifted_ready, 1)
            step(dve.tensor_tensor(one_hot[:], logits[:], over_tiles(top[:]), ALU.is_ge))
            step(dve.tensor_tensor(one_hot[:], one_hot[:], expert_id[:], ALU.mult))
            step(dve.tensor_reduce(chosen[:], one_hot[:], AX, ALU.min))
            step(dve.tensor_scalar(chosen[:], chosen[:], -1.0, None, ALU.min))
            dve.tensor_tensor(one_hot[:], expert_id[:], over_tiles(chosen[:]), ALU.is_equal).then_inc(hot_ready, 1)
            dve.wait_ge(exps_ready, 1)
            step(dve.tensor_reduce(total[:], exps[:], AX, ALU.add))
            dve.reciprocal(gate[:], total[:])
            dve.wait_ge(ranked, 1)
            p_sum_v = p_sum[:].rearrange("p (t e) -> p t e", e=E)
            step(dve.memset(prior[:, 0, :], 0.0))
            for t in range(1, N_TILES):
                step(dve.tensor_tensor(prior[:, t, :], p_sum_v[:, t - 1, :], prior[:, t - 1, :], ALU.add))
            step(dve.tensor_tensor(count[:], p_sum_v[:, N_TILES - 1, :], prior[:, N_TILES - 1, :], ALU.add))
            step(dve.tensor_tensor(over[:], count[:].unsqueeze(2).broadcast_to([P, E, B * S // CT]), steps_of[:],
                                   ALU.is_gt))
            step(dve.tensor_reduce(tiles[:], over[:], AX, ALU.add))
            step(dve.memset(start[:, 0:1], 0.0))
            for e in range(1, E):
                step(dve.tensor_tensor(start[:, e:e + 1], start[:, e - 1:e], tiles[:, e - 1:e], ALU.add))
            step(dve.tensor_tensor(end[:], start[:], tiles[:], ALU.add))
            step(dve.tensor_tensor(past[:], tile_id[:], end[:].unsqueeze(1).broadcast_to([P, TILES, E]), ALU.is_ge))
            step(dve.tensor_reduce(owner_f[:], past[:], AX, ALU.add))
            dve.tensor_scalar(owner[:], owner_f[:], float(E - 1), None, ALU.min)
            step(dve.tensor_scalar(start[:], start[:], float(CT), None, ALU.mult))
            step(dve.tensor_tensor(prior[:], prior[:], start[:].unsqueeze(1).broadcast_to([P, N_TILES, E]), ALU.add))
            step(dve.tensor_tensor(prior[:], p_rank[:].rearrange("p (t e) -> p t e", e=E), prior[:], ALU.add))
            step(dve.tensor_tensor(prior[:], prior[:], one_hot[:], ALU.mult))
            step(dve.tensor_reduce(slot_f[:], prior[:], AX, ALU.add))
            dve.tensor_copy(slot[:], slot_f[:]).then_inc(slots_ready, 1)

        @block.tensor
        def _(pe):
            pe.wait_ge(loaded, 32)
            pe.wait_ge(consts, 1)
            with pe.Fori(0, B) as b:
                xn_ready.wait(pe, b, 1)
                for t in range(NT):
                    if t >= 2:
                        copied.wait(pe, b, t - 1)
                    for c in range(DC):
                        mm = pe.transpose(p_t[:, t % 2, c * P:(c + 1) * P], xn[:, t, c * P:(c + 1) * P], ident[:])
                    mm.then_inc(turned.sem, 1)
                copied.wait(pe, b, NT)
                for t in range(NT):
                    for c in range(DC):
                        mm = pe.matmul(p_l[:, t, :], xn_t[:, c, P * t:P * (t + 1)], wr[:, c, :],
                                       start=(c == 0), stop=(c == DC - 1))
                mm.then_inc(l_full.sem, 1)
                l_read.wait(pe, b, 1)
            pe.wait_ge(hot_ready, 1)
            hot = one_hot[:].rearrange("p t e -> p (t e)")
            pe.matmul(p_rank[:], before[:], hot, start=True, stop=True)
            pe.matmul(p_sum[:], ones[:], hot, start=True, stop=True).then_inc(ranked, 1)


def experts(nc, x_all, slot, gate, owner, A):
    with ExitStack() as ctx:
        def sb(name, shape, dt=F32):
            return ctx.enter_context(nc.sbuf_tensor("e_" + name, shape, dt))

        def ps(name, shape, dt=F32):
            return ctx.enter_context(nc.psum_tensor("e_" + name, shape, dt))

        def sem(name):
            return ctx.enter_context(nc.semaphore("e_" + name))

        ident = sb("ident", [P, P])
        rows = sb("rows", [P, RING, TT, D])
        w1 = sb("w1", [P, RING, DC, FF])
        w2 = sb("w2", [P, RING, FC, D])
        b1 = sb("b1", [P, RING, FC])
        b2 = sb("b2", [P, RING, D])
        rows_t = sb("rows_t", [P, 2, DC, CT])
        hidden = sb("hidden", [P, 4, CT])
        y = sb("y", [P, RING, TT, D])
        back = sb("back", [P, N_TILES, D])

        p_t = ps("p_t", [P, DC, CT])
        p_h = ps("p_h", [P, 4, S])
        p_y = ps("p_y", [P, TT, S])

        cleared, consts = sem("cleared"), sem("consts")
        rows_in = [Count(sem(f"rows_in{r}"), 16) for r in range(RING)]
        w_in = [Count(sem(f"w_in{r}"), 64) for r in range(RING)]
        turned = Count(sem("turned"), RING)
        rows_t_ready = Count(sem("rows_t_ready"), RING)
        h_full = Count(sem("h_full"), RING * FC)
        h_ready = Count(sem("h_ready"), RING * FC)
        h_used = Count(sem("h_used"), RING * FC)
        y_ready = Count(sem("y_ready"), RING)
        y_stored = Count(sem("y_stored"), 16 * RING)
        gathered, scaled = sem("gathered"), sem("scaled")
        block = ctx.enter_context(nc.Block())
        TURNS = TILES // RING

        @block.sync
        def _(sp):
            def load(i, r):
                e = sp.value_load(owner[0:1, bass.ds(i * RING + r, 1)], min_val=0, max_val=E - 1)
                sp.dma_start(rows[:, r, :, :], A["x_slots"][bass.ds((i * RING + r) * CT, CT), :]
                             .rearrange("(t p) d -> p t d", p=P)).then_inc(rows_in[r].sem, 16)
                sp.dma_start(w1[:, r, :, :], A["L0_w1"][bass.ds(e, 1)].rearrange("o p c f -> p (o c) f"))\
                  .then_inc(w_in[r].sem, 16)
                sp.dma_start(b1[:, r, :], A["L0_b1"][bass.ds(e, 1)].rearrange("o p c -> p (o c)"))\
                  .then_inc(w_in[r].sem, 16)
                sp.dma_start(b2[:, r, :], A["L0_b2"][bass.ds(e, 1)].rearrange("o p d -> p (o d)"))\
                  .then_inc(w_in[r].sem, 16)
                sp.dma_start(w2[:, r, :, :], A["L0_w2"][bass.ds(e, 1)].rearrange("o p c d -> p (o c) d"))\
                  .then_inc(w_in[r].sem, 16)

            for r in range(RING):
                load(0, r)
            with sp.Fori(0, TURNS - 1) as i:
                for r in range(RING):
                    y_ready.wait(sp, i, r + 1)
                    load(i + 1, r)

        @block.gpsimd
        def _(pool):
            pool.memset(ident[:], 0.0).then_inc(cleared, 1)
            pool.wait_ge(cleared, 1)
            pool.affine_select(out=ident[:], in_=ident[:], compare_op=ALU.not_equal, fill=1.0, base=0,
                               pattern=[[-1, P]], channel_multiplier=1).then_inc(consts, 1)
            with pool.Fori(0, TURNS) as i:
                for r in range(RING):
                    y_ready.wait(pool, i, r + 1)
                    pool.dma_start(A["y_slots"][bass.ds((i * RING + r) * CT, CT), :]
                                   .rearrange("(t p) d -> p t d", p=P), y[:, r, :, :]).then_inc(y_stored.sem, 16)
            pool.wait_ge(y_stored.sem, 16 * TILES)
            for t in range(N_TILES):
                pool.indirect_dma_start(out=back[:, t, :], out_offset=None, in_=A["y_slots"],
                                        in_offset=bass.IndirectOffsetOnAxis(ap=slot[:, t:t + 1], axis=0))\
                    .then_inc(gathered, 16)

        @block.scalar
        def _(act):
            with act.Fori(0, TURNS) as i:
                for r in range(RING):
                    for c in range(FC):
                        n = FC * r + c
                        h_full.wait(act, i, n + 1)
                        if c == 0:
                            w_in[r].wait(act, i, 64)
                        if n >= 4:
                            h_used.wait(act, i, n - 3)
                        act.activation(hidden[:, c % 4, :], p_h[:, c % 4, 0:CT], ACT.Gelu, bias=b1[:, r, c:c + 1])\
                           .then_inc(h_ready.sem, 1)
                h_used.wait(act, i, RING * FC)

        @block.vector
        def _(dve):
            with dve.Fori(0, TURNS) as i:
                for r in range(RING):
                    turned.wait(dve, i, r + 1)
                    dve.tensor_copy(rows_t[:, r % 2, :, :], p_t[:]).then_inc(rows_t_ready.sem, 1)
                    h_used.wait(dve, i, FC * (r + 1))
                    if r:
                        y_stored.wait(dve, i, 16 * r)
                    dve.tensor_tensor(y[:, r, :, :], p_y[:, :, 0:D], b2[:, r, :].unsqueeze(1).broadcast_to([P, TT, D]),
                                      ALU.add).then_inc(y_ready.sem, 1)
            dve.wait_ge(gathered, 16 * N_TILES)
            for t in range(N_TILES):
                dve.scalar_tensor_tensor(out=x_all[:, t, :], in0=back[:, t, :], scalar=gate[:, t:t + 1],
                                         in1=x_all[:, t, :], op0=ALU.mult, op1=ALU.add).then_inc(scaled, 1)
            dve.wait_ge(scaled, N_TILES)

        @block.tensor
        def _(pe):
            pe.wait_ge(consts, 1)
            with pe.Fori(0, TURNS) as i:
                for r in range(RING):
                    rows_in[r].wait(pe, i, 16)
                    for t in range(TT):
                        for c in range(DC):
                            mm = pe.transpose(p_t[:, c, P * t:P * (t + 1)], rows[:, r, t, P * c:P * (c + 1)], ident[:])
                    mm.then_inc(turned.sem, 1)
                    w_in[r].wait(pe, i, 64)
                    rows_t_ready.wait(pe, i, r + 1)
                    for c in range(FC + 2):
                        if c < FC:
                            n = FC * r + c
                            if n >= 4:
                                h_ready.wait(pe, i, n - 3)
                            for k in range(DC):
                                mm = pe.matmul(p_h[:, c % 4, 0:CT], w1[:, r, k, P * c:P * (c + 1)],
                                               rows_t[:, r % 2, k, :], start=(k == 0), stop=(k == DC - 1))
                            mm.then_inc(h_full.sem, 1)
                        if c >= 2:
                            d = c - 2
                            h_ready.wait(pe, i, FC * r + d + 1)
                            if d == 0 and r:
                                y_ready.wait(pe, i, r)
                            for t in range(TT):
                                mm = pe.matmul(p_y[:, t, 0:D], hidden[:, d % 4, P * t:P * (t + 1)], w2[:, r, d, :],
                                               start=(d == 0), stop=(d == FC - 1))
                            mm.then_inc(h_used.sem, 1)
                y_ready.wait(pe, i, RING)


def mixture(nc, x_all, A):
    with nc.sbuf_tensor("slot", [P, N_TILES], U32) as slot, nc.sbuf_tensor("gate", [P, N_TILES], F32) as gate, \
         nc.sbuf_tensor("owner", [P, TILES], I32) as owner:
        with nc.sbuf_tensor("xn_all", [P, N_TILES, D], F32) as xn_all:
            route(nc, x_all, xn_all, slot, gate, owner, A)
        experts(nc, x_all, slot, gate, owner, A)


def attention1(nc, x_all, A):
    with ExitStack() as ctx:
        def sb(name, shape, dt=F32):
            return ctx.enter_context(nc.sbuf_tensor("a1_" + name, shape, dt))

        def ps(name, shape, dt=F32):
            return ctx.enter_context(nc.psum_tensor("a1_" + name, shape, dt))

        def sem(name):
            return ctx.enter_context(nc.semaphore("a1_" + name))

        HD = H1 * DK
        ROWS = DK + 1
        AHEAD = 3
        wq, wk, wv = sb("wq", [P, DC, HD]), sb("wk", [P, DC, HD]), sb("wv", [P, DC, HD])
        wo = sb("wo", [P, PAIRS, D])
        bv = sb("bv", [P, HD])
        bo = sb("bo", [P, D])
        bqk = sb("bqk", [P, 2, PAIRS])
        ident = sb("ident", [P, P])
        ones = sb("ones", [P, DK])
        ctx_t = sb("ctx_t", [P, DC, S])
        xn_t = sb("xn_t", [P, DC, S])
        stats = sb("stats", [P, NT, 6])
        mean_var = sb("mean_var", [P, NT, 2])
        rstd = sb("rstd", [P, NT])
        minus_half = sb("minus_half", [P, NT])
        full = sb("full", [P, S])
        hi = sb("hi", [P, 2, S], F32R)
        lo = sb("lo", [P, 2, S], F32R)
        q_hh = sb("q_hh", [P, 2 * AHEAD, S], F32R)
        k_hl = sb("k_hl", [P, 2 * AHEAD, S], F32R)
        q_lm = sb("q_lm", [ROWS, 2 * AHEAD, S], F32R)
        k_h1 = sb("k_h1", [ROWS, 2 * AHEAD, S], F32R)
        mem_hl = sb("mem_hl", [P, H1, MEM], F32R)
        mem_h1 = sb("mem_h1", [ROWS, H1, MEM], F32R)
        v = sb("v", [P, KT1, HD])
        probs = sb("probs", [P, 3, 2, S])
        max_ctx = sb("max_ctx", [P, 2 * NT])
        max_mem = sb("max_mem", [P, 2 * NT])
        mx = sb("mx", [P, 2 * NT])
        neg_max = sb("neg_max", [2 * NT, P], F32R)
        recip = sb("recip", [P, S])
        o_norm = sb("o_norm", [P, PAIRS, S])
        xn = o_norm[:, 0:2, :].rearrange("p a (t d) -> p (a t) d", d=D)

        p_s = ps("p_s", [P, 2, 2, S])
        p_m = ps("p_m", [P, 2, S])
        p_o = ps("p_o", [P, S])
        p_sum = ps("p_sum", [P, S])

        PER_MAX = 2 * (NT + 1)
        M_USES = NT + 2 * NT + 2 * PAIRS + PER_MAX * PAIRS + PAIRS + NT
        assert M_USES % 2 == 0
        loaded, filled_s, consts, prep = sem("loaded"), sem("filled"), sem("consts"), sem("prep")
        mem_in = sem("mem_in")
        ctx_in = Count(sem("ctx_in"), 16)
        stats_done = Count(sem("stats_done"), 3)
        rstd_ready = Count(sem("rstd_ready"), 1)
        xn_ready = Count(sem("xn_ready"), 1)
        m_full = Count(sem("m_full"), M_USES)
        m_free = Count(sem("m_free"), M_USES)
        hi_ready = Count(sem("hi_ready"), 2 * PAIRS)
        split_ready = Count(sem("split_ready"), 2 * PAIRS)
        stacked = Count(sem("stacked"), 16 * 12 * PAIRS)
        mx_ready = Count(sem("mx_ready"), PAIRS)
        nm_ready = Count(sem("nm_ready"), PAIRS)
        nm_in = Count(sem("nm_in"), 16 * PAIRS)
        s_full = Count(sem("s_full"), KT1 * PAIRS)
        exp_done = Count(sem("exp_done"), KT1 * PAIRS)
        pv_done = Count(sem("pv_done"), KT1 * PAIRS)
        recip_ready = Count(sem("recip_ready"), PAIRS)
        o_free = Count(sem("o_free"), PAIRS)
        added = Count(sem("added"), NT)
        MAXIMA = [2, 3, 3, 2, 0]
        assert sum(MAXIMA) == PER_MAX
        block = ctx.enter_context(nc.Block())

        @block.sync
        def _(sp):
            for dst, src in ((xn_t[:].rearrange("p c n -> p (c n)"), A["L1_mk"]), (bqk[:], A["L1_bqk"]),
                             (wq[:], A["L1_wq"]), (wk[:], A["L1_wk"]), (wv[:], A["L1_wv"]), (wo[:], A["L1_wo"]),
                             (bv[:], A["L1_bv"].partition_broadcast(P)), (bo[:], A["L1_bo"].partition_broadcast(P)),
                             (v[:, NT, :], A["L1_mv"])):
                sp.dma_start(dst, src).then_inc(loaded, 16)
            sp.wait_ge(prep, 3)
            for i in range(2):
                rows = slice(DK * i, DK * (i + 1))
                for dst, part in ((mem_hl[0:DK], hi), (mem_hl[DK:P], lo), (mem_h1[0:DK], hi)):
                    sp.dma_start(dst[:, i::2, :].bitcast(F32),
                                 part[rows, :, :].rearrange("p a (c n) -> p (a c) n", n=MEM).bitcast(F32))\
                      .then_inc(mem_in, 16)
            with sp.Fori(0, B) as b:
                sp.dma_start(ctx_t[:], A["ctx_t"][b]).then_inc(ctx_in.sem, 16)

                def stack(p):
                    if p >= AHEAD:
                        scored = s_full.value(sp, b, KT1 * (p - AHEAD + 1))
                        split_ready.wait(sp, b, 2 * p + 1)
                        sp.wait_ge(s_full.sem, scored)
                    else:
                        split_ready.wait(sp, b, 2 * p + 1)
                    for n in range(2):
                        if n == 1:
                            split_ready.wait(sp, b, 2 * p + 2)
                        parts = (((q_hh[0:DK], hi), (q_hh[DK:P], hi), (q_lm[0:DK], lo)),
                                 ((k_hl[0:DK], hi), (k_hl[DK:P], lo), (k_h1[0:DK], hi)))[n]
                        for i in range(2):
                            for dst, part in parts:
                                sp.dma_start(dst[:, 2 * (p % AHEAD) + i, :].bitcast(F32),
                                             part[DK * i:DK * (i + 1), n, :].bitcast(F32))\
                                  .then_inc(stacked.sem, 16)

                def bring_maxima(p):
                    nm_ready.wait(sp, b, p + 1)
                    s = 2 * (p % AHEAD)
                    sp.dma_start(q_lm[DK:ROWS, s:s + 2, :].bitcast(F32), neg_max[:].bitcast(F32))\
                      .then_inc(nm_in.sem, 16)

                stack(0)
                stack(1)
                bring_maxima(0)
                for p in range(PAIRS):
                    if p + 2 < PAIRS:
                        stack(p + 2)
                    if p + 1 < PAIRS:
                        bring_maxima(p + 1)
                s_full.wait_apart(sp, b, KT1 * PAIRS, loaded, 16 * 9)

        @block.gpsimd
        def _(pool):
            pool.memset(ident[:], 0.0)
            pool.memset(ones[:], 1.0)
            pool.memset(minus_half[:], -0.5)
            pool.memset(k_h1[:].bitcast(F32), 1.0)
            pool.memset(mem_h1[:].bitcast(F32), 1.0).then_inc(filled_s, 1)
            pool.wait_ge(filled_s, 1)
            pool.affine_select(out=ident[:], in_=ident[:], compare_op=ALU.not_equal, fill=1.0, base=0,
                               pattern=[[-1, P]], channel_multiplier=1).then_inc(consts, 1)
            with pool.Fori(0, B) as b:
                stats_done.wait(pool, b, 3)
                pool.tensor_tensor(rstd[:], rstd[:], minus_half[:], ALU.pow).then_inc(rstd_ready.sem, 1)

        @block.scalar
        def _(act):
            with act.Fori(0, B) as b:
                for n in range(KT1 * PAIRS):
                    s_full.wait(act, b, n + 1)
                    if n >= 3:
                        pv_done.wait(act, b, n - 2)
                    act.activation(probs[:, n % 3, :, :], p_s[:, n % 2, :, :], ACT.Exp).then_inc(exp_done.sem, 1)
                pv_done.wait(act, b, KT1 * PAIRS)

        @block.vector
        def _(dve):
            dve.wait_ge(loaded, 16 * 9)
            dve.wait_ge(consts, 1)
            mem_keys = xn_t[:].rearrange("p c n -> p (c n)")
            flat = lambda t: t[:].rearrange("p c n -> p (c n)")
            dve.tensor_scalar(bqk[:, 0, :], bqk[:, 0, :], DK ** -0.5, None, ALU.mult).then_inc(prep, 1)
            dve.tensor_copy(flat(hi), mem_keys).then_inc(prep, 1)
            dve.wait_ge(prep, 2)
            dve.tensor_tensor(flat(lo), mem_keys, flat(hi).bitcast(F32), ALU.subtract).then_inc(prep, 1)
            dve.wait_ge(mem_in, 16 * 6)
            with dve.Fori(0, B) as b:
                xb = x_all[:, bass.ds(b * NT, NT), :]
                use = [0]

                def filled():
                    use[0] += 1
                    m_full.wait(dve, b, use[0])
                    return p_m[:, (use[0] - 1) % 2, :]

                for t in range(NT):
                    last = dve.bn_stats(stats[:, t, :], xb[:, t, :])
                last.then_inc(stats_done.sem, 1)
                stats_done.wait_apart(dve, b, 1, prep, 3)
                for t in range(NT):
                    last = dve.bn_aggr(mean_var[:, t, :], stats[:, t, :])
                last.then_inc(stats_done.sem, 1)
                stats_done.wait(dve, b, 2)
                dve.tensor_scalar(rstd[:], mean_var[:, :, 1], EPS, None, ALU.add).then_inc(stats_done.sem, 1)
                rstd_ready.wait(dve, b, 1)
                for t in range(NT):
                    last = dve.tensor_scalar(xn[:, t, :], xb[:, t, :], mean_var[:, t, 0:1], rstd[:, t:t + 1],
                                             ALU.subtract, ALU.mult)
                last.then_inc(xn_ready.sem, 1)
                for t in range(NT):
                    m = filled()
                    dve.tensor_copy(xn_t[:, :, P * t:P * (t + 1)],
                                    m[:, 0:D].rearrange("p (c n) -> p c n", c=DC)).then_inc(m_free.sem, 1)
                for t in range(NT):
                    for half in range(2):
                        m = filled()
                        dve.tensor_tensor(v[:, t, S * half:S * (half + 1)], m, bv[:, S * half:S * (half + 1)],
                                          ALU.add).then_inc(m_free.sem, 1)

                def split(p):
                    for n in range(2):
                        m = filled()
                        if p + n:
                            split_ready.wait(dve, b, 2 * p + n)
                        if n == 0:
                            dve.tensor_scalar(full[:], m, DK ** -0.5, bqk[:, 0, p:p + 1], ALU.mult,
                                              ALU.add).then_inc(m_free.sem, 1)
                        else:
                            dve.tensor_scalar(full[:], m, bqk[:, 1, p:p + 1], None, ALU.add).then_inc(m_free.sem, 1)
                        m_free.wait(dve, b, use[0])
                        if n == 0 and p:
                            stacked.wait(dve, b, 16 * 12 * p)
                        dve.tensor_copy(hi[:, n, :], full[:]).then_inc(hi_ready.sem, 1)
                        hi_ready.wait(dve, b, 2 * p + n + 1)
                        dve.tensor_tensor(lo[:, n, :], full[:], hi[:, n, :].bitcast(F32),
                                          ALU.subtract).then_inc(split_ready.sem, 1)

                def maxima(n, k):
                    for i in range(n, n + k):
                        m = filled()
                        head, t = i // (NT + 1), i % (NT + 1)
                        if t < NT:
                            dve.tensor_reduce(max_ctx[:, NT * head + t:NT * head + t + 1], m, AX, ALU.max)\
                               .then_inc(m_free.sem, 1)
                        else:
                            dve.tensor_reduce(max_mem[:, NT * head:NT * (head + 1)],
                                              m.rearrange("p (t n) -> p t n", n=MEM), AX, ALU.max)\
                               .then_inc(m_free.sem, 1)

                def turn_maxima(p):
                    m_free.wait(dve, b, use[0])
                    dve.tensor_tensor(mx[:], max_ctx[:], max_mem[:], ALU.max).then_inc(mx_ready.sem, 1)
                    m = filled()
                    if p:
                        nm_in.wait(dve, b, 16 * p)
                    dve.tensor_scalar(neg_max[:], m[0:2 * NT, 0:P], -1.0, None, ALU.mult)\
                       .then_inc(nm_ready.sem, 1)
                    nm_ready.wait_apart(dve, b, p + 1, prep, 3)
                    dve.engine_nop().then_inc(m_free.sem, 1)

                def normalize(p):
                    pv_done.wait(dve, b, KT1 * (p + 1))
                    if p:
                        o_free.wait(dve, b, p)
                    dve.reciprocal(recip[:], p_sum[:]).then_inc(recip_ready.sem, 1)
                    recip_ready.wait(dve, b, p + 1)
                    dve.tensor_tensor(o_norm[:, p, :], p_o[:], recip[:], ALU.mult).then_inc(o_free.sem, 1)

                split(0)
                split(1)
                maxima(0, PER_MAX)
                turn_maxima(0)
                for p in range(PAIRS):
                    if p:
                        normalize(p - 1)
                    if p + 2 < PAIRS:
                        split(p + 2)
                    if p + 1 < PAIRS:
                        maxima(0, PER_MAX)
                        turn_maxima(p + 1)
                normalize(PAIRS - 1)
                for t in range(NT):
                    m = filled()
                    dve.tensor_tensor(recip[:, 0:D], m[:, 0:D], bo[:], ALU.add)\
                       .then_inc(m_free.sem, 1)
                    m_free.wait(dve, b, use[0])
                    dve.tensor_tensor(xb[:, t, :], xb[:, t, :], recip[:, 0:D], ALU.add).then_inc(added.sem, 1)
                    added.wait(dve, b, t + 1)
                split_ready.wait(dve, b, 2 * PAIRS)
                stacked.wait(dve, b, 16 * 12 * PAIRS)
                assert use[0] == M_USES

        @block.tensor
        def _(pe):
            pe.wait_ge(loaded, 16 * 9)
            pe.wait_ge(consts, 1)
            pe.wait_ge(prep, 3)
            pe.wait_ge(mem_in, 16 * 6)
            with pe.Fori(0, B) as b:
                use = [0]

                def free():
                    if use[0] >= 2:
                        m_free.wait(pe, b, use[0] - 1)
                    use[0] += 1
                    return p_m[:, (use[0] - 1) % 2, :]

                def done(mm):
                    mm.then_inc(m_full.sem, 1)

                xn_ready.wait(pe, b, 1)
                for t in range(NT):
                    m = free()
                    for c in range(DC):
                        mm = pe.transpose(m[:, c * P:(c + 1) * P], xn[:, t, c * P:(c + 1) * P], ident[:])
                    done(mm)
                ctx_in.wait(pe, b, 16)
                for t in range(NT):
                    for half in range(2):
                        m = free()
                        for c in range(DC):
                            mm = pe.matmul(m, ctx_t[:, c, P * t:P * (t + 1)], wv[:, c, S * half:S * (half + 1)],
                                           start=(c == 0), stop=(c == DC - 1))
                        done(mm)

                def project(p):
                    for w, src in ((wq, xn_t), (wk, ctx_t)):
                        m = free()
                        if p == 0 and w is wq:
                            m_free.wait(pe, b, NT)
                        for c in range(DC):
                            mm = pe.matmul(m, w[:, c, P * p:P * (p + 1)], src[:, c, :],
                                           start=(c == 0), stop=(c == DC - 1))
                        done(mm)

                def maxima(p, n, k):
                    for i in range(n, n + k):
                        head, t = i // (NT + 1), i % (NT + 1)
                        s = 2 * (p % AHEAD) + head
                        m = free()
                        if i == 0:
                            stacked.wait(pe, b, 16 * 12 * (p + 1))
                        if t < NT:
                            done(pe.matmul(m, q_hh[:, s, P * t:P * (t + 1)], k_hl[:, s, :], start=True, stop=True))
                        else:
                            for t in range(NT):
                                mm = pe.matmul(m[:, MEM * t:MEM * (t + 1)], q_hh[:, s, P * t:P * (t + 1)],
                                               mem_hl[:, 2 * p + head, :], start=True, stop=True)
                            done(mm)

                def turn_maxima(p):
                    m = free()
                    mx_ready.wait(pe, b, p + 1)
                    done(pe.transpose(m[0:2 * NT, 0:P], mx[:], ident[:]))

                def scores(p, kt):
                    n = KT1 * p + kt
                    if kt == 0:
                        nm_in.wait(pe, b, 16 * (p + 1))
                    if n >= 2:
                        exp_done.wait(pe, b, n - 1)
                    for i in range(2):
                        s = 2 * (p % AHEAD) + i
                        if kt < NT:
                            first, second = (t[:, s, P * kt:P * (kt + 1)] for t in (k_hl, k_h1))
                        else:
                            first, second = (t[:, 2 * p + i, :] for t in (mem_hl, mem_h1))
                        pe.matmul(p_s[:, n % 2, i, :], first, q_hh[:, s, :], start=True, stop=False)
                        mm = pe.matmul(p_s[:, n % 2, i, :], second, q_lm[:, s, :], start=False, stop=True)
                    mm.then_inc(s_full.sem, 1)

                def times_v(p, kt):
                    n = KT1 * p + kt
                    exp_done.wait(pe, b, n + 1)
                    if kt == 0 and p:
                        o_free.wait(pe, b, p)
                    for i in range(2):
                        h = 2 * p + i
                        pe.matmul(p_o[DK * i:DK * (i + 1), :], v[:, kt, DK * h:DK * (h + 1)], probs[:, n % 3, i, :],
                                  start=(kt == 0), stop=(kt == KT1 - 1))
                    for i in range(2):
                        mm = pe.matmul(p_sum[DK * i:DK * (i + 1), :], ones[:], probs[:, n % 3, i, :],
                                       start=(kt == 0), stop=(kt == KT1 - 1))
                    mm.then_inc(pv_done.sem, 1)

                project(0)
                project(1)
                maxima(0, 0, PER_MAX)
                turn_maxima(0)
                for p in range(PAIRS):
                    at = 0
                    for kt in range(KT1):
                        scores(p, kt)
                        if kt == 0 and p + 2 < PAIRS:
                            project(p + 2)
                        if p + 1 < PAIRS:
                            maxima(p + 1, at, MAXIMA[kt])
                            at += MAXIMA[kt]
                            if kt == 3:
                                turn_maxima(p + 1)
                        if kt:
                            times_v(p, kt - 1)
                    times_v(p, KT1 - 1)
                for t in range(NT):
                    m = free()
                    if t == 0:
                        o_free.wait(pe, b, PAIRS)
                    for p in range(PAIRS):
                        mm = pe.matmul(m[:, 0:D], o_norm[:, p, P * t:P * (t + 1)], wo[:, p, :],
                                       start=(p == 0), stop=(p == PAIRS - 1))
                    done(mm)
                m_free.wait(pe, b, use[0])
                assert use[0] == M_USES


def feed_forward1(nc, x_all, A):
    with ExitStack() as ctx:
        def sb(name, shape, dt=F32):
            return ctx.enter_context(nc.sbuf_tensor("f1_" + name, shape, dt))

        def ps(name, shape, dt=F32):
            return ctx.enter_context(nc.psum_tensor("f1_" + name, shape, dt))

        def sem(name):
            return ctx.enter_context(nc.semaphore("f1_" + name))

        STREAMS = 2
        BLOCKS = NLIN // 2
        quant = sb("quant", [P, NLIN, DC, D], I32)
        scale = sb("scale", [P, NLIN, DC, D])
        lora_a, lora_b = sb("lora_a", [LR, NLIN, D]), sb("lora_b", [LR, NLIN, D])
        w = sb("w", [P, NLIN, DC, D])
        bias = sb("bias", [P, NLIN, D])
        gamma, beta = sb("gamma", [P, BLOCKS, DC]), sb("beta", [P, BLOCKS, DC])
        ident = sb("ident", [P, P])
        minus_half = sb("minus_half", [P, NT])
        h = sb("h", [P, STREAMS, NT, D])
        h_t = sb("h_t", [P, STREAMS, DC, S])
        y = sb("y", [P, STREAMS, NT, D])
        y_t = sb("y_t", [P, STREAMS, DC, S])
        stats = sb("stats", [P, STREAMS, NT, 6])
        mean_var = sb("mean_var", [P, STREAMS, NT, 2])
        rstd = sb("rstd", [P, STREAMS, NT])

        p_t = ps("p_t", [P, STREAMS, DC, S])
        p_y = ps("p_y", [P, STREAMS, NT, D])

        cleared, consts, loaded = sem("cleared"), sem("consts"), sem("loaded")
        dequant, lora_full, w_ready = sem("dequant"), sem("lora_full"), sem("w_ready")
        NORMS = BLOCKS + 1

        def per_stream(name, per):
            return [Count(sem(f"{name}{u}"), per) for u in range(STREAMS)]

        stats_done = per_stream("stats_done", 3 * NORMS)
        rstd_ready = per_stream("rstd_ready", NORMS)
        h_ready = per_stream("h_ready", 1)
        y_ready = per_stream("y_ready", BLOCKS)
        t_full = per_stream("t_full", 2 * BLOCKS)
        h_t_ready = per_stream("h_t_ready", BLOCKS)
        y_t_ready = per_stream("y_t_ready", BLOCKS)
        lin_full = per_stream("lin_full", 2 * BLOCKS)
        lin_read = per_stream("lin_read", 2 * BLOCKS)
        biased = per_stream("biased", BLOCKS)
        added = per_stream("added", 1)
        block = ctx.enter_context(nc.Block())
        TURNS = B // STREAMS

        @block.sync
        def _(sp):
            for dst, src in ((quant[:], A["f1_q"]), (scale[:], A["f1_scale"]), (lora_a[:], A["f1_la"]),
                             (lora_b[:], A["f1_lb"]), (gamma[:], A["f1_gamma"]), (beta[:], A["f1_beta"])):
                sp.dma_start(dst, src).then_inc(loaded, 16)
            sp.dma_start(bias[:].rearrange("p l d -> p (l d)"), A["f1_bias"].partition_broadcast(P)).then_inc(loaded, 16)

        @block.gpsimd
        def _(pool):
            pool.memset(ident[:], 0.0)
            pool.memset(minus_half[:], -0.5).then_inc(cleared, 1)
            pool.wait_ge(cleared, 1)
            pool.affine_select(out=ident[:], in_=ident[:], compare_op=ALU.not_equal, fill=1.0, base=0,
                               pattern=[[-1, P]], channel_multiplier=1).then_inc(consts, 1)

            def pow_rstd(i, u, n):
                stats_done[u].wait(pool, i, 3 * n + 3)
                pool.tensor_tensor(rstd[:, u, :], rstd[:, u, :], minus_half[:], ALU.pow)\
                    .then_inc(rstd_ready[u].sem, 1)

            pool.wait_ge(loaded, 16 * 7)
            with pool.Fori(0, TURNS) as i:
                for u in range(STREAMS):
                    pow_rstd(i, u, 0)
                for blk in range(BLOCKS):
                    for u in range(STREAMS):
                        pow_rstd(i, u, blk + 1)
                    for u in range(STREAMS):
                        t_full[u].wait(pool, i, 2 * blk + 1)
                        for t in range(NT):
                            last = pool.tensor_tensor(h[:, u, t, :], h[:, u, t, :], bias[:, 2 * blk + 1, :], ALU.add)
                        last.then_inc(biased[u].sem, 1)

        @block.scalar
        def _(act):
            act.wait_ge(loaded, 16 * 7)
            with act.Fori(0, TURNS) as i:
                for blk in range(BLOCKS):
                    for u in range(STREAMS):
                        t_full[u].wait(act, i, 2 * blk + 1)
                        act.activation(h_t[:, u, :, :], p_t[:, u, :, :], ACT.Copy).then_inc(h_t_ready[u].sem, 1)
                    for u in range(STREAMS):
                        t_full[u].wait(act, i, 2 * blk + 2)
                        for c in range(DC):
                            last = act.activation(y_t[:, u, c, :], p_t[:, u, c, :], ACT.Gelu,
                                                  bias=beta[:, blk, c:c + 1], scale=gamma[:, blk, c:c + 1])
                        last.then_inc(y_t_ready[u].sem, 1)

        @block.vector
        def _(dve):
            dve.wait_ge(loaded, 16 * 7)
            flat = lambda t: t[:].rearrange("p l c d -> p (l c d)")
            dve.tensor_scalar(flat(w), flat(quant), 1.0 / 7.5, -1.0, ALU.mult, ALU.add).then_inc(dequant, 1)
            dve.wait_ge(dequant, 1)
            dve.tensor_tensor(flat(w), flat(w), flat(scale), ALU.mult).then_inc(dequant, 1)
            dve.wait_ge(dequant, 2)
            for lin in range(NLIN):
                dve.wait_ge(lora_full, lin + 1)
                dve.tensor_tensor(w[:, lin, :, :], w[:, lin, :, :], p_y[:, lin % 2, 0:DC, :], ALU.add)\
                   .then_inc(w_ready, 1)
            dve.wait_ge(w_ready, NLIN)

            def norm(i, u, n, src):
                for t in range(NT):
                    last = dve.bn_stats(stats[:, u, t, :], src[:, t, :])
                last.then_inc(stats_done[u].sem, 1)
                stats_done[u].wait_apart(dve, i, 3 * n + 1, loaded, 16 * 7)
                for t in range(NT):
                    last = dve.bn_aggr(mean_var[:, u, t, :], stats[:, u, t, :])
                last.then_inc(stats_done[u].sem, 1)
                stats_done[u].wait(dve, i, 3 * n + 2)
                dve.tensor_scalar(rstd[:, u, :], mean_var[:, u, :, 1], EPS, None, ALU.add)\
                   .then_inc(stats_done[u].sem, 1)

            def scale_rows(i, u, n, src, dst, ready):
                rstd_ready[u].wait(dve, i, n + 1)
                for t in range(NT):
                    last = dve.tensor_scalar(dst[:, t, :], src[:, t, :], mean_var[:, u, t, 0:1],
                                             rstd[:, u, t:t + 1], ALU.subtract, ALU.mult)
                last.then_inc(ready.sem, 1)

            with dve.Fori(0, TURNS) as i:
                def x_of(u):
                    return x_all[:, bass.ds((i * STREAMS + u) * NT, NT), :]

                for u in range(STREAMS):
                    norm(i, u, 0, x_of(u))
                for u in range(STREAMS):
                    scale_rows(i, u, 0, x_of(u), h[:, u], h_ready[u])
                for blk in range(BLOCKS):
                    for u in range(STREAMS):
                        lin_full[u].wait(dve, i, 2 * blk + 1)
                        dve.tensor_tensor(y[:, u], p_y[:, u], bias[:, 2 * blk, :].unsqueeze(1).broadcast_to([P, NT, D]),
                                          ALU.add).then_inc(lin_read[u].sem, 1)
                        lin_read[u].wait(dve, i, 2 * blk + 1)
                        norm(i, u, blk + 1, y[:, u])
                    for u in range(STREAMS):
                        scale_rows(i, u, blk + 1, y[:, u], y[:, u], y_ready[u])
                    for u in range(STREAMS):
                        biased[u].wait(dve, i, blk + 1)
                        lin_full[u].wait(dve, i, 2 * blk + 2)
                        dve.tensor_tensor(h[:, u], p_y[:, u], h[:, u], ALU.add).then_inc(lin_read[u].sem, 1)
                        lin_read[u].wait(dve, i, 2 * blk + 2)
                for u in range(STREAMS):
                    dve.tensor_tensor(x_of(u), x_of(u), h[:, u], ALU.add).then_inc(added[u].sem, 1)
                    added[u].wait(dve, i, 1)

        @block.tensor
        def _(pe):
            pe.wait_ge(loaded, 16 * 7)
            pe.wait_ge(consts, 1)
            for lin in range(NLIN):
                if lin >= 2:
                    pe.wait_ge(w_ready, lin - 1)
                for c in range(DC):
                    mm = pe.matmul(p_y[:, lin % 2, c, :], lora_a[:, lin, P * c:P * (c + 1)], lora_b[:, lin, :],
                                   start=True, stop=True)
                mm.then_inc(lora_full, 1)
            pe.wait_ge(w_ready, NLIN)

            def turn(u, src, full):
                for t in range(NT):
                    for c in range(DC):
                        mm = pe.transpose(p_t[:, u, c, P * t:P * (t + 1)], src[:, u, t, P * c:P * (c + 1)], ident[:])
                mm.then_inc(full.sem, 1)

            def linear(u, lin, src_t):
                for t in range(NT):
                    for c in range(DC):
                        mm = pe.matmul(p_y[:, u, t, :], src_t[:, u, c, P * t:P * (t + 1)], w[:, lin, c, :],
                                       start=(c == 0), stop=(c == DC - 1))
                mm.then_inc(lin_full[u].sem, 1)

            with pe.Fori(0, TURNS) as i:
                for blk in range(BLOCKS):
                    for u in range(STREAMS):
                        if blk == 0:
                            h_ready[u].wait(pe, i, 1)
                        else:
                            lin_read[u].wait(pe, i, 2 * blk)
                        turn(u, h, t_full[u])
                    for u in range(STREAMS):
                        h_t_ready[u].wait(pe, i, blk + 1)
                        linear(u, 2 * blk, h_t)
                    for u in range(STREAMS):
                        y_ready[u].wait(pe, i, blk + 1)
                        turn(u, y, t_full[u])
                    for u in range(STREAMS):
                        y_t_ready[u].wait(pe, i, blk + 1)
                        linear(u, 2 * blk + 1, y_t)
                for u in range(STREAMS):
                    lin_read[u].wait(pe, i, 2 * BLOCKS)


def store_x(nc, x_all, A):
    with nc.semaphore("stored") as stored, nc.Block() as block:
        @block.sync
        def _(sp):
            for i in range(B):
                sp.dma_start(A["out"][i].rearrange("(t p) d -> p t d", p=P),
                             x_all[:, i * NT:(i + 1) * NT, :]).then_inc(stored, 16)
            sp.wait_ge(stored, 16 * B)


def build(nc, A, stages):
    with ExitStack() as ctx:
        x_all = ctx.enter_context(nc.sbuf_tensor("x_all", [P, N_TILES, D], F32))
        for stage in stages:
            stage(nc, x_all, A)
        store_x(nc, x_all, A)


def lay_out(inputs):
    import numpy as np

    a = {k: np.asarray(v) for k, v in inputs.items()}

    def rows(w):
        return np.ascontiguousarray(w.reshape(-1, P, w.shape[-1]).transpose(1, 0, 2))

    out = {"x": a["x"]}
    out["ctx_t"] = np.ascontiguousarray(a["ctx_1024"].reshape(B, S, DC, P).transpose(0, 3, 2, 1))
    mask = a["mask_SxS2_bk1"]
    out["mask"] = np.ascontiguousarray(np.stack([rows(mask), rows(np.ascontiguousarray(mask.T))], axis=1))
    turned = lambda w: w.reshape(-1, 2, 8, DH0).transpose(0, 1, 3, 2).reshape(-1, D)
    out["L0_wq"] = rows(turned(a["L0_xattn_Wq"].T))
    out["L0_wk"] = rows(turned(a["L0_xattn_Wk"].T))
    wv = np.zeros((D, H0, SLOT), np.float32)
    wv[:, :, :DH0] = a["L0_xattn_Wv"].T.reshape(D, H0, DH0)
    out["L0_wv"] = rows(wv.reshape(D, H0 * SLOT))
    bv = np.zeros((H0, SLOT), np.float32)
    bv[:, :DH0] = a["L0_xattn_bv"].reshape(H0, DH0)
    bv[:, DH0] = 1.0
    out["L0_bv"] = bv.reshape(-1)
    wo = np.zeros((H0, SLOT, D), np.float32)
    wo[:, :DH0, :] = a["L0_xattn_Wo"].T.reshape(H0, DH0, D)
    out["L0_wo"] = rows(wo.reshape(H0 * SLOT, D))
    out["L0_bo"] = a["L0_xattn_bo"]
    out["L0_bqk"] = np.ascontiguousarray(
        np.stack([turned(a["L0_xattn_bq"]).reshape(2, P), turned(a["L0_xattn_bk"]).reshape(2, P)]).transpose(2, 0, 1))
    out["L0_wr"] = rows(a["L0_ffn_Wr"])
    out["L0_br"] = a["L0_ffn_br"]
    out["L0_w1"] = np.ascontiguousarray(a["L0_ffn_W1"].reshape(E, DC, P, FF).transpose(0, 2, 1, 3))
    out["L0_b1"] = np.ascontiguousarray(a["L0_ffn_b1"].reshape(E, FC, P).transpose(0, 2, 1))
    out["L0_w2"] = np.ascontiguousarray(a["L0_ffn_W2"].reshape(E, FC, P, D).transpose(0, 2, 1, 3))
    out["L0_b2"] = np.ascontiguousarray(np.broadcast_to(a["L0_ffn_b2"][:, None, :], (E, P, D)))
    for k in "qkv":
        out["L1_w" + k] = rows(a[f"L1_xattn_w{k}_w"])
    out["L1_wo"] = rows(a["L1_xattn_wo_w"])
    out["L1_bv"], out["L1_bo"] = a["L1_xattn_wv_b"], a["L1_xattn_wo_b"]
    out["L1_bqk"] = np.ascontiguousarray(
        np.stack([a["L1_xattn_wq_b"].reshape(PAIRS, P), a["L1_xattn_wk_b"].reshape(PAIRS, P)]).transpose(2, 0, 1))
    out["L1_mk"] = np.ascontiguousarray(
        a["L1_xattn_mk"].reshape(MEM, PAIRS, P).transpose(2, 1, 0)).reshape(P, PAIRS * MEM)
    out["L1_mv"] = a["L1_xattn_mv"].reshape(MEM, H1 * DK)
    out["f1_q"] = np.ascontiguousarray(
        a["L1_ffn_qweights"].reshape(NLIN, D, DC, P).transpose(3, 0, 2, 1))
    out["f1_scale"] = np.ascontiguousarray(
        np.repeat(a["L1_ffn_scales"], GROUP, axis=2).reshape(NLIN, D, DC, P).transpose(3, 0, 2, 1))
    out["f1_la"] = np.ascontiguousarray(a["L1_ffn_lora_a"].transpose(1, 0, 2))
    out["f1_lb"] = np.ascontiguousarray(a["L1_ffn_lora_b"].transpose(2, 0, 1))
    out["f1_bias"] = a["L1_ffn_biases"].reshape(-1)
    for k in ("gamma", "beta"):
        out["f1_" + k] = np.ascontiguousarray(a["L1_ffn_ln_" + k].reshape(NLIN // 2, DC, P).transpose(2, 0, 1))
    return out


STAGES = (attention0, mixture, attention1, feed_forward1)


def program(nc, arrays):
    A = {k: nc.dram_tensor("in_" + k, v.shape, U8 if v.dtype == bool else mybir.dt.from_np(v.dtype),
                              kind="ExternalInput").ap()
         for k, v in arrays.items()}
    A["out"] = nc.dram_tensor("out", [B, S, D], F32, kind="ExternalOutput").ap()
    for name in ("x_slots", "y_slots"):
        A[name] = nc.dram_tensor(name, [TILES * CT, D], F32, kind="Internal").ap()
    build(nc, A, STAGES)


def kernel(**inputs):
    import concourse.bacc as bacc
    from concourse.bass_utils import run_bass_kernel_spmd

    arrays = lay_out(inputs)
    nc = bacc.Bacc("TRN2", target_bir_lowering=False, num_devices=1)
    program(nc, arrays)
    result = run_bass_kernel_spmd(nc, [{"in_" + k: v for k, v in arrays.items()}], core_ids=[0])
    return result.results[0]["out"]
```

```python
from contextlib import ExitStack

import concourse.bass as bass
from concourse import mybir

F32 = mybir.dt.float32
F32R = mybir.dt.float32r
BF16 = mybir.dt.bfloat16
I32 = mybir.dt.int32
U32 = mybir.dt.uint32
U8 = mybir.dt.uint8
ALU = mybir.AluOpType
ACT = mybir.ActivationFunctionType
AX = mybir.AxisListType.X

P = 128
B, S, D = 4, 512, 256
NT = S // P
DC = D // P
N_TILES = B * NT
EPS = 1e-5

H0, DH0 = 16, 16
SLOT = 32
G0 = P // SLOT
NG0 = H0 // G0
ROWS0 = 3 * DH0 + 1
MASKED = 2.0 ** 120


H1, DK = 16, 64
MEM = P
PAIRS = H1 // 2
KT1 = NT + 1

NLIN, LR, GROUP = 6, 32, 16

E, FF = 8, 1024
FC = FF // P
CT = 256
TT = CT // P
TILES = B * S // CT + E - 1
RING = 3
assert TILES % RING == 0


class Count:

    def __init__(self, sem, per, before=0):
        self.sem, self.per, self.before = sem, per, before

    def at(self, b, n):
        assert isinstance(b, int) or self.before + n > 0
        return b * self.per + (self.before + n)

    def wait(self, eng, b, n):
        at = self.at(b, n)
        if not isinstance(at, int) or at > 0:
            eng.wait_ge(self.sem, at)

    def wait_apart(self, eng, b, n, met, at):
        value = self.at(b, n)
        if not isinstance(value, int):
            value = eng.to_reg(value)
        eng.wait_ge(met, at)
        eng.wait_ge(self.sem, value)


def attention0(nc, x_all, A):
    with ExitStack() as ctx:
        def sb(name, shape, dt=F32):
            return ctx.enter_context(nc.sbuf_tensor("a0_" + name, shape, dt))

        def ps(name, shape, dt=F32):
            return ctx.enter_context(nc.psum_tensor("a0_" + name, shape, dt))

        def sem(name):
            return ctx.enter_context(nc.semaphore("a0_" + name))

        wq, wk = sb("wq", [P, DC, D]), sb("wk", [P, DC, D])
        wv = sb("wv", [P, DC, H0 * SLOT])
        wo = sb("wo", [P, NG0, D])
        bv = sb("bv", [P, H0 * SLOT])
        bo = sb("bo", [P, D])
        bqk = sb("bqk", [P, 2, 2])
        ident = sb("ident", [P, P])
        ident_b = sb("ident_b", [P, P], BF16)
        spread = sb("spread", [P, P])
        mask_in = sb("mask_in", [P, 2, NT, S], U8)
        bias_q = sb("bias_q", [P, NT, S], BF16)
        bias_k = sb("bias_k", [P, NT, S], BF16)
        least_masked = sb("least_masked", [P, NT])
        nan_row = sb("nan_row", [P, NT])
        ctx_t = sb("ctx_t", [P, DC, S])
        xn = sb("xn", [P, NT, D])
        xn_t = sb("xn_t", [P, DC, S])
        stats = sb("stats", [P, NT, 6])
        mean_var = sb("mean_var", [P, NT, 2])
        rstd = sb("rstd", [P, NT])
        minus_half = sb("minus_half", [P, NT])
        full = sb("full", [P, 2, S])
        hi = sb("hi", [P, 4, S], F32R)
        lo = sb("lo", [P, 4, S], F32R)
        q_stack = sb("q_stack", [ROWS0, H0, S], F32R)
        k_stack = sb("k_stack", [ROWS0, H0, S], F32R)
        v = sb("v", [P, NT, H0 * SLOT])
        probs = sb("probs", [P, 4, 2, S])
        scratch = sb("scratch", [P, 2, S], BF16)
        mx = sb("mx", [P, G0 * NT])
        neg_max = sb("neg_max", [G0 * NT, P], F32R)
        o_raw = sb("o_raw", [P, S])
        recip = sb("recip", [P, S])
        o_norm = sb("o_norm", [P, NG0, S])

        p_s = ps("p_s", [P, 2, 2, S])
        p_m = ps("p_m", [P, 2, S])
        p_o = ps("p_o", [P, S])

        M_USES = NT + 4 + NT + H0 * NT + NG0 + NG0 + NT
        assert M_USES % 2 == 0
        loaded = sem("loaded")
        consts = sem("consts")
        prep = sem("prep")
        ctx_in = Count(sem("ctx_in"), 16)
        stats_done = Count(sem("stats_done"), 3)
        rstd_ready = Count(sem("rstd_ready"), 1)
        xn_ready = Count(sem("xn_ready"), 1)
        m_full = Count(sem("m_full"), M_USES)
        m_free = Count(sem("m_free"), M_USES)
        hi_ready = Count(sem("hi_ready"), 4)
        split_ready = Count(sem("split_ready"), 4)
        stacked = Count(sem("stacked"), 16 * 12)
        nm_ready = Count(sem("nm_ready"), NG0)
        nm_in = Count(sem("nm_in"), 16 * NG0)
        s_full = Count(sem("s_full"), NG0 * 8)
        exp_done = Count(sem("exp_done"), NG0 * 8)
        pv_done = Count(sem("pv_done"), NG0 * NT)
        o_free = Count(sem("o_free"), NG0)
        recip_ready = Count(sem("recip_ready"), NG0)
        norm_ready = Count(sem("norm_ready"), NG0)
        added = Count(sem("added"), NT)

        N_LOADS = 8 + B
        block = ctx.enter_context(nc.Block())

        @block.sync
        def _(sp):
            for dst, src in ((wq[:], A["L0_wq"]), (wk[:], A["L0_wk"]), (wv[:], A["L0_wv"]), (wo[:], A["L0_wo"]),
                             (bv[:], A["L0_bv"].partition_broadcast(P)), (bo[:], A["L0_bo"].partition_broadcast(P)),
                             (bqk[:], A["L0_bqk"]), (mask_in[:], A["mask"])):
                sp.dma_start(dst, src).then_inc(loaded, 16)
            for i in range(B):
                sp.dma_start(x_all[:, i * NT:(i + 1) * NT, :],
                             A["x"][i].rearrange("(t p) d -> p t d", p=P)).then_inc(loaded, 16)
            with sp.Fori(0, B) as b:
                sp.dma_start(ctx_t[:], A["ctx_t"][b]).then_inc(ctx_in.sem, 16)
                for n in range(4):
                    split_ready.wait(sp, b, n + 1)
                    stack, parts = ((q_stack, (hi, hi, lo)), (k_stack, (hi, lo, hi)))[n // 2]
                    for k, part in enumerate(parts):
                        sp.dma_start(stack[DH0 * k:DH0 * (k + 1), 8 * (n % 2):8 * (n % 2 + 1), :].bitcast(F32),
                                     part[:, n, :].bitcast(F32)).then_inc(stacked.sem, 16)
                for g in range(NG0):
                    nm_ready.wait(sp, b, g + 1)
                    sp.dma_start(q_stack[3 * DH0:ROWS0, G0 * g:G0 * (g + 1), :].bitcast(F32), neg_max[:].bitcast(F32))\
                      .then_inc(nm_in.sem, 16)
                m_full.wait_apart(sp, b, 2 * NT + 4, loaded, 16 * N_LOADS)

        @block.gpsimd
        def _(pool):
            pool.memset(ident[:], 0.0)
            pool.memset(ident_b[:], 0.0)
            pool.memset(minus_half[:], -0.5)
            pool.memset(spread[:], 1.0)
            pool.memset(k_stack[:].bitcast(F32), 1.0).then_inc(consts, 1)
            pool.wait_ge(consts, 1)
            for m in (ident, ident_b):
                pool.affine_select(out=m[:], in_=m[:], compare_op=ALU.not_equal, fill=1.0, base=0,
                                   pattern=[[-1, P]], channel_multiplier=1)
            spread_v = spread[:].rearrange("p (g m) -> p g m", g=G0)
            pool.affine_select(out=spread_v, in_=spread_v, compare_op=ALU.is_equal, fill=0.0, base=-DH0,
                               pattern=[[-SLOT, G0], [0, SLOT]], channel_multiplier=1).then_inc(consts, 1)
            with pool.Fori(0, B) as b:
                stats_done.wait(pool, b, 3)
                pool.tensor_tensor(rstd[:], rstd[:], minus_half[:], ALU.pow).then_inc(rstd_ready.sem, 1)

        @block.scalar
        def _(act):
            with act.Fori(0, B) as b:
                for g in range(NG0):
                    for j in range(8):
                        s_full.wait(act, b, 8 * g + j + 1)
                        if g or j >= 4:
                            pv_done.wait(act, b, NT * g + j // 2 - 1)
                        act.activation(probs[:, j % 4, :, :], p_s[:, j % 2, :, :], ACT.Exp)\
                           .then_inc(exp_done.sem, 1)

        @block.vector
        def _(dve):
            dve.wait_ge(loaded, 16 * N_LOADS)
            dve.tensor_scalar(bqk[:, 0, :], bqk[:, 0, :], DH0 ** -0.5, None, ALU.mult)
            dve.tensor_scalar(bias_k[:], mask_in[:, 1, :, :], -MASKED, None, ALU.mult)
            dve.tensor_scalar(bias_q[:], mask_in[:, 0, :, :], -MASKED, None, ALU.mult).then_inc(prep, 1)
            dve.wait_ge(prep, 1)
            dve.tensor_reduce(least_masked[:], bias_q[:], AX, ALU.max).then_inc(prep, 1)
            dve.wait_ge(prep, 2)
            dve.tensor_scalar(nan_row[:], least_masked[:], MASKED, MASKED, ALU.mult, ALU.mult).then_inc(prep, 1)
            dve.wait_ge(prep, 3)
            dve.tensor_tensor(nan_row[:], nan_row[:], nan_row[:], ALU.subtract).then_inc(prep, 1)
            dve.wait_ge(prep, 4)
            with dve.Fori(0, B) as b:
                xb = x_all[:, bass.ds(b * NT, NT), :]
                use = [0]

                def filled(apart=False):
                    use[0] += 1
                    if apart:
                        m_full.wait_apart(dve, b, use[0], prep, 4)
                    else:
                        m_full.wait(dve, b, use[0])
                    return p_m[:, (use[0] - 1) % 2, :]

                for t in range(NT):
                    last = dve.bn_stats(stats[:, t, :], xb[:, t, :])
                last.then_inc(stats_done.sem, 1)
                stats_done.wait_apart(dve, b, 1, prep, 4)
                for t in range(NT):
                    last = dve.bn_aggr(mean_var[:, t, :], stats[:, t, :])
                last.then_inc(stats_done.sem, 1)
                stats_done.wait(dve, b, 2)
                dve.tensor_scalar(rstd[:], mean_var[:, :, 1], EPS, None, ALU.add).then_inc(stats_done.sem, 1)
                rstd_ready.wait(dve, b, 1)
                for t in range(NT):
                    last = dve.tensor_scalar(xn[:, t, :], xb[:, t, :], mean_var[:, t, 0:1], rstd[:, t:t + 1],
                                             ALU.subtract, ALU.mult)
                last.then_inc(xn_ready.sem, 1)
                for t in range(NT):
                    m = filled()
                    dve.tensor_copy(xn_t[:, :, P * t:P * (t + 1)],
                                    m[:, 0:D].rearrange("p (c n) -> p c n", c=DC)).then_inc(m_free.sem, 1)
                for n in range(4):
                    m = filled()
                    if n < 2:
                        dve.tensor_scalar(full[:, n % 2, :], m, DH0 ** -0.5, bqk[:, 0, n:n + 1], ALU.mult,
                                          ALU.add).then_inc(m_free.sem, 1)
                    else:
                        dve.tensor_scalar(full[:, n % 2, :], m, bqk[:, 1, n - 2:n - 1], None,
                                          ALU.add).then_inc(m_free.sem, 1)
                    m_free.wait(dve, b, use[0])
                    dve.tensor_copy(hi[:, n, :], full[:, n % 2, :]).then_inc(hi_ready.sem, 1)
                    hi_ready.wait(dve, b, n + 1)
                    dve.tensor_tensor(lo[:, n, :], full[:, n % 2, :], hi[:, n, :].bitcast(F32),
                                      ALU.subtract).then_inc(split_ready.sem, 1)
                for t in range(NT):
                    m = filled()
                    dve.tensor_tensor(v[:, t, :], m, bv[:], ALU.add).then_inc(m_free.sem, 1)

                def maxima(n):
                    for i in range(n, min(n + 3, G0 * NT)):
                        m = filled(apart=True)
                        dve.tensor_tensor_reduce(scratch[:, use[0] % 2, :], m, bias_q[:, i % NT, :], 1.0, -3.0e38, ALU.add,
                                                 ALU.max, mx[:, i:i + 1]).then_inc(m_free.sem, 1)

                def turn_maxima(g):
                    m = filled()
                    if g:
                        nm_in.wait(dve, b, 16 * g)
                    dve.tensor_scalar(neg_max[:], m[0:G0 * NT, 0:P], -1.0, None, ALU.mult)\
                       .then_inc(nm_ready.sem, 1)
                    nm_ready.wait_apart(dve, b, g + 1, prep, 4)
                    dve.engine_nop().then_inc(m_free.sem, 1)

                def normalize(g):
                    m = filled()
                    dve.reciprocal(recip[:], m).then_inc(recip_ready.sem, 1)
                    recip_ready.wait(dve, b, g + 1)
                    dve.tensor_tensor(o_norm[:, g, :], o_raw[:], recip[:], ALU.mult).then_inc(m_free.sem, 1)

                for i in range(0, G0 * NT, 3):
                    maxima(i)
                turn_maxima(0)
                for g in range(NG0):
                    for j in range(8):
                        if j == 2 and g:
                            normalize(g - 1)
                        if g + 1 < NG0:
                            maxima(3 * j)
                            if j == 5:
                                turn_maxima(g + 1)
                    pv_done.wait(dve, b, NT * (g + 1))
                    m_free.wait(dve, b, use[0])
                    dve.tensor_copy(o_raw[:], p_o[:]).then_inc(o_free.sem, 1)
                normalize(NG0 - 1)
                for t in range(NT):
                    m = filled()
                    dve.scalar_tensor_tensor(out=xn[:, t, :], in0=m[:, 0:D], scalar=nan_row[:, t:t + 1], in1=bo[:],
                                             op0=ALU.add, op1=ALU.add).then_inc(m_free.sem, 1)
                    m_free.wait(dve, b, use[0])
                    dve.tensor_tensor(xb[:, t, :], xb[:, t, :], xn[:, t, :], ALU.add).then_inc(added.sem, 1)
                added.wait(dve, b, NT)
                stacked.wait(dve, b, 16 * 12)
                assert use[0] == M_USES

        @block.tensor
        def _(pe):
            pe.wait_ge(loaded, 16 * N_LOADS)
            pe.wait_ge(consts, 2)
            pe.wait_ge(prep, 4)
            with pe.Fori(0, B) as b:
                use = [0]

                def free():
                    if use[0] >= 2:
                        m_free.wait(pe, b, use[0] - 1)
                    use[0] += 1
                    return p_m[:, (use[0] - 1) % 2, :]

                def done(mm):
                    mm.then_inc(m_full.sem, 1)

                xn_ready.wait(pe, b, 1)
                for t in range(NT):
                    m = free()
                    for c in range(DC):
                        mm = pe.transpose(m[:, c * P:(c + 1) * P], xn[:, t, c * P:(c + 1) * P], ident[:])
                    done(mm)
                ctx_in.wait(pe, b, 16)
                for n in range(4):
                    m = free()
                    if n == 0:
                        m_free.wait(pe, b, NT)
                    w, src = ((wq, xn_t), (wk, ctx_t))[n // 2]
                    for c in range(DC):
                        mm = pe.matmul(m, w[:, c, P * (n % 2):P * (n % 2 + 1)], src[:, c, :],
                                       start=(c == 0), stop=(c == DC - 1))
                    done(mm)
                for t in range(NT):
                    m = free()
                    for c in range(DC):
                        mm = pe.matmul(m, ctx_t[:, c, P * t:P * (t + 1)], wv[:, c, :],
                                       start=(c == 0), stop=(c == DC - 1))
                    done(mm)

                def maxima(g, n):
                    for i in range(n, min(n + 3, G0 * NT)):
                        h, t = G0 * g + i // NT, i % NT
                        m = free()
                        if g == 0 and i == 0:
                            stacked.wait(pe, b, 16 * 12)
                        done(pe.matmul(m, q_stack[0:3 * DH0, h, P * t:P * (t + 1)], k_stack[0:3 * DH0, h, :],
                                       start=True, stop=True))

                def turn_maxima():
                    m = free()
                    m_free.wait(pe, b, use[0] - 1)
                    done(pe.transpose(m[0:G0 * NT, 0:P], mx[:], ident[:]))

                def spread_sums(g):
                    m = free()
                    o_free.wait(pe, b, g + 1)
                    done(pe.matmul(m, spread[:], o_raw[:], start=True, stop=True))

                def scores(g, j):
                    kt, slot = j // 2, j % 2
                    if j == 0:
                        nm_in.wait(pe, b, 16 * (g + 1))
                    n = 8 * g + j
                    if n >= 2:
                        exp_done.wait(pe, b, n - 1)
                    for i in range(2):
                        h = G0 * g + 2 * slot + i
                        pe.matmul(p_s[:, slot, i, :], k_stack[:, h, P * kt:P * (kt + 1)], q_stack[:, h, :],
                                  start=True, stop=False)
                        mm = pe.matmul(p_s[:, slot, i, :], ident_b[:], bias_k[:, kt, :], start=False, stop=True)
                    mm.then_inc(s_full.sem, 1)

                def times_v(g, kt):
                    exp_done.wait(pe, b, 8 * g + 2 * kt + 2)
                    if kt == 0 and g:
                        o_free.wait(pe, b, g)
                    for i in range(G0):
                        h = G0 * g + i
                        mm = pe.matmul(p_o[SLOT * i:SLOT * (i + 1), :], v[:, kt, SLOT * h:SLOT * (h + 1)],
                                       probs[:, (2 * kt + i // 2) % 4, i % 2, :], start=(kt == 0),
                                       stop=(kt == NT - 1))
                    mm.then_inc(pv_done.sem, 1)

                for i in range(0, G0 * NT, 3):
                    maxima(0, i)
                turn_maxima()
                for g in range(NG0):
                    for j in range(8):
                        scores(g, j)
                        if j == 2 and g:
                            spread_sums(g - 1)
                        if g + 1 < NG0:
                            maxima(g + 1, 3 * j)
                            if j == 5:
                                turn_maxima()
                        if j % 2 == 0 and j:
                            times_v(g, j // 2 - 1)
                    times_v(g, NT - 1)
                spread_sums(NG0 - 1)
                for t in range(NT):
                    m = free()
                    if t == 0:
                        m_free.wait(pe, b, use[0] - 1)
                    for g in range(NG0):
                        mm = pe.matmul(m[:, 0:D], o_norm[:, g, P * t:P * (t + 1)], wo[:, g, :],
                                       start=(g == 0), stop=(g == NG0 - 1))
                    done(mm)
                m_free.wait(pe, b, use[0])
                assert use[0] == M_USES


def route(nc, x_all, xn_all, slot, gate, owner, A):
    with ExitStack() as ctx:
        def sb(name, shape, dt=F32):
            return ctx.enter_context(nc.sbuf_tensor("r_" + name, shape, dt))

        def ps(name, shape, dt=F32):
            return ctx.enter_context(nc.psum_tensor("r_" + name, shape, dt))

        def sem(name):
            return ctx.enter_context(nc.semaphore("r_" + name))

        wr = sb("wr", [P, DC, E])
        br = sb("br", [P, E])
        zeros = sb("zeros", [P, 6 * D])
        ident = sb("ident", [P, P])
        before = sb("before", [P, P])
        ones = sb("ones", [P, P])
        expert_id = sb("expert_id", [P, N_TILES, E])
        steps_of = sb("steps_of", [P, E, B * S // CT])
        tile_id = sb("tile_id", [P, TILES, E])
        xn = sb("xn", [P, NT, D])
        xn_t = sb("xn_t", [P, DC, S])
        stats = sb("stats", [P, NT, 6])
        mean_var = sb("mean_var", [P, NT, 2])
        rstd = sb("rstd", [P, NT])
        minus_half = sb("minus_half", [P, NT])
        logits = sb("logits", [P, N_TILES, E])
        top = sb("top", [P, N_TILES])
        shifted = sb("shifted", [P, N_TILES, E])
        exps = sb("exps", [P, N_TILES, E])
        total = sb("total", [P, N_TILES])
        chosen = sb("chosen", [P, N_TILES])
        one_hot = sb("one_hot", [P, N_TILES, E])
        prior = sb("prior", [P, N_TILES, E])
        count = sb("count", [P, E])
        over = sb("over", [P, E, B * S // CT])
        tiles = sb("tiles", [P, E])
        start = sb("start", [P, E])
        end = sb("end", [P, E])
        past = sb("past", [P, TILES, E])
        slot_f = sb("slot_f", [P, N_TILES])
        owner_f = sb("owner_f", [P, TILES])

        p_t = ps("p_t", [P, 2, S])
        p_l = ps("p_l", [P, NT, E])
        p_rank = ps("p_rank", [P, N_TILES * E])
        p_sum = ps("p_sum", [P, N_TILES * E])

        consts, filled = sem("consts"), sem("filled")
        loaded, cleared = sem("loaded"), sem("cleared")
        stats_done = Count(sem("stats_done"), 3)
        rstd_ready = Count(sem("rstd_ready"), 1)
        xn_ready = Count(sem("xn_ready"), 1)
        kept = Count(sem("kept"), 1)
        turned = Count(sem("turned"), NT)
        copied = Count(sem("copied"), NT)
        l_full = Count(sem("l_full"), 1)
        l_read = Count(sem("l_read"), 1)
        shifted_ready, exps_ready, hot_ready = sem("shifted_ready"), sem("exps_ready"), sem("hot_ready")
        ranked, step_done, slots_ready, scattered = sem("ranked"), sem("step_done"), sem("slots_ready"), sem("scattered")
        block = ctx.enter_context(nc.Block())

        @block.sync
        def _(sp):
            sp.dma_start(wr[:], A["L0_wr"]).then_inc(loaded, 16)
            sp.dma_start(br[:], A["L0_br"].partition_broadcast(P)).then_inc(loaded, 16)
            sp.wait_ge(filled, 1)
            rows = TILES * CT // 5
            for i in range(5):
                sp.dma_start(A["x_slots"][i * rows:(i + 1) * rows, :].rearrange("(p r) d -> p (r d)", p=P),
                             zeros[:]).then_inc(cleared, 16)

        @block.gpsimd
        def _(pool):
            pool.memset(zeros[:], 0.0).then_inc(filled, 1)
            pool.memset(ident[:], 0.0)
            pool.memset(before[:], 1.0)
            pool.memset(ones[:], 1.0)
            pool.memset(minus_half[:], -0.5)
            pool.iota(expert_id[:], pattern=[[0, N_TILES], [1, E]], base=-E, channel_multiplier=0,
                      allow_small_or_imprecise_dtypes=True)
            pool.iota(steps_of[:], pattern=[[0, E], [CT, B * S // CT]], base=0, channel_multiplier=0,
                      allow_small_or_imprecise_dtypes=True)
            pool.iota(tile_id[:], pattern=[[1, TILES], [0, E]], base=0, channel_multiplier=0,
                      allow_small_or_imprecise_dtypes=True).then_inc(filled, 1)
            pool.wait_ge(filled, 2)
            pool.affine_select(out=ident[:], in_=ident[:], compare_op=ALU.not_equal, fill=1.0, base=0,
                               pattern=[[-1, P]], channel_multiplier=1)
            pool.affine_select(out=before[:], in_=before[:], compare_op=ALU.is_gt, fill=0.0, base=0,
                               pattern=[[1, P]], channel_multiplier=-1).then_inc(consts, 1)
            with pool.Fori(0, B) as b:
                stats_done.wait(pool, b, 3)
                pool.tensor_tensor(rstd[:], rstd[:], minus_half[:], ALU.pow).then_inc(rstd_ready.sem, 1)
                xn_ready.wait(pool, b, 1)
                pool.tensor_copy(xn_all[:, bass.ds(b * NT, NT), :], xn[:]).then_inc(kept.sem, 1)
            pool.wait_ge(kept.sem, B)
            pool.wait_ge(cleared, 16 * 5)
            pool.wait_ge(slots_ready, 1)
            for t in range(N_TILES):
                pool.indirect_dma_start(out=A["x_slots"], out_offset=bass.IndirectOffsetOnAxis(ap=slot[:, t:t + 1], axis=0),
                                        in_=xn_all[:, t, :], in_offset=None).then_inc(scattered, 16)
            pool.wait_ge(scattered, 16 * N_TILES)

        @block.scalar
        def _(act):
            act.wait_ge(shifted_ready, 1)
            act.activation(exps[:], shifted[:], ACT.Exp).then_inc(exps_ready, 1)

        @block.vector
        def _(dve):
            dve.wait_ge(loaded, 32)
            with dve.Fori(0, B) as b:
                xb = x_all[:, bass.ds(b * NT, NT), :]
                for t in range(NT):
                    last = dve.bn_stats(stats[:, t, :], xb[:, t, :])
                last.then_inc(stats_done.sem, 1)
                stats_done.wait_apart(dve, b, 1, loaded, 32)
                for t in range(NT):
                    last = dve.bn_aggr(mean_var[:, t, :], stats[:, t, :])
                last.then_inc(stats_done.sem, 1)
                stats_done.wait(dve, b, 2)
                dve.tensor_scalar(rstd[:], mean_var[:, :, 1], EPS, None, ALU.add).then_inc(stats_done.sem, 1)
                rstd_ready.wait(dve, b, 1)
                for t in range(NT):
                    last = dve.tensor_scalar(xn[:, t, :], xb[:, t, :], mean_var[:, t, 0:1], rstd[:, t:t + 1],
                                             ALU.subtract, ALU.mult)
                last.then_inc(xn_ready.sem, 1)
                for t in range(NT):
                    turned.wait(dve, b, t + 1)
                    dve.tensor_copy(xn_t[:, :, P * t:P * (t + 1)],
                                    p_t[:, t % 2, 0:D].rearrange("p (c n) -> p c n", c=DC)).then_inc(copied.sem, 1)
                l_full.wait(dve, b, 1)
                dve.tensor_tensor(logits[:, bass.ds(b * NT, NT), :], p_l[:],
                                  br[:].unsqueeze(1).broadcast_to([P, NT, E]), ALU.add).then_inc(l_read.sem, 1)
                kept.wait(dve, b, 1)
            dve.wait_ge(l_read.sem, B)
            dve.wait_ge(consts, 1)
            n = [0]

            def step(ins):
                n[0] += 1
                ins.then_inc(step_done, 1)
                dve.wait_ge(step_done, n[0])

            def over_tiles(v):
                return v.unsqueeze(2).broadcast_to([P, N_TILES, E])

            step(dve.tensor_reduce(top[:], logits[:], AX, ALU.max))
            dve.tensor_tensor(shifted[:], logits[:], over_tiles(top[:]), ALU.subtract).then_inc(shifted_ready, 1)
            step(dve.tensor_tensor(one_hot[:], logits[:], over_tiles(top[:]), ALU.is_ge))
            step(dve.tensor_tensor(one_hot[:], one_hot[:], expert_id[:], ALU.mult))
            step(dve.tensor_reduce(chosen[:], one_hot[:], AX, ALU.min))
            step(dve.tensor_scalar(chosen[:], chosen[:], -1.0, None, ALU.min))
            dve.tensor_tensor(one_hot[:], expert_id[:], over_tiles(chosen[:]), ALU.is_equal).then_inc(hot_ready, 1)
            dve.wait_ge(exps_ready, 1)
            step(dve.tensor_reduce(total[:], exps[:], AX, ALU.add))
            dve.reciprocal(gate[:], total[:])
            dve.wait_ge(ranked, 1)
            p_sum_v = p_sum[:].rearrange("p (t e) -> p t e", e=E)
            step(dve.memset(prior[:, 0, :], 0.0))
            for t in range(1, N_TILES):
                step(dve.tensor_tensor(prior[:, t, :], p_sum_v[:, t - 1, :], prior[:, t - 1, :], ALU.add))
            step(dve.tensor_tensor(count[:], p_sum_v[:, N_TILES - 1, :], prior[:, N_TILES - 1, :], ALU.add))
            step(dve.tensor_tensor(over[:], count[:].unsqueeze(2).broadcast_to([P, E, B * S // CT]), steps_of[:],
                                   ALU.is_gt))
            step(dve.tensor_reduce(tiles[:], over[:], AX, ALU.add))
            step(dve.memset(start[:, 0:1], 0.0))
            for e in range(1, E):
                step(dve.tensor_tensor(start[:, e:e + 1], start[:, e - 1:e], tiles[:, e - 1:e], ALU.add))
            step(dve.tensor_tensor(end[:], start[:], tiles[:], ALU.add))
            step(dve.tensor_tensor(past[:], tile_id[:], end[:].unsqueeze(1).broadcast_to([P, TILES, E]), ALU.is_ge))
            step(dve.tensor_reduce(owner_f[:], past[:], AX, ALU.add))
            dve.tensor_scalar(owner[:], owner_f[:], float(E - 1), None, ALU.min)
            step(dve.tensor_scalar(start[:], start[:], float(CT), None, ALU.mult))
            step(dve.tensor_tensor(prior[:], prior[:], start[:].unsqueeze(1).broadcast_to([P, N_TILES, E]), ALU.add))
            step(dve.tensor_tensor(prior[:], p_rank[:].rearrange("p (t e) -> p t e", e=E), prior[:], ALU.add))
            step(dve.tensor_tensor(prior[:], prior[:], one_hot[:], ALU.mult))
            step(dve.tensor_reduce(slot_f[:], prior[:], AX, ALU.add))
            dve.tensor_copy(slot[:], slot_f[:]).then_inc(slots_ready, 1)

        @block.tensor
        def _(pe):
            pe.wait_ge(loaded, 32)
            pe.wait_ge(consts, 1)
            with pe.Fori(0, B) as b:
                xn_ready.wait(pe, b, 1)
                for t in range(NT):
                    if t >= 2:
                        copied.wait(pe, b, t - 1)
                    for c in range(DC):
                        mm = pe.transpose(p_t[:, t % 2, c * P:(c + 1) * P], xn[:, t, c * P:(c + 1) * P], ident[:])
                    mm.then_inc(turned.sem, 1)
                copied.wait(pe, b, NT)
                for t in range(NT):
                    for c in range(DC):
                        mm = pe.matmul(p_l[:, t, :], xn_t[:, c, P * t:P * (t + 1)], wr[:, c, :],
                                       start=(c == 0), stop=(c == DC - 1))
                mm.then_inc(l_full.sem, 1)
                l_read.wait(pe, b, 1)
            pe.wait_ge(hot_ready, 1)
            hot = one_hot[:].rearrange("p t e -> p (t e)")
            pe.matmul(p_rank[:], before[:], hot, start=True, stop=True)
            pe.matmul(p_sum[:], ones[:], hot, start=True, stop=True).then_inc(ranked, 1)


def experts(nc, x_all, slot, gate, owner, A):
    with ExitStack() as ctx:
        def sb(name, shape, dt=F32):
            return ctx.enter_context(nc.sbuf_tensor("e_" + name, shape, dt))

        def ps(name, shape, dt=F32):
            return ctx.enter_context(nc.psum_tensor("e_" + name, shape, dt))

        def sem(name):
            return ctx.enter_context(nc.semaphore("e_" + name))

        ident = sb("ident", [P, P])
        rows = sb("rows", [P, RING, TT, D])
        w1 = sb("w1", [P, RING, DC, FF])
        w2 = sb("w2", [P, RING, FC, D])
        b1 = sb("b1", [P, RING, FC])
        b2 = sb("b2", [P, RING, D])
        rows_t = sb("rows_t", [P, 2, DC, CT])
        hidden = sb("hidden", [P, 4, CT])
        y = sb("y", [P, RING, TT, D])
        back = sb("back", [P, N_TILES, D])

        p_t = ps("p_t", [P, DC, CT])
        p_h = ps("p_h", [P, 4, S])
        p_y = ps("p_y", [P, TT, S])

        cleared, consts = sem("cleared"), sem("consts")
        rows_in = [Count(sem(f"rows_in{r}"), 16) for r in range(RING)]
        w_in = [Count(sem(f"w_in{r}"), 64) for r in range(RING)]
        turned = Count(sem("turned"), RING)
        rows_t_ready = Count(sem("rows_t_ready"), RING)
        h_full = Count(sem("h_full"), RING * FC)
        h_ready = Count(sem("h_ready"), RING * FC)
        h_used = Count(sem("h_used"), RING * FC)
        y_ready = Count(sem("y_ready"), RING)
        y_stored = Count(sem("y_stored"), 16 * RING)
        gathered, scaled = sem("gathered"), sem("scaled")
        block = ctx.enter_context(nc.Block())
        TURNS = TILES // RING

        @block.sync
        def _(sp):
            def load(i, r):
                e = sp.value_load(owner[0:1, bass.ds(i * RING + r, 1)], min_val=0, max_val=E - 1)
                sp.dma_start(rows[:, r, :, :], A["x_slots"][bass.ds((i * RING + r) * CT, CT), :]
                             .rearrange("(t p) d -> p t d", p=P)).then_inc(rows_in[r].sem, 16)
                sp.dma_start(w1[:, r, :, :], A["L0_w1"][bass.ds(e, 1)].rearrange("o p c f -> p (o c) f"))\
                  .then_inc(w_in[r].sem, 16)
                sp.dma_start(b1[:, r, :], A["L0_b1"][bass.ds(e, 1)].rearrange("o p c -> p (o c)"))\
                  .then_inc(w_in[r].sem, 16)
                sp.dma_start(b2[:, r, :], A["L0_b2"][bass.ds(e, 1)].rearrange("o p d -> p (o d)"))\
                  .then_inc(w_in[r].sem, 16)
                sp.dma_start(w2[:, r, :, :], A["L0_w2"][bass.ds(e, 1)].rearrange("o p c d -> p (o c) d"))\
                  .then_inc(w_in[r].sem, 16)

            for r in range(RING):
                load(0, r)
            with sp.Fori(0, TURNS - 1) as i:
                for r in range(RING):
                    y_ready.wait(sp, i, r + 1)
                    load(i + 1, r)

        @block.gpsimd
        def _(pool):
            pool.memset(ident[:], 0.0).then_inc(cleared, 1)
            pool.wait_ge(cleared, 1)
            pool.affine_select(out=ident[:], in_=ident[:], compare_op=ALU.not_equal, fill=1.0, base=0,
                               pattern=[[-1, P]], channel_multiplier=1).then_inc(consts, 1)
            with pool.Fori(0, TURNS) as i:
                for r in range(RING):
                    y_ready.wait(pool, i, r + 1)
                    pool.dma_start(A["y_slots"][bass.ds((i * RING + r) * CT, CT), :]
                                   .rearrange("(t p) d -> p t d", p=P), y[:, r, :, :]).then_inc(y_stored.sem, 16)
            pool.wait_ge(y_stored.sem, 16 * TILES)
            for t in range(N_TILES):
                pool.indirect_dma_start(out=back[:, t, :], out_offset=None, in_=A["y_slots"],
                                        in_offset=bass.IndirectOffsetOnAxis(ap=slot[:, t:t + 1], axis=0))\
                    .then_inc(gathered, 16)

        @block.scalar
        def _(act):
            with act.Fori(0, TURNS) as i:
                for r in range(RING):
                    for c in range(FC):
                        n = FC * r + c
                        h_full.wait(act, i, n + 1)
                        if c == 0:
                            w_in[r].wait(act, i, 64)
                        if n >= 4:
                            h_used.wait(act, i, n - 3)
                        act.activation(hidden[:, c % 4, :], p_h[:, c % 4, 0:CT], ACT.Gelu, bias=b1[:, r, c:c + 1])\
                           .then_inc(h_ready.sem, 1)
                h_used.wait(act, i, RING * FC)

        @block.vector
        def _(dve):
            with dve.Fori(0, TURNS) as i:
                for r in range(RING):
                    turned.wait(dve, i, r + 1)
                    dve.tensor_copy(rows_t[:, r % 2, :, :], p_t[:]).then_inc(rows_t_ready.sem, 1)
                    h_used.wait(dve, i, FC * (r + 1))
                    if r:
                        y_stored.wait(dve, i, 16 * r)
                    dve.tensor_tensor(y[:, r, :, :], p_y[:, :, 0:D], b2[:, r, :].unsqueeze(1).broadcast_to([P, TT, D]),
                                      ALU.add).then_inc(y_ready.sem, 1)
            dve.wait_ge(gathered, 16 * N_TILES)
            for t in range(N_TILES):
                dve.scalar_tensor_tensor(out=x_all[:, t, :], in0=back[:, t, :], scalar=gate[:, t:t + 1],
                                         in1=x_all[:, t, :], op0=ALU.mult, op1=ALU.add).then_inc(scaled, 1)
            dve.wait_ge(scaled, N_TILES)

        @block.tensor
        def _(pe):
            pe.wait_ge(consts, 1)
            with pe.Fori(0, TURNS) as i:
                for r in range(RING):
                    rows_in[r].wait(pe, i, 16)
                    for t in range(TT):
                        for c in range(DC):
                            mm = pe.transpose(p_t[:, c, P * t:P * (t + 1)], rows[:, r, t, P * c:P * (c + 1)], ident[:])
                    mm.then_inc(turned.sem, 1)
                    w_in[r].wait(pe, i, 64)
                    rows_t_ready.wait(pe, i, r + 1)
                    for c in range(FC + 2):
                        if c < FC:
                            n = FC * r + c
                            if n >= 4:
                                h_ready.wait(pe, i, n - 3)
                            for k in range(DC):
                                mm = pe.matmul(p_h[:, c % 4, 0:CT], w1[:, r, k, P * c:P * (c + 1)],
                                               rows_t[:, r % 2, k, :], start=(k == 0), stop=(k == DC - 1))
                            mm.then_inc(h_full.sem, 1)
                        if c >= 2:
                            d = c - 2
                            h_ready.wait(pe, i, FC * r + d + 1)
                            if d == 0 and r:
                                y_ready.wait(pe, i, r)
                            for t in range(TT):
                                mm = pe.matmul(p_y[:, t, 0:D], hidden[:, d % 4, P * t:P * (t + 1)], w2[:, r, d, :],
                                               start=(d == 0), stop=(d == FC - 1))
                            mm.then_inc(h_used.sem, 1)
                y_ready.wait(pe, i, RING)


def mixture(nc, x_all, A):
    with nc.sbuf_tensor("slot", [P, N_TILES], U32) as slot, nc.sbuf_tensor("gate", [P, N_TILES], F32) as gate, \
         nc.sbuf_tensor("owner", [P, TILES], I32) as owner:
        with nc.sbuf_tensor("xn_all", [P, N_TILES, D], F32) as xn_all:
            route(nc, x_all, xn_all, slot, gate, owner, A)
        experts(nc, x_all, slot, gate, owner, A)


def attention1(nc, x_all, A):
    with ExitStack() as ctx:
        def sb(name, shape, dt=F32):
            return ctx.enter_context(nc.sbuf_tensor("a1_" + name, shape, dt))

        def ps(name, shape, dt=F32):
            return ctx.enter_context(nc.psum_tensor("a1_" + name, shape, dt))

        def sem(name):
            return ctx.enter_context(nc.semaphore("a1_" + name))

        HD = H1 * DK
        ROWS = DK + 1
        HELD = 4
        assert PAIRS % HELD == 0
        wq, wk, wv = sb("wq", [P, DC, HD]), sb("wk", [P, DC, HD]), sb("wv", [P, DC, HD])
        wo = sb("wo", [P, PAIRS, D])
        bv = sb("bv", [P, HD])
        bo = sb("bo", [P, D])
        bqk = sb("bqk", [P, 2, PAIRS])
        ident = sb("ident", [P, P])
        ones = sb("ones", [P, DK])
        ctx_t = sb("ctx_t", [P, DC, S])
        xn_t = sb("xn_t", [P, DC, S])
        stats = sb("stats", [P, NT, 6])
        mean_var = sb("mean_var", [P, NT, 2])
        rstd = sb("rstd", [P, NT])
        minus_half = sb("minus_half", [P, NT])
        full = sb("full", [P, 2, S])
        hi = sb("hi", [P, 2, S], F32R)
        lo = sb("lo", [P, 2, S], F32R)
        q_hh = sb("q_hh", [P, 2 * HELD, S], F32R)
        k_hl = sb("k_hl", [P, 2 * HELD, S], F32R)
        q_lm = sb("q_lm", [ROWS, 2 * HELD, S], F32R)
        k_h1 = sb("k_h1", [ROWS, 2 * HELD, S], F32R)
        mem_hl = sb("mem_hl", [P, 2, PAIRS, MEM], F32R)
        mem_h1 = sb("mem_h1", [ROWS, 2, PAIRS, MEM], F32R)
        v = sb("v", [P, 2, NT, 2 * P])
        mem_v = sb("mem_v", [P, HD])
        probs = sb("probs", [P, KT1, 2, S])
        max_ctx = sb("max_ctx", [P, 2 * NT])
        max_mem = sb("max_mem", [P, 2 * NT])
        mx = sb("mx", [P, 2 * NT])
        neg_max = sb("neg_max", [2 * NT, P], F32R)
        recip = sb("recip", [P, S])
        o_norm = sb("o_norm", [P, PAIRS, S])
        xn = o_norm[:, PAIRS - 2:PAIRS, :].rearrange("p a (t d) -> p (a t) d", d=D)

        p_s = ps("p_s", [P, 2, 2, S])
        p_m = ps("p_m", [P, 2, S])
        p_o = ps("p_o", [P, S])
        p_sum = ps("p_sum", [P, S])

        STEPS = (("query", "maximum", "score", "score", "maximum", "times_v", "maximum"),
                 ("key", "maximum", "score", "score", "maximum", "times_v"),
                 ("maximum", "score", "maximum", "score", "maximum", "times_v", "total"),
                 ("maximum", "score", "maximum", "score", "times_v", "value"),
                 ("turn", "score", "score", "times_v", "value", "rows"))
        PER_MAX = 2 * (NT + 1)

        def steps(p, kt, ahead):
            for what in STEPS[kt]:
                if what == "value" and (p % 2 == 0 or p == PAIRS - 1):
                    continue
                if what == "rows" and (p != PAIRS - 3 or not ahead):
                    continue
                if not ahead and (what in ("query", "key") and p + 2 >= PAIRS
                                  or what in ("maximum", "turn") and p + 1 >= PAIRS):
                    continue
                yield what

        FILLS = {"query": 1, "key": 1, "maximum": 1, "turn": 1, "value": 1, "rows": NT}
        DVE_FILLS = {"maximum": 1, "value": 1, "rows": NT}

        def fills(kinds, last_p=PAIRS - 1, last=None):
            return sum(kinds.get(w, 0) for p in range(last_p + 1) for kt in range(KT1) for w in steps(p, kt, True))

        BEFORE = NT + 4 + 2 + PER_MAX + 1
        DVE_BEFORE = NT + 2 + PER_MAX
        PER = fills(FILLS) + 2 + NT
        assert PER % 2 == 0
        loaded, filled_s, consts, prep = sem("loaded"), sem("filled"), sem("consts"), sem("prep")
        mem_in = sem("mem_in")
        ctx_in = Count(sem("ctx_in"), 16)
        stats_done = Count(sem("stats_done"), 3)
        rstd_ready = Count(sem("rstd_ready"), 1)
        xn_ready = Count(sem("xn_ready"), 1)
        biased = Count(sem("biased"), 1)
        m_full = Count(sem("m_full"), PER, BEFORE)
        m_free = Count(sem("m_free"), fills(DVE_FILLS) + 2 + NT, DVE_BEFORE)
        hi_ready = Count(sem("hi_ready"), 2 * PAIRS)
        full_ready = Count(sem("full_ready"), 2 * PAIRS)
        split_ready = Count(sem("split_ready"), 2 * PAIRS)
        stacked = Count(sem("stacked"), 16 * 6 * PAIRS)
        mx_ready = Count(sem("mx_ready"), PAIRS)
        nm_ready = Count(sem("nm_ready"), PAIRS)
        nm_in = Count(sem("nm_in"), 16 * PAIRS)
        s_full = Count(sem("s_full"), KT1 * PAIRS)
        exp_done = Count(sem("exp_done"), KT1 * PAIRS)
        pv_done = Count(sem("pv_done"), KT1 * PAIRS)
        tile_added = Count(sem("tile_added"), NT * PAIRS)
        summed = Count(sem("summed"), PAIRS)
        o_read = Count(sem("o_read"), PAIRS)
        sum_read = Count(sem("sum_read"), PAIRS)
        norm_ready = Count(sem("norm_ready"), PAIRS)
        added = Count(sem("added"), NT)
        block = ctx.enter_context(nc.Block())

        class Fill:

            def __init__(self, start=0):
                self.n = start

            def bank(self):
                self.n += 1
                return p_m[:, (BEFORE + self.n - 1) % 2, :]

        @block.sync
        def _(sp):
            for dst, src in ((xn_t[:].rearrange("p c n -> p (c n)"), A["L1_mk"]), (bqk[:], A["L1_bqk"]),
                             (wq[:], A["L1_wq"]), (wk[:], A["L1_wk"]), (wv[:], A["L1_wv"]), (wo[:], A["L1_wo"]),
                             (bv[:], A["L1_bv"].partition_broadcast(P)), (bo[:], A["L1_bo"].partition_broadcast(P)),
                             (mem_v[:], A["L1_mv"])):
                sp.dma_start(dst, src).then_inc(loaded, 16)
            sp.wait_ge(prep, 3)
            for dst, part in ((mem_hl[0:DK], hi), (mem_hl[DK:P], lo), (mem_h1[0:DK], hi)):
                sp.dma_start(dst.rearrange("p i a n -> p i (a n)").bitcast(F32),
                             part[:].rearrange("p a n -> p (a n)").bitcast(F32)).then_inc(mem_in, 16)

            def stack(b, p):
                for n in range(2):
                    split_ready.wait(sp, b, 2 * p + n + 1)
                    parts = (((q_hh[0:DK], hi), (q_hh[DK:P], hi), (q_lm[0:DK], lo)),
                             ((k_hl[0:DK], hi), (k_hl[DK:P], lo), (k_h1[0:DK], hi)))[n]
                    for dst, part in parts:
                        sp.dma_start(dst[:, 2 * (p % HELD):2 * (p % HELD) + 2, :].bitcast(F32),
                                     part[:, n, :].bitcast(F32)).then_inc(stacked.sem, 16)

            def bring_maxima(b, p):
                nm_ready.wait(sp, b, p + 1)
                s = 2 * (p % HELD)
                sp.dma_start(q_lm[DK:ROWS, s:s + 2, :].bitcast(F32), neg_max[:].bitcast(F32))\
                  .then_inc(nm_in.sem, 16)

            def turn(b, ahead):
                for p in range(PAIRS):
                    if ahead or p + 2 < PAIRS:
                        stack(b, p + 2)
                    if ahead or p + 1 < PAIRS:
                        bring_maxima(b, p + 1)
                    if p == PAIRS - 3 and ahead:
                        m_full.wait(sp, b, fills(FILLS, p))
                        sp.dma_start(ctx_t[:], A["ctx_t"][b + 1]).then_inc(ctx_in.sem, 16)

            sp.dma_start(ctx_t[:], A["ctx_t"][0]).then_inc(ctx_in.sem, 16)
            stack(-1, PAIRS)
            stack(-1, PAIRS + 1)
            bring_maxima(-1, PAIRS)
            with sp.Fori(0, B - 1) as b:
                turn(b, True)
            turn(B - 1, False)

        @block.gpsimd
        def _(pool):
            pool.memset(ident[:], 0.0)
            pool.memset(ones[:], 1.0)
            pool.memset(minus_half[:], -0.5)
            pool.memset(k_h1[:].bitcast(F32), 1.0)
            pool.memset(mem_h1[:].bitcast(F32), 1.0).then_inc(filled_s, 1)
            pool.wait_ge(filled_s, 1)
            pool.affine_select(out=ident[:], in_=ident[:], compare_op=ALU.not_equal, fill=1.0, base=0,
                               pattern=[[-1, P]], channel_multiplier=1).then_inc(consts, 1)
            pool.wait_ge(loaded, 16 * 9)

            def invert_deviation(b):
                stats_done.wait(pool, b, 3 + 3)
                pool.tensor_tensor(rstd[:], rstd[:], minus_half[:], ALU.pow).then_inc(rstd_ready.sem, 1)

            def bias(b):
                xn_ready.wait(pool, b, 1 + 1)
                xb = x_all[:, bass.ds((b + 1) * NT, NT), :]
                pool.tensor_tensor(xb, xb, bo[:].unsqueeze(1).broadcast_to([P, NT, D]), ALU.add)\
                    .then_inc(biased.sem, 1)

            def add_tile(b, p, kt):
                if kt > 1:
                    tile_added.wait(pool, b, NT * p + kt - 1)
                pv_done.wait(pool, b, KT1 * p + kt + 1)
                pool.tensor_tensor(probs[:, kt], probs[:, kt - 1], probs[:, kt], ALU.add)\
                    .then_inc(tile_added.sem, 1)

            def turn(b, ahead):
                for p in range(PAIRS):
                    if ahead and p == PAIRS - 4:
                        invert_deviation(b)
                    for kt in range(1, KT1):
                        add_tile(b, p, kt)
                    if ahead and p == PAIRS - 2:
                        bias(b)

            invert_deviation(-1)
            bias(-1)
            with pool.Fori(0, B - 1) as b:
                turn(b, True)
            turn(B - 1, False)

        @block.scalar
        def _(act):
            act.wait_ge(loaded, 16 * 9)
            act.wait_ge(mem_in, 16 * 3)

            def project(b, p, n, m):
                split_ready.wait(act, b, 2 * p + n - 1)
                stacked.wait(act, b, 16 * 6 * p)
                act.activation(full[:, n, :], m, ACT.Identity, bias=bqk[:, n, p % PAIRS:p % PAIRS + 1],
                               scale=(DK ** -0.5, 1.0)[n]).then_inc(full_ready.sem, 1)
                act.activation(hi[:, n, :], m, ACT.Identity, bias=bqk[:, n, p % PAIRS:p % PAIRS + 1],
                               scale=(DK ** -0.5, 1.0)[n]).then_inc(hi_ready.sem, 1)

            def exps(b, p, kt):
                s_full.wait(act, b, KT1 * p + kt + 1)
                if p and kt < NT:
                    tile_added.wait(act, b, NT * (p - 1) + kt + 1)
                elif p:
                    summed.wait(act, b, p)
                act.activation(probs[:, kt, :, :], p_s[:, (KT1 * p + kt) % 2, :, :], ACT.Exp).then_inc(exp_done.sem, 1)

            def read_output(b, p):
                pv_done.wait(act, b, KT1 * (p + 1))
                act.activation(o_norm[:, p, :], p_o[:], ACT.Copy).then_inc(o_read.sem, 1)

            def turn(b, ahead):
                fill = Fill()
                for p in range(PAIRS):
                    for kt in range(KT1):
                        heads = 0
                        for what in steps(p, kt, ahead):
                            if what in ("query", "key"):
                                m = fill.bank()
                                m_full.wait(act, b, fill.n)
                                project(b, p + 2, ("query", "key").index(what), m)
                            elif what in FILLS:
                                for _ in range(FILLS[what]):
                                    fill.bank()
                            elif what == "score":
                                heads += 1
                                if heads == 2:
                                    exps(b, p, kt)
                            elif what == "times_v" and kt == 0 and p:
                                read_output(b, p - 1)
                read_output(b, PAIRS - 1)
                norm_ready.wait(act, b, PAIRS)

            fill = Fill(PER - BEFORE + NT)
            for p in range(2):
                for n in range(2):
                    m = fill.bank()
                    m_full.wait(act, -1, fill.n)
                    project(-1, PAIRS + p, n, m)
            with act.Fori(0, B - 1) as b:
                turn(b, True)
            turn(B - 1, False)

        @block.vector
        def _(dve):
            dve.wait_ge(loaded, 16 * 9)
            dve.wait_ge(consts, 1)
            mem_keys = xn_t[:].rearrange("p c n -> p (c n)")
            flat = lambda t: t[:].rearrange("p c n -> p (c n)")
            dve.tensor_scalar(bqk[:, 0, :], bqk[:, 0, :], DK ** -0.5, None, ALU.mult).then_inc(prep, 1)
            dve.tensor_copy(flat(hi), mem_keys).then_inc(prep, 1)
            dve.wait_ge(prep, 2)
            dve.tensor_tensor(flat(lo), mem_keys, flat(hi).bitcast(F32), ALU.subtract).then_inc(prep, 1)
            dve.wait_ge(mem_in, 16 * 3)

            def begin_norm(b):
                xb = x_all[:, bass.ds((b + 1) * NT, NT), :]
                for t in range(NT):
                    last = dve.bn_stats(stats[:, t, :], xb[:, t, :])
                last.then_inc(stats_done.sem, 1)
                stats_done.wait_apart(dve, b, 3 + 1, prep, 3)
                for t in range(NT):
                    last = dve.bn_aggr(mean_var[:, t, :], stats[:, t, :])
                last.then_inc(stats_done.sem, 1)
                stats_done.wait(dve, b, 3 + 2)
                dve.tensor_scalar(rstd[:], mean_var[:, :, 1], EPS, None, ALU.add).then_inc(stats_done.sem, 1)

            def end_norm(b):
                xb = x_all[:, bass.ds((b + 1) * NT, NT), :]
                rstd_ready.wait(dve, b, 1 + 1)
                for t in range(NT):
                    last = dve.tensor_scalar(xn[:, t, :], xb[:, t, :], mean_var[:, t, 0:1], rstd[:, t:t + 1],
                                             ALU.subtract, ALU.mult)
                last.then_inc(xn_ready.sem, 1)

            def turned_rows(b, fill):
                for t in range(NT):
                    m = fill.bank()
                    m_full.wait(dve, b, fill.n)
                    dve.tensor_copy(xn_t[:, :, P * t:P * (t + 1)],
                                    m[:, 0:D].rearrange("p (c n) -> p c n", c=DC)).then_inc(m_free.sem, 1)

            def values(b, fill, group, half):
                m = fill.bank()
                m_full.wait(dve, b, fill.n)
                cols = bv[:, 2 * P * (group % 4):2 * P * (group % 4 + 1)]
                dve.tensor_tensor(v[:, group % 2, 2 * half:2 * half + 2, :], m.rearrange("p (t d) -> p t d", t=2),
                                  cols.unsqueeze(1).broadcast_to([P, 2, 2 * P]), ALU.add).then_inc(m_free.sem, 1)

            def split(b, p, n):
                hi_ready.wait(dve, b, 2 * p + n + 1)
                if n == 0:
                    stacked.wait(dve, b, 16 * 6 * p)
                dve.tensor_tensor(lo[:, n, :], full[:, n, :], hi[:, n, :].bitcast(F32),
                                  ALU.subtract).then_inc(split_ready.sem, 1)

            def maximum(b, fill, i):
                m = fill.bank()
                m_full.wait(dve, b, fill.n)
                head, t = i // (NT + 1), i % (NT + 1)
                if t < NT:
                    dve.tensor_reduce(max_ctx[:, NT * head + t:NT * head + t + 1], m, AX, ALU.max)\
                       .then_inc(m_free.sem, 1)
                else:
                    dve.tensor_reduce(max_mem[:, NT * head:NT * (head + 1)],
                                      m.rearrange("p (t n) -> p t n", n=MEM), AX, ALU.max)\
                       .then_inc(m_free.sem, 1)

            def join_maxima(b, done):
                m_free.wait(dve, b, done)
                dve.tensor_tensor(mx[:], max_ctx[:], max_mem[:], ALU.max).then_inc(mx_ready.sem, 1)

            def turn_maxima(b, fill, p):
                m = fill.bank()
                m_full.wait(dve, b, fill.n)
                nm_in.wait(dve, b, 16 * p)
                dve.tensor_scalar(neg_max[:], m[0:2 * NT, 0:P], -1.0, None, ALU.mult)\
                   .then_inc(nm_ready.sem, 1)

            def normalize(b, p):
                if p:
                    norm_ready.wait(dve, b, p)
                summed.wait(dve, b, p + 1)
                dve.reciprocal(recip[:], p_sum[:]).then_inc(sum_read.sem, 1)
                sum_read.wait(dve, b, p + 1)
                o_read.wait(dve, b, p + 1)
                dve.tensor_tensor(o_norm[:, p, :], o_norm[:, p, :], recip[:], ALU.mult).then_inc(norm_ready.sem, 1)

            def turn(b, ahead):
                fill = Fill()
                freed = 0
                for p in range(PAIRS):
                    i = 0
                    for kt in range(KT1):
                        for what in steps(p, kt, ahead):
                            freed += DVE_FILLS.get(what, 0)
                            if what == "times_v" and kt == 4 and p:
                                normalize(b, p - 1)
                            elif what == "maximum":
                                maximum(b, fill, i)
                                i += 1
                                if i == PER_MAX:
                                    join_maxima(b, freed)
                            elif what == "turn":
                                turn_maxima(b, fill, p + 1)
                            elif what == "value":
                                values(b, fill, p // 2 + 1, kt - 3)
                            elif what == "rows":
                                turned_rows(b, fill)
                            elif what in FILLS:
                                fill.bank()
                        if kt in (1, 2) and (ahead or p + 2 < PAIRS):
                            split(b, p + 2, kt - 1)
                    if ahead and p == PAIRS - 5:
                        begin_norm(b)
                    if ahead and p == PAIRS - 4:
                        end_norm(b)
                if ahead:
                    for half in range(2):
                        values(b, fill, 4, half)
                normalize(b, PAIRS - 1)
                xb = x_all[:, bass.ds(b * NT, NT), :]
                biased.wait(dve, b, 1)
                for t in range(NT):
                    m = fill.bank()
                    m_full.wait(dve, b, fill.n)
                    dve.tensor_tensor(xb[:, t, :], xb[:, t, :], m[:, 0:D], ALU.add).then_inc(m_free.sem, 1)

            fill = Fill(PER - BEFORE)
            begin_norm(-1)
            end_norm(-1)
            turned_rows(-1, fill)
            for p in range(2):
                for n in range(2):
                    fill.bank()
                    split(-1, PAIRS + p, n)
            for half in range(2):
                values(-1, fill, 4, half)
            for i in range(PER_MAX):
                maximum(-1, fill, i)
            join_maxima(-1, m_free.per)
            turn_maxima(-1, fill, PAIRS)
            with dve.Fori(0, B - 1) as b:
                turn(b, True)
            turn(B - 1, False)

        @block.tensor
        def _(pe):
            pe.wait_ge(loaded, 16 * 9)
            pe.wait_ge(consts, 1)
            pe.wait_ge(prep, 3)
            pe.wait_ge(mem_in, 16 * 3)

            class Banks(Fill):

                def __init__(self, b, start=0, freed=0):
                    super().__init__(start)
                    self.b, self.freed, self.readers = b, freed, []

                def free(self, count=m_free, n=None):
                    if len(self.readers) >= 2:
                        before, at = self.readers[-2]
                        before.wait(pe, self.b, at)
                    if n is None:
                        self.freed += 1
                        n = self.freed
                    self.readers.append((count, n))
                    return self.bank()

            def done(mm):
                mm.then_inc(m_full.sem, 1)

            def turn_rows(b, banks):
                xn_ready.wait(pe, b, 1 + 1)
                for t in range(NT):
                    m = banks.free()
                    for c in range(DC):
                        mm = pe.transpose(m[:, c * P:(c + 1) * P], xn[:, t, c * P:(c + 1) * P], ident[:])
                    done(mm)

            def project(b, banks, p, n):
                m = banks.free(full_and_hi, 2 * p + n + 1)
                if p == PAIRS:
                    if n == 0:
                        m_free.wait(pe, b, banks.freed)
                    else:
                        ctx_in.wait(pe, b, 16 + 16)
                w, src = ((wq, xn_t), (wk, ctx_t))[n]
                at = P * (p % PAIRS)
                for c in range(DC):
                    mm = pe.matmul(m, w[:, c, at:at + P], src[:, c, :], start=(c == 0), stop=(c == DC - 1))
                done(mm)

            full_and_hi = hi_ready

            def values(b, banks, group, half):
                m = banks.free()
                at = 2 * P * (group % 4)
                for i in range(2):
                    t = 2 * half + i
                    for c in range(DC):
                        mm = pe.matmul(m[:, 2 * P * i:2 * P * (i + 1)], ctx_t[:, c, P * t:P * (t + 1)],
                                       wv[:, c, at:at + 2 * P], start=(c == 0), stop=(c == DC - 1))
                done(mm)

            def maximum(b, banks, p, i):
                head, t = i // (NT + 1), i % (NT + 1)
                s = 2 * (p % HELD) + head
                m = banks.free()
                if i == 0:
                    stacked.wait(pe, b, 16 * 6 * (p + 1))
                if t < NT:
                    done(pe.matmul(m, q_hh[:, s, P * t:P * (t + 1)], k_hl[:, s, :], start=True, stop=True))
                else:
                    for t in range(NT):
                        mm = pe.matmul(m[:, MEM * t:MEM * (t + 1)], q_hh[:, s, P * t:P * (t + 1)],
                                       mem_hl[:, head, p % PAIRS, :], start=True, stop=True)
                    done(mm)

            def turn_maxima(b, banks, p):
                m = banks.free(nm_ready, p + 1)
                mx_ready.wait(pe, b, p + 1)
                done(pe.transpose(m[0:2 * NT, 0:P], mx[:], ident[:]))

            def score(b, p, kt, i):
                n = KT1 * p + kt
                if kt == 0 and i == 0:
                    nm_in.wait(pe, b, 16 * (p + 1))
                if n >= 2 and i == 0:
                    exp_done.wait(pe, b, n - 1)
                s = 2 * (p % HELD) + i
                if kt < NT:
                    first, second = (t[:, s, P * kt:P * (kt + 1)] for t in (k_hl, k_h1))
                else:
                    first, second = (t[:, i, p, :] for t in (mem_hl, mem_h1))
                pe.matmul(p_s[:, n % 2, i, :], first, q_hh[:, s, :], start=True, stop=False)
                mm = pe.matmul(p_s[:, n % 2, i, :], second, q_lm[:, s, :], start=False, stop=True)
                if i == 1:
                    mm.then_inc(s_full.sem, 1)

            def times_v(b, p, kt):
                exp_done.wait(pe, b, KT1 * p + kt + 1)
                if kt == 0 and p:
                    o_read.wait(pe, b, p)
                for i in range(2):
                    if kt < NT:
                        vh = v[:, p // 2 % 2, kt, P * (p % 2) + DK * i:P * (p % 2) + DK * (i + 1)]
                    else:
                        vh = mem_v[:, P * p + DK * i:P * p + DK * (i + 1)]
                    mm = pe.matmul(p_o[DK * i:DK * (i + 1), :], vh, probs[:, kt, i, :],
                                   start=(kt == 0), stop=(kt == KT1 - 1))
                mm.then_inc(pv_done.sem, 1)

            def total(b, p):
                tile_added.wait(pe, b, NT * (p + 1))
                if p:
                    sum_read.wait(pe, b, p)
                for i in range(2):
                    mm = pe.matmul(p_sum[DK * i:DK * (i + 1), :], ones[:], probs[:, NT, i, :], start=True, stop=True)
                mm.then_inc(summed.sem, 1)

            def turn(b, ahead):
                m_free.wait(pe, b, 0)
                nm_ready.wait(pe, b, 1)
                banks = Banks(b)
                for p in range(PAIRS):
                    i = 0
                    for kt in range(KT1):
                        head = 0
                        for what in steps(p, kt, ahead):
                            if what in ("query", "key"):
                                project(b, banks, p + 2, ("query", "key").index(what))
                            elif what == "maximum":
                                maximum(b, banks, p + 1, i)
                                i += 1
                            elif what == "turn":
                                turn_maxima(b, banks, p + 1)
                            elif what == "score":
                                score(b, p, kt, head)
                                head += 1
                            elif what == "times_v" and kt:
                                times_v(b, p, kt - 1)
                            elif what == "times_v" and p:
                                times_v(b, p - 1, KT1 - 1)
                            elif what == "value":
                                values(b, banks, p // 2 + 1, kt - 3)
                            elif what == "total" and p:
                                total(b, p - 1)
                            elif what == "rows":
                                turn_rows(b, banks)
                times_v(b, PAIRS - 1, KT1 - 1)
                if ahead:
                    for half in range(2):
                        values(b, banks, 4, half)
                total(b, PAIRS - 1)
                for t in range(NT):
                    m = banks.free()
                    if t == 0:
                        norm_ready.wait(pe, b, PAIRS)
                    for p in range(PAIRS):
                        mm = pe.matmul(m[:, 0:D], o_norm[:, p, P * t:P * (t + 1)], wo[:, p, :],
                                       start=(p == 0), stop=(p == PAIRS - 1))
                    done(mm)
                assert not ahead or (banks.n == m_full.per and banks.freed == m_free.per)

            banks = Banks(-1, m_full.per - BEFORE, m_free.per - DVE_BEFORE)
            turn_rows(-1, banks)
            for p in range(2):
                for n in range(2):
                    project(-1, banks, PAIRS + p, n)
            for half in range(2):
                values(-1, banks, 4, half)
            for i in range(PER_MAX):
                maximum(-1, banks, PAIRS, i)
            turn_maxima(-1, banks, PAIRS)
            with pe.Fori(0, B - 1) as b:
                turn(b, True)
            turn(B - 1, False)


def feed_forward1(nc, x_all, A):
    with ExitStack() as ctx:
        def sb(name, shape, dt=F32):
            return ctx.enter_context(nc.sbuf_tensor("f1_" + name, shape, dt))

        def ps(name, shape, dt=F32):
            return ctx.enter_context(nc.psum_tensor("f1_" + name, shape, dt))

        def sem(name):
            return ctx.enter_context(nc.semaphore("f1_" + name))

        STREAMS = 2
        BLOCKS = NLIN // 2
        quant = sb("quant", [P, NLIN, DC, D], I32)
        scale = sb("scale", [P, NLIN, DC, D])
        lora_a, lora_b = sb("lora_a", [LR, NLIN, D]), sb("lora_b", [LR, NLIN, D])
        w = sb("w", [P, NLIN, DC, D])
        bias = sb("bias", [P, NLIN, D])
        gamma, beta = sb("gamma", [P, BLOCKS, DC]), sb("beta", [P, BLOCKS, DC])
        ident = sb("ident", [P, P])
        minus_half = sb("minus_half", [P, NT])
        h = sb("h", [P, STREAMS, NT, D])
        h_t = sb("h_t", [P, STREAMS, DC, S])
        y = sb("y", [P, STREAMS, NT, D])
        y_t = sb("y_t", [P, STREAMS, DC, S])
        stats = sb("stats", [P, STREAMS, NT, 6])
        mean_var = sb("mean_var", [P, STREAMS, NT, 2])
        rstd = sb("rstd", [P, STREAMS, NT])

        p_t = ps("p_t", [P, STREAMS, DC, S])
        p_y = ps("p_y", [P, STREAMS, NT, D])

        cleared, consts, loaded = sem("cleared"), sem("consts"), sem("loaded")
        dequant, lora_full, w_ready = sem("dequant"), sem("lora_full"), sem("w_ready")
        NORMS = BLOCKS + 1

        def per_stream(name, per):
            return [Count(sem(f"{name}{u}"), per) for u in range(STREAMS)]

        stats_done = per_stream("stats_done", 3 * NORMS)
        rstd_ready = per_stream("rstd_ready", NORMS)
        h_ready = per_stream("h_ready", 1)
        y_ready = per_stream("y_ready", BLOCKS)
        t_full = per_stream("t_full", 2 * BLOCKS)
        h_t_ready = per_stream("h_t_ready", BLOCKS)
        y_t_ready = per_stream("y_t_ready", BLOCKS)
        lin_full = per_stream("lin_full", 2 * BLOCKS)
        lin_read = per_stream("lin_read", 2 * BLOCKS)
        biased = per_stream("biased", BLOCKS)
        added = per_stream("added", 1)
        block = ctx.enter_context(nc.Block())
        TURNS = B // STREAMS

        @block.sync
        def _(sp):
            for dst, src in ((quant[:], A["f1_q"]), (scale[:], A["f1_scale"]), (lora_a[:], A["f1_la"]),
                             (lora_b[:], A["f1_lb"]), (gamma[:], A["f1_gamma"]), (beta[:], A["f1_beta"])):
                sp.dma_start(dst, src).then_inc(loaded, 16)
            sp.dma_start(bias[:].rearrange("p l d -> p (l d)"), A["f1_bias"].partition_broadcast(P)).then_inc(loaded, 16)

        @block.gpsimd
        def _(pool):
            pool.memset(ident[:], 0.0)
            pool.memset(minus_half[:], -0.5).then_inc(cleared, 1)
            pool.wait_ge(cleared, 1)
            pool.affine_select(out=ident[:], in_=ident[:], compare_op=ALU.not_equal, fill=1.0, base=0,
                               pattern=[[-1, P]], channel_multiplier=1).then_inc(consts, 1)

            def pow_rstd(i, u, n):
                stats_done[u].wait(pool, i, 3 * n + 3)
                pool.tensor_tensor(rstd[:, u, :], rstd[:, u, :], minus_half[:], ALU.pow)\
                    .then_inc(rstd_ready[u].sem, 1)

            pool.wait_ge(loaded, 16 * 7)
            with pool.Fori(0, TURNS) as i:
                for u in range(STREAMS):
                    pow_rstd(i, u, 0)
                for blk in range(BLOCKS):
                    for u in range(STREAMS):
                        pow_rstd(i, u, blk + 1)
                    for u in range(STREAMS):
                        t_full[u].wait(pool, i, 2 * blk + 1)
                        for t in range(NT):
                            last = pool.tensor_tensor(h[:, u, t, :], h[:, u, t, :], bias[:, 2 * blk + 1, :], ALU.add)
                        last.then_inc(biased[u].sem, 1)

        @block.scalar
        def _(act):
            act.wait_ge(loaded, 16 * 7)
            with act.Fori(0, TURNS) as i:
                for blk in range(BLOCKS):
                    for u in range(STREAMS):
                        t_full[u].wait(act, i, 2 * blk + 1)
                        act.activation(h_t[:, u, :, :], p_t[:, u, :, :], ACT.Copy).then_inc(h_t_ready[u].sem, 1)
                    for u in range(STREAMS):
                        t_full[u].wait(act, i, 2 * blk + 2)
                        for c in range(DC):
                            last = act.activation(y_t[:, u, c, :], p_t[:, u, c, :], ACT.Gelu,
                                                  bias=beta[:, blk, c:c + 1], scale=gamma[:, blk, c:c + 1])
                        last.then_inc(y_t_ready[u].sem, 1)

        @block.vector
        def _(dve):
            dve.wait_ge(loaded, 16 * 7)
            flat = lambda t: t[:].rearrange("p l c d -> p (l c d)")
            dve.tensor_scalar(flat(w), flat(quant), 1.0 / 7.5, -1.0, ALU.mult, ALU.add).then_inc(dequant, 1)
            dve.wait_ge(dequant, 1)
            dve.tensor_tensor(flat(w), flat(w), flat(scale), ALU.mult).then_inc(dequant, 1)
            dve.wait_ge(dequant, 2)
            for lin in range(NLIN):
                dve.wait_ge(lora_full, lin + 1)
                dve.tensor_tensor(w[:, lin, :, :], w[:, lin, :, :], p_y[:, lin % 2, 0:DC, :], ALU.add)\
                   .then_inc(w_ready, 1)
            dve.wait_ge(w_ready, NLIN)

            def norm(i, u, n, src):
                for t in range(NT):
                    last = dve.bn_stats(stats[:, u, t, :], src[:, t, :])
                last.then_inc(stats_done[u].sem, 1)
                stats_done[u].wait_apart(dve, i, 3 * n + 1, loaded, 16 * 7)
                for t in range(NT):
                    last = dve.bn_aggr(mean_var[:, u, t, :], stats[:, u, t, :])
                last.then_inc(stats_done[u].sem, 1)
                stats_done[u].wait(dve, i, 3 * n + 2)
                dve.tensor_scalar(rstd[:, u, :], mean_var[:, u, :, 1], EPS, None, ALU.add)\
                   .then_inc(stats_done[u].sem, 1)

            def scale_rows(i, u, n, src, dst, ready):
                rstd_ready[u].wait(dve, i, n + 1)
                for t in range(NT):
                    last = dve.tensor_scalar(dst[:, t, :], src[:, t, :], mean_var[:, u, t, 0:1],
                                             rstd[:, u, t:t + 1], ALU.subtract, ALU.mult)
                last.then_inc(ready.sem, 1)

            with dve.Fori(0, TURNS) as i:
                def x_of(u):
                    return x_all[:, bass.ds((i * STREAMS + u) * NT, NT), :]

                for u in range(STREAMS):
                    norm(i, u, 0, x_of(u))
                for u in range(STREAMS):
                    scale_rows(i, u, 0, x_of(u), h[:, u], h_ready[u])
                for blk in range(BLOCKS):
                    for u in range(STREAMS):
                        lin_full[u].wait(dve, i, 2 * blk + 1)
                        dve.tensor_tensor(y[:, u], p_y[:, u], bias[:, 2 * blk, :].unsqueeze(1).broadcast_to([P, NT, D]),
                                          ALU.add).then_inc(lin_read[u].sem, 1)
                        lin_read[u].wait(dve, i, 2 * blk + 1)
                        norm(i, u, blk + 1, y[:, u])
                    for u in range(STREAMS):
                        scale_rows(i, u, blk + 1, y[:, u], y[:, u], y_ready[u])
                    for u in range(STREAMS):
                        biased[u].wait(dve, i, blk + 1)
                        lin_full[u].wait(dve, i, 2 * blk + 2)
                        dve.tensor_tensor(h[:, u], p_y[:, u], h[:, u], ALU.add).then_inc(lin_read[u].sem, 1)
                        lin_read[u].wait(dve, i, 2 * blk + 2)
                for u in range(STREAMS):
                    dve.tensor_tensor(x_of(u), x_of(u), h[:, u], ALU.add).then_inc(added[u].sem, 1)
                    added[u].wait(dve, i, 1)

        @block.tensor
        def _(pe):
            pe.wait_ge(loaded, 16 * 7)
            pe.wait_ge(consts, 1)
            for lin in range(NLIN):
                if lin >= 2:
                    pe.wait_ge(w_ready, lin - 1)
                for c in range(DC):
                    mm = pe.matmul(p_y[:, lin % 2, c, :], lora_a[:, lin, P * c:P * (c + 1)], lora_b[:, lin, :],
                                   start=True, stop=True)
                mm.then_inc(lora_full, 1)
            pe.wait_ge(w_ready, NLIN)

            def turn(u, src, full):
                for t in range(NT):
                    for c in range(DC):
                        mm = pe.transpose(p_t[:, u, c, P * t:P * (t + 1)], src[:, u, t, P * c:P * (c + 1)], ident[:])
                mm.then_inc(full.sem, 1)

            def linear(u, lin, src_t):
                for t in range(NT):
                    for c in range(DC):
                        mm = pe.matmul(p_y[:, u, t, :], src_t[:, u, c, P * t:P * (t + 1)], w[:, lin, c, :],
                                       start=(c == 0), stop=(c == DC - 1))
                mm.then_inc(lin_full[u].sem, 1)

            with pe.Fori(0, TURNS) as i:
                for blk in range(BLOCKS):
                    for u in range(STREAMS):
                        if blk == 0:
                            h_ready[u].wait(pe, i, 1)
                        else:
                            lin_read[u].wait(pe, i, 2 * blk)
                        turn(u, h, t_full[u])
                    for u in range(STREAMS):
                        h_t_ready[u].wait(pe, i, blk + 1)
                        linear(u, 2 * blk, h_t)
                    for u in range(STREAMS):
                        y_ready[u].wait(pe, i, blk + 1)
                        turn(u, y, t_full[u])
                    for u in range(STREAMS):
                        y_t_ready[u].wait(pe, i, blk + 1)
                        linear(u, 2 * blk + 1, y_t)
                for u in range(STREAMS):
                    lin_read[u].wait(pe, i, 2 * BLOCKS)


def store_x(nc, x_all, A):
    with nc.semaphore("stored") as stored, nc.Block() as block:
        @block.sync
        def _(sp):
            for i in range(B):
                sp.dma_start(A["out"][i].rearrange("(t p) d -> p t d", p=P),
                             x_all[:, i * NT:(i + 1) * NT, :]).then_inc(stored, 16)
            sp.wait_ge(stored, 16 * B)


def build(nc, A, stages):
    with ExitStack() as ctx:
        x_all = ctx.enter_context(nc.sbuf_tensor("x_all", [P, N_TILES, D], F32))
        for stage in stages:
            stage(nc, x_all, A)
        store_x(nc, x_all, A)


def lay_out(inputs):
    import numpy as np

    a = {k: np.asarray(v) for k, v in inputs.items()}

    def rows(w):
        return np.ascontiguousarray(w.reshape(-1, P, w.shape[-1]).transpose(1, 0, 2))

    out = {"x": a["x"]}
    out["ctx_t"] = np.ascontiguousarray(a["ctx_1024"].reshape(B, S, DC, P).transpose(0, 3, 2, 1))
    mask = a["mask_SxS2_bk1"]
    out["mask"] = np.ascontiguousarray(np.stack([rows(mask), rows(np.ascontiguousarray(mask.T))], axis=1))
    turned = lambda w: w.reshape(-1, 2, 8, DH0).transpose(0, 1, 3, 2).reshape(-1, D)
    out["L0_wq"] = rows(turned(a["L0_xattn_Wq"].T))
    out["L0_wk"] = rows(turned(a["L0_xattn_Wk"].T))
    wv = np.zeros((D, H0, SLOT), np.float32)
    wv[:, :, :DH0] = a["L0_xattn_Wv"].T.reshape(D, H0, DH0)
    out["L0_wv"] = rows(wv.reshape(D, H0 * SLOT))
    bv = np.zeros((H0, SLOT), np.float32)
    bv[:, :DH0] = a["L0_xattn_bv"].reshape(H0, DH0)
    bv[:, DH0] = 1.0
    out["L0_bv"] = bv.reshape(-1)
    wo = np.zeros((H0, SLOT, D), np.float32)
    wo[:, :DH0, :] = a["L0_xattn_Wo"].T.reshape(H0, DH0, D)
    out["L0_wo"] = rows(wo.reshape(H0 * SLOT, D))
    out["L0_bo"] = a["L0_xattn_bo"]
    out["L0_bqk"] = np.ascontiguousarray(
        np.stack([turned(a["L0_xattn_bq"]).reshape(2, P), turned(a["L0_xattn_bk"]).reshape(2, P)]).transpose(2, 0, 1))
    out["L0_wr"] = rows(a["L0_ffn_Wr"])
    out["L0_br"] = a["L0_ffn_br"]
    out["L0_w1"] = np.ascontiguousarray(a["L0_ffn_W1"].reshape(E, DC, P, FF).transpose(0, 2, 1, 3))
    out["L0_b1"] = np.ascontiguousarray(a["L0_ffn_b1"].reshape(E, FC, P).transpose(0, 2, 1))
    out["L0_w2"] = np.ascontiguousarray(a["L0_ffn_W2"].reshape(E, FC, P, D).transpose(0, 2, 1, 3))
    out["L0_b2"] = np.ascontiguousarray(np.broadcast_to(a["L0_ffn_b2"][:, None, :], (E, P, D)))
    paired = lambda w: w.reshape(-1, PAIRS, 2, DK).transpose(0, 1, 3, 2).reshape(-1, H1 * DK)
    for k in "qk":
        out["L1_w" + k] = rows(paired(a[f"L1_xattn_w{k}_w"]))
    out["L1_wv"] = rows(a["L1_xattn_wv_w"])
    out["L1_wo"] = rows(a["L1_xattn_wo_w"])
    out["L1_bv"], out["L1_bo"] = a["L1_xattn_wv_b"], a["L1_xattn_wo_b"]
    out["L1_bqk"] = np.ascontiguousarray(
        np.stack([paired(a["L1_xattn_wq_b"]).reshape(PAIRS, P),
                  paired(a["L1_xattn_wk_b"]).reshape(PAIRS, P)]).transpose(2, 0, 1))
    out["L1_mk"] = np.ascontiguousarray(
        paired(a["L1_xattn_mk"][0]).reshape(MEM, PAIRS, P).transpose(2, 1, 0)).reshape(P, PAIRS * MEM)
    out["L1_mv"] = a["L1_xattn_mv"].reshape(MEM, H1 * DK)
    out["f1_q"] = np.ascontiguousarray(
        a["L1_ffn_qweights"].reshape(NLIN, D, DC, P).transpose(3, 0, 2, 1))
    out["f1_scale"] = np.ascontiguousarray(
        np.repeat(a["L1_ffn_scales"], GROUP, axis=2).reshape(NLIN, D, DC, P).transpose(3, 0, 2, 1))
    out["f1_la"] = np.ascontiguousarray(a["L1_ffn_lora_a"].transpose(1, 0, 2))
    out["f1_lb"] = np.ascontiguousarray(a["L1_ffn_lora_b"].transpose(2, 0, 1))
    out["f1_bias"] = a["L1_ffn_biases"].reshape(-1)
    for k in ("gamma", "beta"):
        out["f1_" + k] = np.ascontiguousarray(a["L1_ffn_ln_" + k].reshape(NLIN // 2, DC, P).transpose(2, 0, 1))
    return out


STAGES = (attention0, mixture, attention1, feed_forward1)


def program(nc, arrays):
    A = {k: nc.dram_tensor("in_" + k, v.shape, U8 if v.dtype == bool else mybir.dt.from_np(v.dtype),
                              kind="ExternalInput").ap()
         for k, v in arrays.items()}
    A["out"] = nc.dram_tensor("out", [B, S, D], F32, kind="ExternalOutput").ap()
    for name in ("x_slots", "y_slots"):
        A[name] = nc.dram_tensor(name, [TILES * CT, D], F32, kind="Internal").ap()
    build(nc, A, STAGES)


def kernel(**inputs):
    import concourse.bacc as bacc
    from concourse.bass_utils import run_bass_kernel_spmd

    arrays = lay_out(inputs)
    nc = bacc.Bacc("TRN2", target_bir_lowering=False, num_devices=1)
    program(nc, arrays)
    result = run_bass_kernel_spmd(nc, [{"in_" + k: v for k, v in arrays.items()}], core_ids=[0])
    return result.results[0]["out"]
```

```python
from contextlib import ExitStack

import concourse.bass as bass
from concourse import mybir

F32 = mybir.dt.float32
F32R = mybir.dt.float32r
BF16 = mybir.dt.bfloat16
I32 = mybir.dt.int32
U32 = mybir.dt.uint32
U8 = mybir.dt.uint8
ALU = mybir.AluOpType
ACT = mybir.ActivationFunctionType
AX = mybir.AxisListType.X

P = 128
B, S, D = 4, 512, 256
NT = S // P
DC = D // P
N_TILES = B * NT
EPS = 1e-5

H0, DH0 = 16, 16
SLOT = 32
G0 = P // SLOT
NG0 = H0 // G0
ROWS0 = 3 * DH0 + 1
MASKED = 2.0 ** 120


H1, DK = 16, 64
MEM = P
PAIRS = H1 // 2
KT1 = NT + 1

NLIN, LR, GROUP = 6, 32, 16

E, FF = 8, 1024
FC = FF // P
CT = 256
TT = CT // P
TILES = B * S // CT + E - 1
RING = 3
assert TILES % RING == 0


class Count:

    def __init__(self, sem, per, before=0):
        self.sem, self.per, self.before = sem, per, before

    def at(self, b, n):
        assert isinstance(b, int) or self.before + n > 0
        return b * self.per + (self.before + n)

    def wait(self, eng, b, n):
        at = self.at(b, n)
        if not isinstance(at, int) or at > 0:
            eng.wait_ge(self.sem, at)

    def wait_apart(self, eng, b, n, met, at):
        value = self.at(b, n)
        if not isinstance(value, int):
            value = eng.to_reg(value)
        eng.wait_ge(met, at)
        eng.wait_ge(self.sem, value)


def attention0(nc, x_all, A, held):
    with ExitStack() as ctx:
        def sb(name, shape, dt=F32):
            return ctx.enter_context(nc.sbuf_tensor("a0_" + name, shape, dt))

        def ps(name, shape, dt=F32):
            return ctx.enter_context(nc.psum_tensor("a0_" + name, shape, dt))

        def sem(name):
            return ctx.enter_context(nc.semaphore("a0_" + name))

        HALF = H0 // 2 * SLOT
        wq, wk = sb("wq", [P, DC, D]), sb("wk", [P, DC, D])
        wv = sb("wv", [P, DC, H0 * SLOT])
        wo = sb("wo", [P, NG0, D])
        bv = sb("bv", [P, H0 * SLOT])
        bo = sb("bo", [P, D])
        bqk = sb("bqk", [P, 2, 2])
        ident = sb("ident", [P, P])
        ident_b = sb("ident_b", [P, P], BF16)
        spread = sb("spread", [P, P])
        mask_in = sb("mask_in", [P, 2, NT, S], U8)
        bias_q = sb("bias_q", [P, NT, S], BF16)
        bias_k = sb("bias_k", [P, NT, S], BF16)
        least_masked = sb("least_masked", [P, NT])
        nan_row = sb("nan_row", [P, NT])
        ctx_t = sb("ctx_t", [P, DC, S])
        xn = sb("xn", [P, NT, D])
        xn_t = sb("xn_t", [P, DC, S])
        stats = sb("stats", [P, NT, 6])
        mean_var = sb("mean_var", [P, NT, 2])
        rstd = sb("rstd", [P, NT])
        minus_half = sb("minus_half", [P, NT])
        full = sb("full", [P, 2, S])
        hi = sb("hi", [P, 2, S], F32R)
        lo = sb("lo", [P, 2, S], F32R)
        q_stack = sb("q_stack", [ROWS0, H0, S], F32R)
        k_stack = sb("k_stack", [ROWS0, H0, S], F32R)
        v = sb("v", [P, 2, NT, HALF])
        probs = sb("probs", [P, 4, 2, S])
        scratch = sb("scratch", [P, 2, S], BF16)
        mx = sb("mx", [P, G0 * NT])
        neg_max = sb("neg_max", [G0 * NT, P], F32R)
        recip = sb("recip", [P, S])
        o_norm = sb("o_norm", [P, NG0, S])

        p_s = ps("p_s", [P, 2, 2, S])
        p_m = ps("p_m", [P, 2, S])
        p_o = ps("p_o", [P, S])

        STEPS = (("query", "score", "score", "times_v", "maximum"),
                 ("key", "maximum", "score", "maximum", "score", "maximum"),
                 ("maximum", "score", "maximum", "score", "times_v", "maximum"),
                 ("maximum", "score", "maximum", "score", "maximum"),
                 ("maximum", "score", "maximum", "score", "times_v", "maximum"),
                 ("maximum", "score", "maximum", "score", "maximum"),
                 ("score", "score", "turn", "times_v", "value"),
                 ("sums", "score", "score", "value", "rows"))
        PARTS = len(STEPS)
        N_MAX = G0 * NT

        def steps(g, j, ahead):
            for what in STEPS[j]:
                if what in ("query", "key") and (g % 2 or g and not ahead):
                    continue
                if what == "value" and g != 0:
                    continue
                if what == "rows" and (g != 1 or not ahead):
                    continue
                if what == "sums" and g == 0:
                    continue
                if what in ("maximum", "turn") and g + 1 >= NG0 and not ahead:
                    continue
                yield what

        FILLS = {"query": 1, "key": 1, "maximum": 1, "turn": 1, "value": 1, "rows": NT, "sums": 1}
        DVE_FILLS = {"maximum": 1, "value": 1, "rows": NT, "sums": 1}

        def fills(kinds, last_g=NG0 - 1):
            return sum(kinds.get(w, 0) for g in range(last_g + 1) for j in range(PARTS) for w in steps(g, j, True))

        BEFORE = NT + 2 + 2 + N_MAX + 1
        DVE_BEFORE = NT + 2 + N_MAX
        AT_END = 2 + 1 + NT
        assert (fills(FILLS) + AT_END) % 2 == 0
        x_in, weights_in, loaded = sem("x_in"), sem("weights_in"), sem("loaded")
        consts, prep = sem("consts"), sem("prep")
        ctx_in = Count(sem("ctx_in"), 16)
        stats_done = Count(sem("stats_done"), 3)
        rstd_ready = Count(sem("rstd_ready"), 1)
        xn_ready = Count(sem("xn_ready"), 1)
        biased = Count(sem("biased"), 1)
        m_full = Count(sem("m_full"), fills(FILLS) + AT_END, BEFORE)
        m_free = Count(sem("m_free"), fills(DVE_FILLS) + AT_END, DVE_BEFORE)
        hi_ready = Count(sem("hi_ready"), 4)
        split_ready = Count(sem("split_ready"), 4)
        stacked = Count(sem("stacked"), 16 * 12)
        mx_ready = Count(sem("mx_ready"), NG0)
        nm_ready = Count(sem("nm_ready"), NG0)
        nm_in = Count(sem("nm_in"), 16 * NG0)
        s_full = Count(sem("s_full"), NG0 * PARTS)
        exp_done = Count(sem("exp_done"), NG0 * PARTS)
        pv_done = Count(sem("pv_done"), NG0 * NT)
        o_read = Count(sem("o_read"), NG0)
        norm_ready = Count(sem("norm_ready"), NG0)
        block = ctx.enter_context(nc.Block())

        class Fill:

            def __init__(self, start=0):
                self.n = start

            def bank(self):
                self.n += 1
                return p_m[:, (BEFORE + self.n - 1) % 2, :]

        @block.sync
        def _(sp):
            def load_x(i):
                sp.dma_start(x_all[:, i * NT:(i + 1) * NT, :],
                             A["x"][i].rearrange("(t p) d -> p t d", p=P)).then_inc(x_in, 16)

            load_x(0)
            for dst, src in ((bqk[:], A["L0_bqk"]), (wq[:], A["L0_wq"]), (wk[:], A["L0_wk"])):
                sp.dma_start(dst, src).then_inc(weights_in, 16)
            sp.dma_start(ctx_t[:], A["ctx_t"][0]).then_inc(ctx_in.sem, 16)
            for dst, src in ((wv[:], A["L0_wv"]), (bv[:], A["L0_bv"].partition_broadcast(P)), (mask_in[:], A["mask"]),
                             (bo[:], A["L0_bo"].partition_broadcast(P)), (wo[:], A["L0_wo"])):
                sp.dma_start(dst, src).then_inc(loaded, 16)
            for i in range(1, B):
                load_x(i)

            def stack(b, half):
                for n in range(2):
                    split_ready.wait(sp, b, 2 * half + n + 1)
                    stack, parts = ((q_stack, (hi, hi, lo)), (k_stack, (hi, lo, hi)))[n]
                    at = 8 * (half % 2)
                    for k, part in enumerate(parts):
                        sp.dma_start(stack[DH0 * k:DH0 * (k + 1), at:at + 8, :].bitcast(F32),
                                     part[:, n, :].bitcast(F32)).then_inc(stacked.sem, 16)

            def bring_maxima(b, g):
                nm_ready.wait(sp, b, g + 1)
                at = G0 * (g % NG0)
                sp.dma_start(q_stack[3 * DH0:ROWS0, at:at + G0, :].bitcast(F32), neg_max[:].bitcast(F32))\
                  .then_inc(nm_in.sem, 16)

            def turn(b, ahead):
                for g in range(NG0):
                    if g % 2 == 0 and (ahead or g == 0):
                        stack(b, g // 2 + 1)
                    if ahead or g + 1 < NG0:
                        bring_maxima(b, g + 1)
                    if g == 0 and ahead:
                        m_full.wait(sp, b, fills(FILLS, 0))
                        sp.dma_start(ctx_t[:], A["ctx_t"][b + 1]).then_inc(ctx_in.sem, 16)

            sp.wait_ge(consts, 3)
            stack(-1, 2)
            bring_maxima(-1, NG0)
            held.load(sp, A)
            with sp.Fori(0, B - 1) as b:
                turn(b, True)
            turn(B - 1, False)

        @block.gpsimd
        def _(pool):
            pool.memset(minus_half[:], -0.5)
            pool.memset(ident[:], 0.0)
            pool.memset(ident_b[:], 0.0)
            pool.memset(spread[:], 1.0).then_inc(consts, 1)
            pool.wait_ge(consts, 1)
            for m in (ident, ident_b):
                pool.affine_select(out=m[:], in_=m[:], compare_op=ALU.not_equal, fill=1.0, base=0,
                                   pattern=[[-1, P]], channel_multiplier=1)
            spread_v = spread[:].rearrange("p (g m) -> p g m", g=G0)
            pool.affine_select(out=spread_v, in_=spread_v, compare_op=ALU.is_equal, fill=0.0, base=-DH0,
                               pattern=[[-SLOT, G0], [0, SLOT]], channel_multiplier=1).then_inc(consts, 1)

            def invert_deviation(b):
                stats_done.wait(pool, b, 3 + 3)
                pool.tensor_tensor(rstd[:], rstd[:], minus_half[:], ALU.pow).then_inc(rstd_ready.sem, 1)

            def bias(b):
                xn_ready.wait(pool, b, 1 + 1)
                xb = x_all[:, bass.ds((b + 1) * NT, NT), :]
                pool.tensor_tensor(xb, xb, bo[:].unsqueeze(1).broadcast_to([P, NT, D]), ALU.add)\
                    .then_inc(biased.sem, 1)

            invert_deviation(-1)
            pool.memset(k_stack[:].bitcast(F32), 1.0).then_inc(consts, 1)
            pool.wait_ge(loaded, 16 * 5)
            bias(-1)
            with pool.Fori(0, B - 1) as b:
                invert_deviation(b)
                bias(b)

        @block.scalar
        def _(act):
            act.wait_ge(weights_in, 16 * 3)
            act.wait_ge(prep, 1)

            def project(b, half, n, m):
                split_ready.wait(act, b, 2 * half + n - 1)
                stacked.wait(act, b, 16 * 6 * half)
                at = half % 2
                for dst in (full, hi):
                    last = act.activation(dst[:, n, :], m, ACT.Identity, bias=bqk[:, n, at:at + 1],
                                          scale=(DH0 ** -0.5, 1.0)[n])
                last.then_inc(hi_ready.sem, 1)

            def exps(b, g, j):
                s_full.wait(act, b, PARTS * g + j + 1)
                if g or j >= 4:
                    pv_done.wait(act, b, NT * g + j // 2 - 1)
                act.activation(probs[:, j % 4, :, :], p_s[:, j % 2, :, :], ACT.Exp).then_inc(exp_done.sem, 1)

            def read_output(b, g):
                pv_done.wait(act, b, NT * (g + 1))
                act.activation(o_norm[:, g, :], p_o[:], ACT.Copy).then_inc(o_read.sem, 1)

            def turn(b, ahead):
                fill = Fill()
                for g in range(NG0):
                    for j in range(PARTS):
                        heads = 0
                        for what in steps(g, j, ahead):
                            if what in ("query", "key"):
                                m = fill.bank()
                                m_full.wait(act, b, fill.n)
                                project(b, g // 2 + 1, ("query", "key").index(what), m)
                            elif what in FILLS:
                                for _ in range(FILLS[what]):
                                    fill.bank()
                            elif what == "score":
                                heads += 1
                                if heads == 2:
                                    exps(b, g, j)
                            elif what == "times_v" and j == 0 and g:
                                read_output(b, g - 1)
                read_output(b, NG0 - 1)
                norm_ready.wait(act, b, NG0)

            fill = Fill(m_full.per - BEFORE + NT)
            for n in range(2):
                m = fill.bank()
                m_full.wait(act, -1, fill.n)
                project(-1, 2, n, m)
            with act.Fori(0, B - 1) as b:
                turn(b, True)
            turn(B - 1, False)

        @block.vector
        def _(dve):
            def begin_norm(b):
                xb = x_all[:, bass.ds((b + 1) * NT, NT), :]
                for t in range(NT):
                    last = dve.bn_stats(stats[:, t, :], xb[:, t, :])
                last.then_inc(stats_done.sem, 1)
                stats_done.wait_apart(dve, b, 3 + 1, x_in, 16)
                for t in range(NT):
                    last = dve.bn_aggr(mean_var[:, t, :], stats[:, t, :])
                last.then_inc(stats_done.sem, 1)
                stats_done.wait(dve, b, 3 + 2)
                dve.tensor_scalar(rstd[:], mean_var[:, :, 1], EPS, None, ALU.add).then_inc(stats_done.sem, 1)

            def end_norm(b):
                xb = x_all[:, bass.ds((b + 1) * NT, NT), :]
                rstd_ready.wait(dve, b, 1 + 1)
                for t in range(NT):
                    last = dve.tensor_scalar(xn[:, t, :], xb[:, t, :], mean_var[:, t, 0:1], rstd[:, t:t + 1],
                                             ALU.subtract, ALU.mult)
                last.then_inc(xn_ready.sem, 1)

            def turned_rows(b, fill):
                for t in range(NT):
                    m = fill.bank()
                    m_full.wait(dve, b, fill.n)
                    dve.tensor_copy(xn_t[:, :, P * t:P * (t + 1)],
                                    m[:, 0:D].rearrange("p (c n) -> p c n", c=DC)).then_inc(m_free.sem, 1)

            def values(b, fill, half, i):
                m = fill.bank()
                m_full.wait(dve, b, fill.n)
                cols = bv[:, HALF * (half % 2):HALF * (half % 2 + 1)]
                dve.tensor_tensor(v[:, half % 2, 2 * i:2 * i + 2, :], m.rearrange("p (t d) -> p t d", t=2),
                                  cols.unsqueeze(1).broadcast_to([P, 2, HALF]), ALU.add).then_inc(m_free.sem, 1)

            def split(b, half, n):
                hi_ready.wait(dve, b, 2 * half + n + 1)
                if n == 0:
                    stacked.wait(dve, b, 16 * 6 * half)
                dve.tensor_tensor(lo[:, n, :], full[:, n, :], hi[:, n, :].bitcast(F32),
                                  ALU.subtract).then_inc(split_ready.sem, 1)

            def maximum(b, fill, i):
                m = fill.bank()
                m_full.wait_apart(dve, b, fill.n, prep, 5)
                dve.tensor_tensor_reduce(scratch[:, fill.n % 2, :], m, bias_q[:, i % NT, :], 1.0, -3.0e38, ALU.add,
                                         ALU.max, mx[:, i:i + 1]).then_inc(m_free.sem, 1)

            def turn_maxima(b, fill, g):
                m = fill.bank()
                m_full.wait(dve, b, fill.n)
                nm_in.wait(dve, b, 16 * g)
                dve.tensor_scalar(neg_max[:], m[0:N_MAX, 0:P], -1.0, None, ALU.mult).then_inc(nm_ready.sem, 1)

            def normalize(b, fill, freed, g):
                m = fill.bank()
                if g:
                    norm_ready.wait(dve, b, g)
                m_full.wait(dve, b, fill.n)
                dve.reciprocal(recip[:], m).then_inc(m_free.sem, 1)
                m_free.wait(dve, b, freed)
                dve.tensor_tensor(o_norm[:, g, :], o_norm[:, g, :], recip[:], ALU.mult).then_inc(norm_ready.sem, 1)

            def turn(b, ahead):
                fill = Fill()
                freed = 0
                for g in range(NG0):
                    i = 0
                    for j in range(PARTS):
                        for what in steps(g, j, ahead):
                            freed += DVE_FILLS.get(what, 0)
                            if what == "maximum":
                                maximum(b, fill, i)
                                i += 1
                            elif what == "turn":
                                turn_maxima(b, fill, g + 1)
                            elif what == "value":
                                values(b, fill, g // 2 + 1, j - 6)
                            elif what == "rows":
                                turned_rows(b, fill)
                            elif what == "sums":
                                normalize(b, fill, freed, g - 1)
                            elif what in FILLS:
                                fill.bank()
                        if j in (1, 2) and g % 2 == 0 and (ahead or g == 0):
                            split(b, g // 2 + 1, j - 1)
                        if ahead and g == 1 and j == 2:
                            end_norm(b)
                    if ahead and g == 0:
                        begin_norm(b)
                if ahead:
                    values(b, fill, 2, 0)
                    freed += 1
                normalize(b, fill, freed + 1, NG0 - 1)
                if ahead:
                    values(b, fill, 2, 1)
                xb = x_all[:, bass.ds(b * NT, NT), :]
                biased.wait(dve, b, 1)
                for t in range(NT):
                    m = fill.bank()
                    m_full.wait(dve, b, fill.n)
                    dve.scalar_tensor_tensor(out=xb[:, t, :], in0=m[:, 0:D], scalar=nan_row[:, t:t + 1],
                                             in1=xb[:, t, :], op0=ALU.add, op1=ALU.add).then_inc(m_free.sem, 1)

            dve.wait_ge(weights_in, 16 * 3)
            dve.tensor_scalar(bqk[:, 0, :], bqk[:, 0, :], DH0 ** -0.5, None, ALU.mult).then_inc(prep, 1)
            dve.wait_ge(x_in, 16)
            fill = Fill(m_full.per - BEFORE)
            begin_norm(-1)
            end_norm(-1)
            turned_rows(-1, fill)
            for n in range(2):
                fill.bank()
                split(-1, 2, n)
            dve.wait_ge(loaded, 16 * 5)
            dve.tensor_scalar(bias_q[:], mask_in[:, 0, :, :], -MASKED, None, ALU.mult).then_inc(prep, 1)
            for i in range(2):
                values(-1, fill, 2, i)
            dve.tensor_scalar(bias_k[:], mask_in[:, 1, :, :], -MASKED, None, ALU.mult)
            dve.wait_ge(prep, 2)
            dve.tensor_reduce(least_masked[:], bias_q[:], AX, ALU.max).then_inc(prep, 1)
            dve.wait_ge(prep, 3)
            dve.tensor_scalar(nan_row[:], least_masked[:], MASKED, MASKED, ALU.mult, ALU.mult).then_inc(prep, 1)
            dve.wait_ge(prep, 4)
            dve.tensor_tensor(nan_row[:], nan_row[:], nan_row[:], ALU.subtract).then_inc(prep, 1)
            dve.wait_ge(prep, 5)
            for i in range(N_MAX):
                maximum(-1, fill, i)
            turn_maxima(-1, fill, NG0)
            dve.wait_ge(x_in, 16 * B)
            with dve.Fori(0, B - 1) as b:
                turn(b, True)
            turn(B - 1, False)

        @block.tensor
        def _(pe):
            class Banks(Fill):

                def __init__(self, b, start=0, freed=0):
                    super().__init__(start)
                    self.b, self.freed, self.readers = b, freed, []

                def free(self, count=m_free, n=None):
                    if len(self.readers) >= 2:
                        before, at = self.readers[-2]
                        before.wait(pe, self.b, at)
                    if n is None:
                        self.freed += 1
                        n = self.freed
                    self.readers.append((count, n))
                    return self.bank()

            def done(mm):
                mm.then_inc(m_full.sem, 1)

            def turn_rows(b, banks):
                xn_ready.wait(pe, b, 1 + 1)
                for t in range(NT):
                    m = banks.free()
                    for c in range(DC):
                        mm = pe.transpose(m[:, c * P:(c + 1) * P], xn[:, t, c * P:(c + 1) * P], ident[:])
                    done(mm)

            def project(b, banks, half, n):
                m = banks.free(hi_ready, 2 * half + n + 1)
                if half == 2:
                    if n == 0:
                        m_free.wait(pe, b, banks.freed)
                    else:
                        ctx_in.wait(pe, b, 16 + 16)
                w, src = ((wq, xn_t), (wk, ctx_t))[n]
                at = P * (half % 2)
                for c in range(DC):
                    mm = pe.matmul(m, w[:, c, at:at + P], src[:, c, :], start=(c == 0), stop=(c == DC - 1))
                done(mm)

            def values(b, banks, half, i):
                m = banks.free()
                at = HALF * (half % 2)
                for k in range(2):
                    t = 2 * i + k
                    for c in range(DC):
                        mm = pe.matmul(m[:, HALF * k:HALF * (k + 1)], ctx_t[:, c, P * t:P * (t + 1)],
                                       wv[:, c, at:at + HALF], start=(c == 0), stop=(c == DC - 1))
                done(mm)

            def maximum(b, banks, g, i):
                h, t = G0 * (g % NG0) + i // NT, i % NT
                m = banks.free()
                if g % 2 == 0 and i == 0:
                    stacked.wait(pe, b, 16 * 6 * (g // 2 + 1))
                done(pe.matmul(m, q_stack[0:3 * DH0, h, P * t:P * (t + 1)], k_stack[0:3 * DH0, h, :],
                               start=True, stop=True))

            def turn_maxima(b, banks, g):
                m = banks.free(nm_ready, g + 1)
                m_free.wait(pe, b, banks.freed)
                done(pe.transpose(m[0:N_MAX, 0:P], mx[:], ident[:]))

            def spread_sums(b, banks, g):
                m = banks.free()
                o_read.wait(pe, b, g + 1)
                done(pe.matmul(m, spread[:], o_norm[:, g, :], start=True, stop=True))

            def score(b, g, j, i):
                kt, slot = j // 2, j % 2
                n = PARTS * g + j
                if j == 0 and i == 0:
                    nm_in.wait(pe, b, 16 * (g + 1))
                if n >= 2 and i == 0:
                    exp_done.wait(pe, b, n - 1)
                h = G0 * g + 2 * slot + i
                pe.matmul(p_s[:, slot, i, :], k_stack[:, h, P * kt:P * (kt + 1)], q_stack[:, h, :],
                          start=True, stop=False)
                mm = pe.matmul(p_s[:, slot, i, :], ident_b[:], bias_k[:, kt, :], start=False, stop=True)
                if i == 1:
                    mm.then_inc(s_full.sem, 1)

            def times_v(b, g, kt):
                exp_done.wait(pe, b, PARTS * g + 2 * kt + 2)
                if kt == 0 and g:
                    o_read.wait(pe, b, g)
                for i in range(G0):
                    h = G0 * (g % 2) + i
                    mm = pe.matmul(p_o[SLOT * i:SLOT * (i + 1), :], v[:, g // 2, kt, SLOT * h:SLOT * (h + 1)],
                                   probs[:, (2 * kt + i // 2) % 4, i % 2, :], start=(kt == 0), stop=(kt == NT - 1))
                mm.then_inc(pv_done.sem, 1)

            def turn(b, ahead):
                m_free.wait(pe, b, 0)
                nm_ready.wait(pe, b, 1)
                banks = Banks(b)
                for g in range(NG0):
                    i = 0
                    for j in range(PARTS):
                        head = 0
                        for what in steps(g, j, ahead):
                            if what in ("query", "key"):
                                project(b, banks, g // 2 + 1, ("query", "key").index(what))
                            elif what == "maximum":
                                maximum(b, banks, g + 1, i)
                                i += 1
                            elif what == "turn":
                                turn_maxima(b, banks, g + 1)
                            elif what == "score":
                                score(b, g, j, head)
                                head += 1
                            elif what == "times_v" and j:
                                times_v(b, g, j // 2 - 1)
                            elif what == "times_v" and g:
                                times_v(b, g - 1, NT - 1)
                            elif what == "value":
                                values(b, banks, g // 2 + 1, j - 6)
                            elif what == "sums":
                                spread_sums(b, banks, g - 1)
                            elif what == "rows":
                                turn_rows(b, banks)
                times_v(b, NG0 - 1, NT - 1)
                if ahead:
                    values(b, banks, 2, 0)
                spread_sums(b, banks, NG0 - 1)
                if ahead:
                    values(b, banks, 2, 1)
                for t in range(NT):
                    m = banks.free()
                    if t == 0:
                        norm_ready.wait(pe, b, NG0)
                    for g in range(NG0):
                        mm = pe.matmul(m[:, 0:D], o_norm[:, g, P * t:P * (t + 1)], wo[:, g, :],
                                       start=(g == 0), stop=(g == NG0 - 1))
                    done(mm)
                assert not ahead or (banks.n == m_full.per and banks.freed == m_free.per)

            pe.wait_ge(weights_in, 16 * 3)
            pe.wait_ge(consts, 2)
            banks = Banks(-1, m_full.per - BEFORE, m_free.per - DVE_BEFORE)
            turn_rows(-1, banks)
            for n in range(2):
                project(-1, banks, 2, n)
            pe.wait_ge(loaded, 16 * 5)
            pe.wait_ge(consts, 3)
            for i in range(2):
                values(-1, banks, 2, i)
            for i in range(N_MAX):
                maximum(-1, banks, NG0, i)
            turn_maxima(-1, banks, NG0)
            with pe.Fori(0, B - 1) as b:
                turn(b, True)
            turn(B - 1, False)


def route(nc, x_all, xn_all, slot, gate, owner, A):
    with ExitStack() as ctx:
        def sb(name, shape, dt=F32):
            return ctx.enter_context(nc.sbuf_tensor("r_" + name, shape, dt))

        def ps(name, shape, dt=F32):
            return ctx.enter_context(nc.psum_tensor("r_" + name, shape, dt))

        def sem(name):
            return ctx.enter_context(nc.semaphore("r_" + name))

        wr = sb("wr", [P, DC, E])
        br = sb("br", [P, E])
        zeros = sb("zeros", [P, 6 * D])
        ident = sb("ident", [P, P])
        before = sb("before", [P, P])
        ones = sb("ones", [P, P])
        expert_id = sb("expert_id", [P, N_TILES, E])
        steps_of = sb("steps_of", [P, E, B * S // CT])
        tile_id = sb("tile_id", [P, TILES, E])
        xn = sb("xn", [P, NT, D])
        xn_t = sb("xn_t", [P, DC, S])
        stats = sb("stats", [P, NT, 6])
        mean_var = sb("mean_var", [P, NT, 2])
        rstd = sb("rstd", [P, NT])
        minus_half = sb("minus_half", [P, NT])
        logits = sb("logits", [P, N_TILES, E])
        top = sb("top", [P, N_TILES])
        shifted = sb("shifted", [P, N_TILES, E])
        exps = sb("exps", [P, N_TILES, E])
        total = sb("total", [P, N_TILES])
        chosen = sb("chosen", [P, N_TILES])
        one_hot = sb("one_hot", [P, N_TILES, E])
        prior = sb("prior", [P, N_TILES, E])
        count = sb("count", [P, E])
        over = sb("over", [P, E, B * S // CT])
        tiles = sb("tiles", [P, E])
        start = sb("start", [P, E])
        end = sb("end", [P, E])
        past = sb("past", [P, TILES, E])
        slot_f = sb("slot_f", [P, N_TILES])
        owner_f = sb("owner_f", [P, TILES])

        p_t = ps("p_t", [P, 2, S])
        p_l = ps("p_l", [P, NT, E])
        p_rank = ps("p_rank", [P, N_TILES * E])
        p_sum = ps("p_sum", [P, N_TILES * E])

        consts, filled = sem("consts"), sem("filled")
        loaded, cleared = sem("loaded"), sem("cleared")
        stats_done = Count(sem("stats_done"), 3)
        rstd_ready = Count(sem("rstd_ready"), 1)
        xn_ready = Count(sem("xn_ready"), 1)
        kept = Count(sem("kept"), 1)
        turned = Count(sem("turned"), NT)
        copied = Count(sem("copied"), NT)
        l_full = Count(sem("l_full"), 1)
        l_read = Count(sem("l_read"), 1)
        shifted_ready, exps_ready, hot_ready = sem("shifted_ready"), sem("exps_ready"), sem("hot_ready")
        ranked, step_done, slots_ready, scattered = sem("ranked"), sem("step_done"), sem("slots_ready"), sem("scattered")
        block = ctx.enter_context(nc.Block())

        @block.sync
        def _(sp):
            sp.dma_start(wr[:], A["L0_wr"]).then_inc(loaded, 16)
            sp.dma_start(br[:], A["L0_br"].partition_broadcast(P)).then_inc(loaded, 16)
            sp.wait_ge(filled, 1)
            rows = TILES * CT // 5
            for i in range(5):
                sp.dma_start(A["x_slots"][i * rows:(i + 1) * rows, :].rearrange("(p r) d -> p (r d)", p=P),
                             zeros[:]).then_inc(cleared, 16)

        @block.gpsimd
        def _(pool):
            pool.memset(zeros[:], 0.0).then_inc(filled, 1)
            pool.memset(ident[:], 0.0)
            pool.memset(before[:], 1.0)
            pool.memset(ones[:], 1.0)
            pool.memset(minus_half[:], -0.5)
            pool.iota(expert_id[:], pattern=[[0, N_TILES], [1, E]], base=-E, channel_multiplier=0,
                      allow_small_or_imprecise_dtypes=True)
            pool.iota(steps_of[:], pattern=[[0, E], [CT, B * S // CT]], base=0, channel_multiplier=0,
                      allow_small_or_imprecise_dtypes=True)
            pool.iota(tile_id[:], pattern=[[1, TILES], [0, E]], base=0, channel_multiplier=0,
                      allow_small_or_imprecise_dtypes=True).then_inc(filled, 1)
            pool.wait_ge(filled, 2)
            pool.affine_select(out=ident[:], in_=ident[:], compare_op=ALU.not_equal, fill=1.0, base=0,
                               pattern=[[-1, P]], channel_multiplier=1)
            pool.affine_select(out=before[:], in_=before[:], compare_op=ALU.is_gt, fill=0.0, base=0,
                               pattern=[[1, P]], channel_multiplier=-1).then_inc(consts, 1)
            with pool.Fori(0, B) as b:
                stats_done.wait(pool, b, 3)
                pool.tensor_tensor(rstd[:], rstd[:], minus_half[:], ALU.pow).then_inc(rstd_ready.sem, 1)
                xn_ready.wait(pool, b, 1)
                pool.tensor_copy(xn_all[:, bass.ds(b * NT, NT), :], xn[:]).then_inc(kept.sem, 1)
            pool.wait_ge(kept.sem, B)
            pool.wait_ge(cleared, 16 * 5)
            pool.wait_ge(slots_ready, 1)
            for t in range(N_TILES):
                pool.indirect_dma_start(out=A["x_slots"], out_offset=bass.IndirectOffsetOnAxis(ap=slot[:, t:t + 1], axis=0),
                                        in_=xn_all[:, t, :], in_offset=None).then_inc(scattered, 16)
            pool.wait_ge(scattered, 16 * N_TILES)

        @block.scalar
        def _(act):
            act.wait_ge(shifted_ready, 1)
            act.activation(exps[:], shifted[:], ACT.Exp).then_inc(exps_ready, 1)

        @block.vector
        def _(dve):
            dve.wait_ge(loaded, 32)
            with dve.Fori(0, B) as b:
                xb = x_all[:, bass.ds(b * NT, NT), :]
                for t in range(NT):
                    last = dve.bn_stats(stats[:, t, :], xb[:, t, :])
                last.then_inc(stats_done.sem, 1)
                stats_done.wait_apart(dve, b, 1, loaded, 32)
                for t in range(NT):
                    last = dve.bn_aggr(mean_var[:, t, :], stats[:, t, :])
                last.then_inc(stats_done.sem, 1)
                stats_done.wait(dve, b, 2)
                dve.tensor_scalar(rstd[:], mean_var[:, :, 1], EPS, None, ALU.add).then_inc(stats_done.sem, 1)
                rstd_ready.wait(dve, b, 1)
                for t in range(NT):
                    last = dve.tensor_scalar(xn[:, t, :], xb[:, t, :], mean_var[:, t, 0:1], rstd[:, t:t + 1],
                                             ALU.subtract, ALU.mult)
                last.then_inc(xn_ready.sem, 1)
                for t in range(NT):
                    turned.wait(dve, b, t + 1)
                    dve.tensor_copy(xn_t[:, :, P * t:P * (t + 1)],
                                    p_t[:, t % 2, 0:D].rearrange("p (c n) -> p c n", c=DC)).then_inc(copied.sem, 1)
                l_full.wait(dve, b, 1)
                dve.tensor_tensor(logits[:, bass.ds(b * NT, NT), :], p_l[:],
                                  br[:].unsqueeze(1).broadcast_to([P, NT, E]), ALU.add).then_inc(l_read.sem, 1)
                kept.wait(dve, b, 1)
            dve.wait_ge(l_read.sem, B)
            dve.wait_ge(consts, 1)
            n = [0]

            def step(ins):
                n[0] += 1
                ins.then_inc(step_done, 1)
                dve.wait_ge(step_done, n[0])

            def over_tiles(v):
                return v.unsqueeze(2).broadcast_to([P, N_TILES, E])

            step(dve.tensor_reduce(top[:], logits[:], AX, ALU.max))
            dve.tensor_tensor(shifted[:], logits[:], over_tiles(top[:]), ALU.subtract).then_inc(shifted_ready, 1)
            step(dve.tensor_tensor(one_hot[:], logits[:], over_tiles(top[:]), ALU.is_ge))
            step(dve.tensor_tensor(one_hot[:], one_hot[:], expert_id[:], ALU.mult))
            step(dve.tensor_reduce(chosen[:], one_hot[:], AX, ALU.min))
            step(dve.tensor_scalar(chosen[:], chosen[:], -1.0, None, ALU.min))
            dve.tensor_tensor(one_hot[:], expert_id[:], over_tiles(chosen[:]), ALU.is_equal).then_inc(hot_ready, 1)
            dve.wait_ge(exps_ready, 1)
            step(dve.tensor_reduce(total[:], exps[:], AX, ALU.add))
            dve.reciprocal(gate[:], total[:])
            dve.wait_ge(ranked, 1)
            p_sum_v = p_sum[:].rearrange("p (t e) -> p t e", e=E)
            step(dve.memset(prior[:, 0, :], 0.0))
            for t in range(1, N_TILES):
                step(dve.tensor_tensor(prior[:, t, :], p_sum_v[:, t - 1, :], prior[:, t - 1, :], ALU.add))
            step(dve.tensor_tensor(count[:], p_sum_v[:, N_TILES - 1, :], prior[:, N_TILES - 1, :], ALU.add))
            step(dve.tensor_tensor(over[:], count[:].unsqueeze(2).broadcast_to([P, E, B * S // CT]), steps_of[:],
                                   ALU.is_gt))
            step(dve.tensor_reduce(tiles[:], over[:], AX, ALU.add))
            step(dve.memset(start[:, 0:1], 0.0))
            for e in range(1, E):
                step(dve.tensor_tensor(start[:, e:e + 1], start[:, e - 1:e], tiles[:, e - 1:e], ALU.add))
            step(dve.tensor_tensor(end[:], start[:], tiles[:], ALU.add))
            step(dve.tensor_tensor(past[:], tile_id[:], end[:].unsqueeze(1).broadcast_to([P, TILES, E]), ALU.is_ge))
            step(dve.tensor_reduce(owner_f[:], past[:], AX, ALU.add))
            dve.tensor_scalar(owner[:], owner_f[:], float(E - 1), None, ALU.min)
            step(dve.tensor_scalar(start[:], start[:], float(CT), None, ALU.mult))
            step(dve.tensor_tensor(prior[:], prior[:], start[:].unsqueeze(1).broadcast_to([P, N_TILES, E]), ALU.add))
            step(dve.tensor_tensor(prior[:], p_rank[:].rearrange("p (t e) -> p t e", e=E), prior[:], ALU.add))
            step(dve.tensor_tensor(prior[:], prior[:], one_hot[:], ALU.mult))
            step(dve.tensor_reduce(slot_f[:], prior[:], AX, ALU.add))
            dve.tensor_copy(slot[:], slot_f[:]).then_inc(slots_ready, 1)

        @block.tensor
        def _(pe):
            pe.wait_ge(loaded, 32)
            pe.wait_ge(consts, 1)
            with pe.Fori(0, B) as b:
                xn_ready.wait(pe, b, 1)
                for t in range(NT):
                    if t >= 2:
                        copied.wait(pe, b, t - 1)
                    for c in range(DC):
                        mm = pe.transpose(p_t[:, t % 2, c * P:(c + 1) * P], xn[:, t, c * P:(c + 1) * P], ident[:])
                    mm.then_inc(turned.sem, 1)
                copied.wait(pe, b, NT)
                for t in range(NT):
                    for c in range(DC):
                        mm = pe.matmul(p_l[:, t, :], xn_t[:, c, P * t:P * (t + 1)], wr[:, c, :],
                                       start=(c == 0), stop=(c == DC - 1))
                mm.then_inc(l_full.sem, 1)
                l_read.wait(pe, b, 1)
            pe.wait_ge(hot_ready, 1)
            hot = one_hot[:].rearrange("p t e -> p (t e)")
            pe.matmul(p_rank[:], before[:], hot, start=True, stop=True)
            pe.matmul(p_sum[:], ones[:], hot, start=True, stop=True).then_inc(ranked, 1)


def experts(nc, x_all, slot, gate, owner, A):
    with ExitStack() as ctx:
        def sb(name, shape, dt=F32):
            return ctx.enter_context(nc.sbuf_tensor("e_" + name, shape, dt))

        def ps(name, shape, dt=F32):
            return ctx.enter_context(nc.psum_tensor("e_" + name, shape, dt))

        def sem(name):
            return ctx.enter_context(nc.semaphore("e_" + name))

        ident = sb("ident", [P, P])
        rows = sb("rows", [P, RING, TT, D])
        w1 = sb("w1", [P, RING, DC, FF])
        w2 = sb("w2", [P, RING, FC, D])
        b1 = sb("b1", [P, RING, FC])
        b2 = sb("b2", [P, RING, D])
        rows_t = sb("rows_t", [P, 2, DC, CT])
        hidden = sb("hidden", [P, 4, CT])
        y = sb("y", [P, RING, TT, D])
        back = sb("back", [P, N_TILES, D])

        p_t = ps("p_t", [P, DC, CT])
        p_h = ps("p_h", [P, 4, S])
        p_y = ps("p_y", [P, TT, S])

        cleared, consts = sem("cleared"), sem("consts")
        rows_in = [Count(sem(f"rows_in{r}"), 16) for r in range(RING)]
        w_in = [Count(sem(f"w_in{r}"), 64) for r in range(RING)]
        turned = Count(sem("turned"), RING)
        rows_t_ready = Count(sem("rows_t_ready"), RING)
        h_full = Count(sem("h_full"), RING * FC)
        h_ready = Count(sem("h_ready"), RING * FC)
        h_used = Count(sem("h_used"), RING * FC)
        y_ready = Count(sem("y_ready"), RING)
        y_stored = Count(sem("y_stored"), 16 * RING)
        gathered, scaled = sem("gathered"), sem("scaled")
        block = ctx.enter_context(nc.Block())
        TURNS = TILES // RING

        @block.sync
        def _(sp):
            def load(i, r):
                e = sp.value_load(owner[0:1, bass.ds(i * RING + r, 1)], min_val=0, max_val=E - 1)
                sp.dma_start(rows[:, r, :, :], A["x_slots"][bass.ds((i * RING + r) * CT, CT), :]
                             .rearrange("(t p) d -> p t d", p=P)).then_inc(rows_in[r].sem, 16)
                sp.dma_start(w1[:, r, :, :], A["L0_w1"][bass.ds(e, 1)].rearrange("o p c f -> p (o c) f"))\
                  .then_inc(w_in[r].sem, 16)
                sp.dma_start(b1[:, r, :], A["L0_b1"][bass.ds(e, 1)].rearrange("o p c -> p (o c)"))\
                  .then_inc(w_in[r].sem, 16)
                sp.dma_start(b2[:, r, :], A["L0_b2"][bass.ds(e, 1)].rearrange("o p d -> p (o d)"))\
                  .then_inc(w_in[r].sem, 16)
                sp.dma_start(w2[:, r, :, :], A["L0_w2"][bass.ds(e, 1)].rearrange("o p c d -> p (o c) d"))\
                  .then_inc(w_in[r].sem, 16)

            for r in range(RING):
                load(0, r)
            with sp.Fori(0, TURNS - 1) as i:
                for r in range(RING):
                    y_ready.wait(sp, i, r + 1)
                    load(i + 1, r)

        @block.gpsimd
        def _(pool):
            pool.memset(ident[:], 0.0).then_inc(cleared, 1)
            pool.wait_ge(cleared, 1)
            pool.affine_select(out=ident[:], in_=ident[:], compare_op=ALU.not_equal, fill=1.0, base=0,
                               pattern=[[-1, P]], channel_multiplier=1).then_inc(consts, 1)
            with pool.Fori(0, TURNS) as i:
                for r in range(RING):
                    y_ready.wait(pool, i, r + 1)
                    pool.dma_start(A["y_slots"][bass.ds((i * RING + r) * CT, CT), :]
                                   .rearrange("(t p) d -> p t d", p=P), y[:, r, :, :]).then_inc(y_stored.sem, 16)
            pool.wait_ge(y_stored.sem, 16 * TILES)
            for t in range(N_TILES):
                pool.indirect_dma_start(out=back[:, t, :], out_offset=None, in_=A["y_slots"],
                                        in_offset=bass.IndirectOffsetOnAxis(ap=slot[:, t:t + 1], axis=0))\
                    .then_inc(gathered, 16)

        @block.scalar
        def _(act):
            with act.Fori(0, TURNS) as i:
                for r in range(RING):
                    for c in range(FC):
                        n = FC * r + c
                        h_full.wait(act, i, n + 1)
                        if c == 0:
                            w_in[r].wait(act, i, 64)
                        if n >= 4:
                            h_used.wait(act, i, n - 3)
                        act.activation(hidden[:, c % 4, :], p_h[:, c % 4, 0:CT], ACT.Gelu, bias=b1[:, r, c:c + 1])\
                           .then_inc(h_ready.sem, 1)
                h_used.wait(act, i, RING * FC)

        @block.vector
        def _(dve):
            with dve.Fori(0, TURNS) as i:
                for r in range(RING):
                    turned.wait(dve, i, r + 1)
                    dve.tensor_copy(rows_t[:, r % 2, :, :], p_t[:]).then_inc(rows_t_ready.sem, 1)
                    h_used.wait(dve, i, FC * (r + 1))
                    if r:
                        y_stored.wait(dve, i, 16 * r)
                    dve.tensor_tensor(y[:, r, :, :], p_y[:, :, 0:D], b2[:, r, :].unsqueeze(1).broadcast_to([P, TT, D]),
                                      ALU.add).then_inc(y_ready.sem, 1)
            dve.wait_ge(gathered, 16 * N_TILES)
            for t in range(N_TILES):
                dve.scalar_tensor_tensor(out=x_all[:, t, :], in0=back[:, t, :], scalar=gate[:, t:t + 1],
                                         in1=x_all[:, t, :], op0=ALU.mult, op1=ALU.add).then_inc(scaled, 1)
            dve.wait_ge(scaled, N_TILES)

        @block.tensor
        def _(pe):
            pe.wait_ge(consts, 1)
            with pe.Fori(0, TURNS) as i:
                for r in range(RING):
                    rows_in[r].wait(pe, i, 16)
                    for t in range(TT):
                        for c in range(DC):
                            mm = pe.transpose(p_t[:, c, P * t:P * (t + 1)], rows[:, r, t, P * c:P * (c + 1)], ident[:])
                    mm.then_inc(turned.sem, 1)
                    w_in[r].wait(pe, i, 64)
                    rows_t_ready.wait(pe, i, r + 1)
                    for c in range(FC + 2):
                        if c < FC:
                            n = FC * r + c
                            if n >= 4:
                                h_ready.wait(pe, i, n - 3)
                            for k in range(DC):
                                mm = pe.matmul(p_h[:, c % 4, 0:CT], w1[:, r, k, P * c:P * (c + 1)],
                                               rows_t[:, r % 2, k, :], start=(k == 0), stop=(k == DC - 1))
                            mm.then_inc(h_full.sem, 1)
                        if c >= 2:
                            d = c - 2
                            h_ready.wait(pe, i, FC * r + d + 1)
                            if d == 0 and r:
                                y_ready.wait(pe, i, r)
                            for t in range(TT):
                                mm = pe.matmul(p_y[:, t, 0:D], hidden[:, d % 4, P * t:P * (t + 1)], w2[:, r, d, :],
                                               start=(d == 0), stop=(d == FC - 1))
                            mm.then_inc(h_used.sem, 1)
                y_ready.wait(pe, i, RING)


def mixture(nc, x_all, A, held):
    with nc.sbuf_tensor("slot", [P, N_TILES], U32) as slot, nc.sbuf_tensor("gate", [P, N_TILES], F32) as gate, \
         nc.sbuf_tensor("owner", [P, TILES], I32) as owner:
        with nc.sbuf_tensor("xn_all", [P, N_TILES, D], F32) as xn_all:
            route(nc, x_all, xn_all, slot, gate, owner, A)
        experts(nc, x_all, slot, gate, owner, A)


class Attention1Weights:

    HD = H1 * DK
    LOADS = 16 * 7

    def __init__(self, nc, ctx):
        def sb(name, shape):
            return ctx.enter_context(nc.sbuf_tensor("a1_" + name, shape, F32))

        self.wq, self.wk, self.wv = (sb(name, [P, DC, self.HD]) for name in ("wq", "wk", "wv"))
        self.wo = sb("wo", [P, PAIRS, D])
        self.bv = sb("bv", [P, self.HD])
        self.bo = sb("bo", [P, D])
        self.bqk = sb("bqk", [P, 2, PAIRS])
        self.loaded = ctx.enter_context(nc.semaphore("a1_weights_in"))

    def load(self, sp, A):
        for dst, src in ((self.bqk[:], A["L1_bqk"]), (self.wq[:], A["L1_wq"]), (self.wk[:], A["L1_wk"]),
                         (self.wv[:], A["L1_wv"]), (self.wo[:], A["L1_wo"]),
                         (self.bv[:], A["L1_bv"].partition_broadcast(P)),
                         (self.bo[:], A["L1_bo"].partition_broadcast(P))):
            sp.dma_start(dst, src).then_inc(self.loaded, 16)


def attention1(nc, x_all, A, held):
    with ExitStack() as ctx:
        def sb(name, shape, dt=F32):
            return ctx.enter_context(nc.sbuf_tensor("a1_" + name, shape, dt))

        def ps(name, shape, dt=F32):
            return ctx.enter_context(nc.psum_tensor("a1_" + name, shape, dt))

        def sem(name):
            return ctx.enter_context(nc.semaphore("a1_" + name))

        HD = H1 * DK
        ROWS = DK + 1
        HELD = 4
        assert PAIRS % HELD == 0
        wq, wk, wv, wo, bv, bo, bqk = held.wq, held.wk, held.wv, held.wo, held.bv, held.bo, held.bqk
        ident = sb("ident", [P, P])
        ones = sb("ones", [P, DK])
        ctx_t = sb("ctx_t", [P, DC, S])
        xn_t = sb("xn_t", [P, DC, S])
        stats = sb("stats", [P, NT, 6])
        mean_var = sb("mean_var", [P, NT, 2])
        rstd = sb("rstd", [P, NT])
        minus_half = sb("minus_half", [P, NT])
        full = sb("full", [P, 2, S])
        hi = sb("hi", [P, 2, S], F32R)
        lo = sb("lo", [P, 2, S], F32R)
        q_hh = sb("q_hh", [P, 2 * HELD, S], F32R)
        k_hl = sb("k_hl", [P, 2 * HELD, S], F32R)
        q_lm = sb("q_lm", [ROWS, 2 * HELD, S], F32R)
        k_h1 = sb("k_h1", [ROWS, 2 * HELD, S], F32R)
        mem_hl = sb("mem_hl", [P, 2, PAIRS, MEM], F32R)
        mem_h1 = sb("mem_h1", [ROWS, 2, PAIRS, MEM], F32R)
        v = sb("v", [P, 2, NT, 2 * P])
        mem_v = sb("mem_v", [P, HD])
        probs = sb("probs", [P, KT1, 2, S])
        max_ctx = sb("max_ctx", [P, 2 * NT])
        max_mem = sb("max_mem", [P, 2 * NT])
        mx = sb("mx", [P, 2 * NT])
        neg_max = sb("neg_max", [2 * NT, P], F32R)
        recip = sb("recip", [P, S])
        o_norm = sb("o_norm", [P, PAIRS, S])
        xn = o_norm[:, PAIRS - 2:PAIRS, :].rearrange("p a (t d) -> p (a t) d", d=D)

        p_s = ps("p_s", [P, 2, 2, S])
        p_m = ps("p_m", [P, 2, S])
        p_o = ps("p_o", [P, S])
        p_sum = ps("p_sum", [P, S])

        STEPS = (("query", "score", "score", "maximum", "times_v", "maximum"),
                 ("key", "maximum", "score", "score", "times_v", "maximum", "maximum"),
                 ("maximum", "score", "maximum", "score", "maximum", "times_v"),
                 ("maximum", "score", "maximum", "score", "times_v", "value"),
                 ("total", "turn", "score", "score", "times_v", "value", "rows"))
        PER_MAX = 2 * (NT + 1)

        def steps(p, kt, ahead):
            for what in STEPS[kt]:
                if what == "value" and (p % 2 == 0 or p == PAIRS - 1):
                    continue
                if what == "rows" and (p != PAIRS - 3 or not ahead):
                    continue
                if not ahead and (what in ("query", "key") and p + 2 >= PAIRS
                                  or what in ("maximum", "turn") and p + 1 >= PAIRS):
                    continue
                yield what

        FILLS = {"query": 1, "key": 1, "maximum": 1, "turn": 1, "value": 1, "rows": NT}
        DVE_FILLS = {"maximum": 1, "value": 1, "rows": NT}

        def fills(kinds, last_p=PAIRS - 1, last=None):
            return sum(kinds.get(w, 0) for p in range(last_p + 1) for kt in range(KT1) for w in steps(p, kt, True))

        BEFORE = NT + 4 + 2 + PER_MAX + 1
        DVE_BEFORE = NT + 2 + PER_MAX
        PER = fills(FILLS) + 2 + NT
        assert PER % 2 == 0
        loaded, filled_s, consts, prep = sem("loaded"), sem("filled"), sem("consts"), sem("prep")
        mem_in = sem("mem_in")
        ctx_in = Count(sem("ctx_in"), 16)
        stats_done = Count(sem("stats_done"), 3)
        rstd_ready = Count(sem("rstd_ready"), 1)
        xn_ready = Count(sem("xn_ready"), 1)
        biased = Count(sem("biased"), 1)
        m_full = Count(sem("m_full"), PER, BEFORE)
        m_free = Count(sem("m_free"), fills(DVE_FILLS) + 2 + NT, DVE_BEFORE)
        hi_ready = Count(sem("hi_ready"), 2 * PAIRS)
        split_ready = Count(sem("split_ready"), 2 * PAIRS)
        stacked = Count(sem("stacked"), 16 * 6 * PAIRS)
        mx_ready = Count(sem("mx_ready"), PAIRS)
        nm_ready = Count(sem("nm_ready"), PAIRS)
        nm_in = Count(sem("nm_in"), 16 * PAIRS)
        s_full = Count(sem("s_full"), KT1 * PAIRS)
        exp_done = Count(sem("exp_done"), KT1 * PAIRS)
        pv_done = Count(sem("pv_done"), KT1 * PAIRS)
        tile_added = Count(sem("tile_added"), NT * PAIRS)
        summed = Count(sem("summed"), PAIRS)
        o_read = Count(sem("o_read"), PAIRS)
        sum_read = Count(sem("sum_read"), PAIRS)
        norm_ready = Count(sem("norm_ready"), PAIRS)
        block = ctx.enter_context(nc.Block())

        class Fill:

            def __init__(self, start=0):
                self.n = start

            def bank(self):
                self.n += 1
                return p_m[:, (BEFORE + self.n - 1) % 2, :]

        @block.sync
        def _(sp):
            for dst, src in ((xn_t[:].rearrange("p c n -> p (c n)"), A["L1_mk"]), (mem_v[:], A["L1_mv"])):
                sp.dma_start(dst, src).then_inc(loaded, 16)
            sp.wait_ge(prep, 3)
            for dst, part in ((mem_hl[0:DK], hi), (mem_hl[DK:P], lo), (mem_h1[0:DK], hi)):
                sp.dma_start(dst.rearrange("p i a n -> p i (a n)").bitcast(F32),
                             part[:].rearrange("p a n -> p (a n)").bitcast(F32)).then_inc(mem_in, 16)

            def stack(b, p):
                for n in range(2):
                    split_ready.wait(sp, b, 2 * p + n + 1)
                    parts = (((q_hh[0:DK], hi), (q_hh[DK:P], hi), (q_lm[0:DK], lo)),
                             ((k_hl[0:DK], hi), (k_hl[DK:P], lo), (k_h1[0:DK], hi)))[n]
                    for dst, part in parts:
                        sp.dma_start(dst[:, 2 * (p % HELD):2 * (p % HELD) + 2, :].bitcast(F32),
                                     part[:, n, :].bitcast(F32)).then_inc(stacked.sem, 16)

            def bring_maxima(b, p):
                nm_ready.wait(sp, b, p + 1)
                s = 2 * (p % HELD)
                sp.dma_start(q_lm[DK:ROWS, s:s + 2, :].bitcast(F32), neg_max[:].bitcast(F32))\
                  .then_inc(nm_in.sem, 16)

            def turn(b, ahead):
                for p in range(PAIRS):
                    if ahead or p + 2 < PAIRS:
                        stack(b, p + 2)
                    if ahead or p + 1 < PAIRS:
                        bring_maxima(b, p + 1)
                    if p == PAIRS - 3 and ahead:
                        m_full.wait(sp, b, fills(FILLS, p))
                        sp.dma_start(ctx_t[:], A["ctx_t"][b + 1]).then_inc(ctx_in.sem, 16)

            sp.dma_start(ctx_t[:], A["ctx_t"][0]).then_inc(ctx_in.sem, 16)
            stack(-1, PAIRS)
            stack(-1, PAIRS + 1)
            bring_maxima(-1, PAIRS)
            with sp.Fori(0, B - 1) as b:
                turn(b, True)
            turn(B - 1, False)

        @block.gpsimd
        def _(pool):
            pool.memset(ident[:], 0.0)
            pool.memset(ones[:], 1.0)
            pool.memset(minus_half[:], -0.5)
            pool.memset(k_h1[:].bitcast(F32), 1.0)
            pool.memset(mem_h1[:].bitcast(F32), 1.0).then_inc(filled_s, 1)
            pool.wait_ge(filled_s, 1)
            pool.affine_select(out=ident[:], in_=ident[:], compare_op=ALU.not_equal, fill=1.0, base=0,
                               pattern=[[-1, P]], channel_multiplier=1).then_inc(consts, 1)
            pool.wait_ge(held.loaded, held.LOADS)

            def invert_deviation(b):
                stats_done.wait(pool, b, 3 + 3)
                pool.tensor_tensor(rstd[:], rstd[:], minus_half[:], ALU.pow).then_inc(rstd_ready.sem, 1)

            def bias(b):
                xn_ready.wait(pool, b, 1 + 1)
                xb = x_all[:, bass.ds((b + 1) * NT, NT), :]
                pool.tensor_tensor(xb, xb, bo[:].unsqueeze(1).broadcast_to([P, NT, D]), ALU.add)\
                    .then_inc(biased.sem, 1)

            def add_tile(b, p, kt):
                if kt > 1:
                    tile_added.wait(pool, b, NT * p + kt - 1)
                pv_done.wait(pool, b, KT1 * p + kt + 1)
                pool.tensor_tensor(probs[:, kt], probs[:, kt - 1], probs[:, kt], ALU.add)\
                    .then_inc(tile_added.sem, 1)

            def turn(b, ahead):
                for p in range(PAIRS):
                    if ahead and p == PAIRS - 4:
                        invert_deviation(b)
                    for kt in range(1, KT1):
                        add_tile(b, p, kt)
                    if ahead and p == PAIRS - 2:
                        bias(b)

            invert_deviation(-1)
            bias(-1)
            with pool.Fori(0, B - 1) as b:
                turn(b, True)
            turn(B - 1, False)

        @block.scalar
        def _(act):
            act.wait_ge(held.loaded, held.LOADS)
            act.wait_ge(mem_in, 16 * 3)

            def project(b, p, n, m):
                split_ready.wait(act, b, 2 * p + n - 1)
                stacked.wait(act, b, 16 * 6 * p)
                for dst in (full, hi):
                    last = act.activation(dst[:, n, :], m, ACT.Identity, bias=bqk[:, n, p % PAIRS:p % PAIRS + 1],
                                          scale=(DK ** -0.5, 1.0)[n])
                last.then_inc(hi_ready.sem, 1)

            def exps(b, p, kt):
                s_full.wait(act, b, KT1 * p + kt + 1)
                if p and kt < NT:
                    tile_added.wait(act, b, NT * (p - 1) + kt + 1)
                elif p:
                    summed.wait(act, b, p)
                act.activation(probs[:, kt, :, :], p_s[:, (KT1 * p + kt) % 2, :, :], ACT.Exp).then_inc(exp_done.sem, 1)

            def read_output(b, p):
                pv_done.wait(act, b, KT1 * (p + 1))
                act.activation(o_norm[:, p, :], p_o[:], ACT.Copy).then_inc(o_read.sem, 1)

            def turn(b, ahead):
                fill = Fill()
                for p in range(PAIRS):
                    for kt in range(KT1):
                        heads = 0
                        for what in steps(p, kt, ahead):
                            if what in ("query", "key"):
                                m = fill.bank()
                                m_full.wait(act, b, fill.n)
                                project(b, p + 2, ("query", "key").index(what), m)
                            elif what in FILLS:
                                for _ in range(FILLS[what]):
                                    fill.bank()
                            elif what == "score":
                                heads += 1
                                if heads == 2:
                                    exps(b, p, kt)
                            elif what == "times_v" and kt == 0 and p:
                                read_output(b, p - 1)
                read_output(b, PAIRS - 1)
                norm_ready.wait(act, b, PAIRS)

            fill = Fill(PER - BEFORE + NT)
            for p in range(2):
                for n in range(2):
                    m = fill.bank()
                    m_full.wait(act, -1, fill.n)
                    project(-1, PAIRS + p, n, m)
            with act.Fori(0, B - 1) as b:
                turn(b, True)
            turn(B - 1, False)

        @block.vector
        def _(dve):
            dve.wait_ge(held.loaded, held.LOADS)
            dve.wait_ge(loaded, 16 * 2)
            dve.wait_ge(consts, 1)
            mem_keys = xn_t[:].rearrange("p c n -> p (c n)")
            flat = lambda t: t[:].rearrange("p c n -> p (c n)")
            dve.tensor_scalar(bqk[:, 0, :], bqk[:, 0, :], DK ** -0.5, None, ALU.mult).then_inc(prep, 1)
            dve.tensor_copy(flat(hi), mem_keys).then_inc(prep, 1)
            dve.wait_ge(prep, 2)
            dve.tensor_tensor(flat(lo), mem_keys, flat(hi).bitcast(F32), ALU.subtract).then_inc(prep, 1)
            dve.wait_ge(mem_in, 16 * 3)

            def begin_norm(b):
                xb = x_all[:, bass.ds((b + 1) * NT, NT), :]
                for t in range(NT):
                    last = dve.bn_stats(stats[:, t, :], xb[:, t, :])
                last.then_inc(stats_done.sem, 1)
                stats_done.wait_apart(dve, b, 3 + 1, prep, 3)
                for t in range(NT):
                    last = dve.bn_aggr(mean_var[:, t, :], stats[:, t, :])
                last.then_inc(stats_done.sem, 1)
                stats_done.wait(dve, b, 3 + 2)
                dve.tensor_scalar(rstd[:], mean_var[:, :, 1], EPS, None, ALU.add).then_inc(stats_done.sem, 1)

            def end_norm(b):
                xb = x_all[:, bass.ds((b + 1) * NT, NT), :]
                rstd_ready.wait(dve, b, 1 + 1)
                for t in range(NT):
                    last = dve.tensor_scalar(xn[:, t, :], xb[:, t, :], mean_var[:, t, 0:1], rstd[:, t:t + 1],
                                             ALU.subtract, ALU.mult)
                last.then_inc(xn_ready.sem, 1)

            def turned_rows(b, fill):
                for t in range(NT):
                    m = fill.bank()
                    m_full.wait(dve, b, fill.n)
                    dve.tensor_copy(xn_t[:, :, P * t:P * (t + 1)],
                                    m[:, 0:D].rearrange("p (c n) -> p c n", c=DC)).then_inc(m_free.sem, 1)

            def values(b, fill, group, half):
                m = fill.bank()
                m_full.wait(dve, b, fill.n)
                cols = bv[:, 2 * P * (group % 4):2 * P * (group % 4 + 1)]
                dve.tensor_tensor(v[:, group % 2, 2 * half:2 * half + 2, :], m.rearrange("p (t d) -> p t d", t=2),
                                  cols.unsqueeze(1).broadcast_to([P, 2, 2 * P]), ALU.add).then_inc(m_free.sem, 1)

            def split(b, p, n):
                hi_ready.wait(dve, b, 2 * p + n + 1)
                if n == 0:
                    stacked.wait(dve, b, 16 * 6 * p)
                dve.tensor_tensor(lo[:, n, :], full[:, n, :], hi[:, n, :].bitcast(F32),
                                  ALU.subtract).then_inc(split_ready.sem, 1)

            def maximum(b, fill, i):
                m = fill.bank()
                m_full.wait(dve, b, fill.n)
                head, t = i // (NT + 1), i % (NT + 1)
                if t < NT:
                    dve.tensor_reduce(max_ctx[:, NT * head + t:NT * head + t + 1], m, AX, ALU.max)\
                       .then_inc(m_free.sem, 1)
                else:
                    dve.tensor_reduce(max_mem[:, NT * head:NT * (head + 1)],
                                      m.rearrange("p (t n) -> p t n", n=MEM), AX, ALU.max)\
                       .then_inc(m_free.sem, 1)

            def join_maxima(b, done):
                m_free.wait(dve, b, done)
                dve.tensor_tensor(mx[:], max_ctx[:], max_mem[:], ALU.max).then_inc(mx_ready.sem, 1)

            def turn_maxima(b, fill, p):
                m = fill.bank()
                m_full.wait(dve, b, fill.n)
                nm_in.wait(dve, b, 16 * p)
                dve.tensor_scalar(neg_max[:], m[0:2 * NT, 0:P], -1.0, None, ALU.mult)\
                   .then_inc(nm_ready.sem, 1)

            def normalize(b, p):
                if p:
                    norm_ready.wait(dve, b, p)
                summed.wait(dve, b, p + 1)
                dve.reciprocal(recip[:], p_sum[:]).then_inc(sum_read.sem, 1)
                sum_read.wait(dve, b, p + 1)
                o_read.wait(dve, b, p + 1)
                dve.tensor_tensor(o_norm[:, p, :], o_norm[:, p, :], recip[:], ALU.mult).then_inc(norm_ready.sem, 1)

            def turn(b, ahead):
                fill = Fill()
                freed = 0
                for p in range(PAIRS):
                    i = 0
                    for kt in range(KT1):
                        for what in steps(p, kt, ahead):
                            freed += DVE_FILLS.get(what, 0)
                            if what == "times_v" and kt == 4 and p:
                                normalize(b, p - 1)
                            elif what == "maximum":
                                maximum(b, fill, i)
                                i += 1
                                if i == PER_MAX:
                                    join_maxima(b, freed)
                            elif what == "turn":
                                turn_maxima(b, fill, p + 1)
                            elif what == "value":
                                values(b, fill, p // 2 + 1, kt - 3)
                            elif what == "rows":
                                turned_rows(b, fill)
                            elif what in FILLS:
                                fill.bank()
                        if kt in (1, 2) and (ahead or p + 2 < PAIRS):
                            split(b, p + 2, kt - 1)
                    if ahead and p == PAIRS - 5:
                        begin_norm(b)
                    if ahead and p == PAIRS - 4:
                        end_norm(b)
                if ahead:
                    for half in range(2):
                        values(b, fill, 4, half)
                normalize(b, PAIRS - 1)
                xb = x_all[:, bass.ds(b * NT, NT), :]
                biased.wait(dve, b, 1)
                for t in range(NT):
                    m = fill.bank()
                    m_full.wait(dve, b, fill.n)
                    dve.tensor_tensor(xb[:, t, :], xb[:, t, :], m[:, 0:D], ALU.add).then_inc(m_free.sem, 1)

            fill = Fill(PER - BEFORE)
            begin_norm(-1)
            end_norm(-1)
            turned_rows(-1, fill)
            for p in range(2):
                for n in range(2):
                    fill.bank()
                    split(-1, PAIRS + p, n)
            for half in range(2):
                values(-1, fill, 4, half)
            for i in range(PER_MAX):
                maximum(-1, fill, i)
            join_maxima(-1, m_free.per)
            turn_maxima(-1, fill, PAIRS)
            with dve.Fori(0, B - 1) as b:
                turn(b, True)
            turn(B - 1, False)

        @block.tensor
        def _(pe):
            pe.wait_ge(held.loaded, held.LOADS)
            pe.wait_ge(loaded, 16 * 2)
            pe.wait_ge(consts, 1)
            pe.wait_ge(prep, 3)
            pe.wait_ge(mem_in, 16 * 3)

            class Banks(Fill):

                def __init__(self, b, start=0, freed=0):
                    super().__init__(start)
                    self.b, self.freed, self.readers = b, freed, []

                def free(self, count=m_free, n=None):
                    if len(self.readers) >= 2:
                        before, at = self.readers[-2]
                        before.wait(pe, self.b, at)
                    if n is None:
                        self.freed += 1
                        n = self.freed
                    self.readers.append((count, n))
                    return self.bank()

            def done(mm):
                mm.then_inc(m_full.sem, 1)

            def turn_rows(b, banks):
                xn_ready.wait(pe, b, 1 + 1)
                for t in range(NT):
                    m = banks.free()
                    for c in range(DC):
                        mm = pe.transpose(m[:, c * P:(c + 1) * P], xn[:, t, c * P:(c + 1) * P], ident[:])
                    done(mm)

            def project(b, banks, p, n):
                m = banks.free(hi_ready, 2 * p + n + 1)
                if p == PAIRS:
                    if n == 0:
                        m_free.wait(pe, b, banks.freed)
                    else:
                        ctx_in.wait(pe, b, 16 + 16)
                w, src = ((wq, xn_t), (wk, ctx_t))[n]
                at = P * (p % PAIRS)
                for c in range(DC):
                    mm = pe.matmul(m, w[:, c, at:at + P], src[:, c, :], start=(c == 0), stop=(c == DC - 1))
                done(mm)

            def values(b, banks, group, half):
                m = banks.free()
                at = 2 * P * (group % 4)
                for i in range(2):
                    t = 2 * half + i
                    for c in range(DC):
                        mm = pe.matmul(m[:, 2 * P * i:2 * P * (i + 1)], ctx_t[:, c, P * t:P * (t + 1)],
                                       wv[:, c, at:at + 2 * P], start=(c == 0), stop=(c == DC - 1))
                done(mm)

            def maximum(b, banks, p, i):
                head, t = i // (NT + 1), i % (NT + 1)
                s = 2 * (p % HELD) + head
                m = banks.free()
                if i == 0:
                    stacked.wait(pe, b, 16 * 6 * (p + 1))
                if t < NT:
                    done(pe.matmul(m, q_hh[:, s, P * t:P * (t + 1)], k_hl[:, s, :], start=True, stop=True))
                else:
                    for t in range(NT):
                        mm = pe.matmul(m[:, MEM * t:MEM * (t + 1)], q_hh[:, s, P * t:P * (t + 1)],
                                       mem_hl[:, head, p % PAIRS, :], start=True, stop=True)
                    done(mm)

            def turn_maxima(b, banks, p):
                m = banks.free(nm_ready, p + 1)
                mx_ready.wait(pe, b, p + 1)
                done(pe.transpose(m[0:2 * NT, 0:P], mx[:], ident[:]))

            def score(b, p, kt, i):
                n = KT1 * p + kt
                if kt == 0 and i == 0:
                    nm_in.wait(pe, b, 16 * (p + 1))
                if n >= 2 and i == 0:
                    exp_done.wait(pe, b, n - 1)
                s = 2 * (p % HELD) + i
                if kt < NT:
                    first, second = (t[:, s, P * kt:P * (kt + 1)] for t in (k_hl, k_h1))
                else:
                    first, second = (t[:, i, p, :] for t in (mem_hl, mem_h1))
                pe.matmul(p_s[:, n % 2, i, :], first, q_hh[:, s, :], start=True, stop=False)
                mm = pe.matmul(p_s[:, n % 2, i, :], second, q_lm[:, s, :], start=False, stop=True)
                if i == 1:
                    mm.then_inc(s_full.sem, 1)

            def times_v(b, p, kt):
                exp_done.wait(pe, b, KT1 * p + kt + 1)
                if kt == 0 and p:
                    o_read.wait(pe, b, p)
                for i in range(2):
                    if kt < NT:
                        vh = v[:, p // 2 % 2, kt, P * (p % 2) + DK * i:P * (p % 2) + DK * (i + 1)]
                    else:
                        vh = mem_v[:, P * p + DK * i:P * p + DK * (i + 1)]
                    mm = pe.matmul(p_o[DK * i:DK * (i + 1), :], vh, probs[:, kt, i, :],
                                   start=(kt == 0), stop=(kt == KT1 - 1))
                mm.then_inc(pv_done.sem, 1)

            def total(b, p):
                tile_added.wait(pe, b, NT * (p + 1))
                if p:
                    sum_read.wait(pe, b, p)
                for i in range(2):
                    mm = pe.matmul(p_sum[DK * i:DK * (i + 1), :], ones[:], probs[:, NT, i, :], start=True, stop=True)
                mm.then_inc(summed.sem, 1)

            def turn(b, ahead):
                m_free.wait(pe, b, 0)
                nm_ready.wait(pe, b, 1)
                banks = Banks(b)
                for p in range(PAIRS):
                    i = 0
                    for kt in range(KT1):
                        head = 0
                        for what in steps(p, kt, ahead):
                            if what in ("query", "key"):
                                project(b, banks, p + 2, ("query", "key").index(what))
                            elif what == "maximum":
                                maximum(b, banks, p + 1, i)
                                i += 1
                            elif what == "turn":
                                turn_maxima(b, banks, p + 1)
                            elif what == "score":
                                score(b, p, kt, head)
                                head += 1
                            elif what == "times_v" and kt:
                                times_v(b, p, kt - 1)
                            elif what == "times_v" and p:
                                times_v(b, p - 1, KT1 - 1)
                            elif what == "value":
                                values(b, banks, p // 2 + 1, kt - 3)
                            elif what == "total" and p:
                                total(b, p - 1)
                            elif what == "rows":
                                turn_rows(b, banks)
                times_v(b, PAIRS - 1, KT1 - 1)
                if ahead:
                    for half in range(2):
                        values(b, banks, 4, half)
                total(b, PAIRS - 1)
                for t in range(NT):
                    m = banks.free()
                    if t == 0:
                        norm_ready.wait(pe, b, PAIRS)
                    for p in range(PAIRS):
                        mm = pe.matmul(m[:, 0:D], o_norm[:, p, P * t:P * (t + 1)], wo[:, p, :],
                                       start=(p == 0), stop=(p == PAIRS - 1))
                    done(mm)
                assert not ahead or (banks.n == m_full.per and banks.freed == m_free.per)

            banks = Banks(-1, m_full.per - BEFORE, m_free.per - DVE_BEFORE)
            turn_rows(-1, banks)
            for p in range(2):
                for n in range(2):
                    project(-1, banks, PAIRS + p, n)
            for half in range(2):
                values(-1, banks, 4, half)
            for i in range(PER_MAX):
                maximum(-1, banks, PAIRS, i)
            turn_maxima(-1, banks, PAIRS)
            with pe.Fori(0, B - 1) as b:
                turn(b, True)
            turn(B - 1, False)


def feed_forward1(nc, x_all, A, held):
    with ExitStack() as ctx:
        def sb(name, shape, dt=F32):
            return ctx.enter_context(nc.sbuf_tensor("f1_" + name, shape, dt))

        def ps(name, shape, dt=F32):
            return ctx.enter_context(nc.psum_tensor("f1_" + name, shape, dt))

        def sem(name):
            return ctx.enter_context(nc.semaphore("f1_" + name))

        BLOCKS = NLIN // 2
        quant = sb("quant", [P, NLIN, DC, D], I32)
        scale = sb("scale", [P, NLIN, DC, D])
        lora_a, lora_b = sb("lora_a", [LR, NLIN, D]), sb("lora_b", [LR, NLIN, D])
        w = sb("w", [P, NLIN, DC, D])
        bias = sb("bias", [P, NLIN, D])
        gamma, beta = sb("gamma", [P, BLOCKS, DC]), sb("beta", [P, BLOCKS, DC])
        ident = sb("ident", [P, P])
        minus_half = sb("minus_half", [P, NT])
        h = sb("h", [P, B, NT, D])
        h_t = sb("h_t", [P, B, DC, S])
        y = sb("y", [P, B, NT, D])
        y_t = sb("y_t", [P, B, DC, S])
        stats = sb("stats", [P, B, NT, 6])
        mean_var = sb("mean_var", [P, B, NT, 2])
        rstd = sb("rstd", [P, B, NT])

        p_t = ps("p_t", [P, 2, DC, S])
        p_y = ps("p_y", [P, 2, NT, D])

        STEPS = [(blk, second, u) for blk in range(BLOCKS) for second in range(2) for u in range(B)]
        FIRST_LOADS, LOADS = 16 * 4, 16 * 5
        cleared, consts, first_in, loaded = sem("cleared"), sem("consts"), sem("first_in"), sem("loaded")
        dequant, lora_full, w_ready = sem("dequant"), sem("lora_full"), sem("w_ready")
        stats_done, rstd_ready = sem("stats_done"), sem("rstd_ready")
        h_ready, y_ready = sem("h_ready"), sem("y_ready")
        t_full, t_read, lin_full, lin_read = sem("t_full"), sem("t_read"), sem("lin_full"), sem("lin_read")
        biased, joined, stored = sem("biased"), sem("joined"), sem("stored")
        block = ctx.enter_context(nc.Block())

        def norms_before(blk, u):
            return B * (blk + 1) + u

        @block.sync
        def _(sp):
            for dst, src in ((lora_a[:], A["f1_la"]), (lora_b[:], A["f1_lb"]), (quant[:, 0], A["f1_q"][:, 0]),
                             (scale[:, 0], A["f1_scale"][:, 0])):
                sp.dma_start(dst, src).then_inc(first_in, 16)
            sp.dma_start(bias[:].rearrange("p l d -> p (l d)"), A["f1_bias"].partition_broadcast(P)).then_inc(loaded, 16)
            for dst, src in ((gamma[:], A["f1_gamma"]), (beta[:], A["f1_beta"]), (quant[:, 1:], A["f1_q"][:, 1:]),
                             (scale[:, 1:], A["f1_scale"][:, 1:])):
                sp.dma_start(dst, src).then_inc(loaded, 16)
            for u in range(B):
                sp.wait_ge(lin_read, len(STEPS) - B + u + 1)
                sp.dma_start(A["out"][u].rearrange("(t p) d -> p t d", p=P),
                             x_all[:, u * NT:(u + 1) * NT, :]).then_inc(stored, 16)
            sp.wait_ge(stored, 16 * B)

        @block.gpsimd
        def _(pool):
            pool.memset(ident[:], 0.0)
            pool.memset(minus_half[:], -0.5).then_inc(cleared, 1)
            pool.wait_ge(cleared, 1)
            pool.affine_select(out=ident[:], in_=ident[:], compare_op=ALU.not_equal, fill=1.0, base=0,
                               pattern=[[-1, P]], channel_multiplier=1).then_inc(consts, 1)

            def invert_deviation(blk, u):
                pool.wait_ge(stats_done, 3 * norms_before(blk, u) + 3)
                pool.tensor_tensor(rstd[:, u, :], rstd[:, u, :], minus_half[:], ALU.pow).then_inc(rstd_ready, 1)

            def add_bias(blk, u):
                pool.wait_ge(t_full, 2 * B * blk + u + 1)
                pool.tensor_tensor(h[:, u], h[:, u], bias[:, 2 * blk + 1, :].unsqueeze(1).broadcast_to([P, NT, D]),
                                   ALU.add).then_inc(biased, 1)

            for u in range(B):
                invert_deviation(-1, u)
            pool.wait_ge(loaded, LOADS)
            for blk in range(BLOCKS):
                for u in range(B):
                    add_bias(blk, u)
                    if u:
                        invert_deviation(blk, u - 1)
                invert_deviation(blk, B - 1)
            for u in range(B):
                pool.wait_ge(biased, B * (BLOCKS - 1) + u + 1)
                xu = x_all[:, u * NT:(u + 1) * NT, :]
                pool.tensor_tensor(xu, xu, h[:, u], ALU.add).then_inc(joined, 1)

        @block.scalar
        def _(act):
            act.wait_ge(loaded, LOADS)
            for k, (blk, second, u) in enumerate(STEPS):
                act.wait_ge(t_full, k + 1)
                for c in range(DC):
                    if second:
                        last = act.activation(y_t[:, u, c, :], p_t[:, k % 2, c, :], ACT.Gelu,
                                              bias=beta[:, blk, c:c + 1], scale=gamma[:, blk, c:c + 1])
                    else:
                        last = act.activation(h_t[:, u, c, :], p_t[:, k % 2, c, :], ACT.Copy)
                last.then_inc(t_read, 1)

        @block.vector
        def _(dve):
            def measure(blk, u, src):
                n = 3 * norms_before(blk, u)
                for t in range(NT):
                    last = dve.bn_stats(stats[:, u, t, :], src[:, t, :])
                last.then_inc(stats_done, 1)
                dve.wait_ge(stats_done, n + 1)
                for t in range(NT):
                    last = dve.bn_aggr(mean_var[:, u, t, :], stats[:, u, t, :])
                last.then_inc(stats_done, 1)
                dve.wait_ge(stats_done, n + 2)
                dve.tensor_scalar(rstd[:, u, :], mean_var[:, u, :, 1], EPS, None, ALU.add).then_inc(stats_done, 1)

            def scale_rows(blk, u, src, dst, ready):
                dve.wait_ge(rstd_ready, norms_before(blk, u) + 1)
                for t in range(NT):
                    last = dve.tensor_scalar(dst[:, t, :], src[:, t, :], mean_var[:, u, t, 0:1],
                                             rstd[:, u, t:t + 1], ALU.subtract, ALU.mult)
                last.then_inc(ready, 1)

            def x_of(u):
                return x_all[:, u * NT:(u + 1) * NT, :]

            def dequantize(lin):
                dve.tensor_scalar(w[:, lin], quant[:, lin], 1.0 / 7.5, -1.0, ALU.mult, ALU.add).then_inc(dequant, 1)
                dve.wait_ge(dequant, 2 * lin + 1)
                dve.tensor_tensor(w[:, lin], w[:, lin], scale[:, lin], ALU.mult).then_inc(dequant, 1)
                dve.wait_ge(dequant, 2 * lin + 2)
                dve.wait_ge(lora_full, lin + 1)
                dve.tensor_tensor(w[:, lin], w[:, lin], p_y[:, lin % 2, 0:DC, :], ALU.add).then_inc(w_ready, 1)

            for u in range(B):
                measure(-1, u, x_of(u))
                if u:
                    scale_rows(-1, u - 1, x_of(u - 1), h[:, u - 1], h_ready)
            scale_rows(-1, B - 1, x_of(B - 1), h[:, B - 1], h_ready)
            dve.wait_ge(first_in, FIRST_LOADS)
            dequantize(0)
            dve.wait_ge(loaded, LOADS)
            for lin in range(1, NLIN):
                dequantize(lin)
            for k, (blk, second, u) in enumerate(STEPS):
                if not second:
                    dve.wait_ge(lin_full, k + 1)
                    dve.tensor_tensor(y[:, u], p_y[:, k % 2], bias[:, 2 * blk, :].unsqueeze(1).broadcast_to([P, NT, D]),
                                      ALU.add).then_inc(lin_read, 1)
                    dve.wait_ge(lin_read, k + 1)
                    measure(blk, u, y[:, u])
                    scale_rows(blk, u, y[:, u], y[:, u], y_ready)
                    continue
                if blk < BLOCKS - 1:
                    dve.wait_ge(biased, B * blk + u + 1)
                    into = h[:, u]
                else:
                    dve.wait_ge(joined, u + 1)
                    into = x_of(u)
                dve.wait_ge(lin_full, k + 1)
                dve.tensor_tensor(into, p_y[:, k % 2], into, ALU.add).then_inc(lin_read, 1)

        @block.tensor
        def _(pe):
            pe.wait_ge(consts, 1)
            pe.wait_ge(first_in, FIRST_LOADS)
            for lin in range(NLIN):
                if lin >= 2:
                    pe.wait_ge(w_ready, lin - 1)
                for c in range(DC):
                    mm = pe.matmul(p_y[:, lin % 2, c, :], lora_a[:, lin, P * c:P * (c + 1)], lora_b[:, lin, :],
                                   start=True, stop=True)
                mm.then_inc(lora_full, 1)

            def turn(k):
                blk, second, u = STEPS[k]
                src = (h, y)[second]
                if second:
                    pe.wait_ge(y_ready, B * blk + u + 1)
                elif blk == 0:
                    pe.wait_ge(h_ready, u + 1)
                else:
                    pe.wait_ge(lin_read, k - B + 1)
                if k >= 2:
                    pe.wait_ge(t_read, k - 1)
                for t in range(NT):
                    for c in range(DC):
                        mm = pe.transpose(p_t[:, k % 2, c, P * t:P * (t + 1)], src[:, u, t, P * c:P * (c + 1)], ident[:])
                mm.then_inc(t_full, 1)

            def linear(k):
                blk, second, u = STEPS[k]
                lin, src_t = 2 * blk + second, (h_t, y_t)[second]
                pe.wait_ge(t_read, k + 1)
                if k == 0:
                    pe.wait_ge(w_ready, NLIN)
                if k >= 2:
                    pe.wait_ge(lin_read, k - 1)
                for t in range(NT):
                    for c in range(DC):
                        mm = pe.matmul(p_y[:, k % 2, t, :], src_t[:, u, c, P * t:P * (t + 1)], w[:, lin, c, :],
                                       start=(c == 0), stop=(c == DC - 1))
                mm.then_inc(lin_full, 1)

            turn(0)
            for k in range(len(STEPS)):
                if k + 1 < len(STEPS):
                    turn(k + 1)
                linear(k)


def build(nc, A, stages):
    with ExitStack() as ctx:
        x_all = ctx.enter_context(nc.sbuf_tensor("x_all", [P, N_TILES, D], F32))
        with ExitStack() as held_ctx:
            held = Attention1Weights(nc, held_ctx)
            for stage in stages[:-1]:
                stage(nc, x_all, A, held)
        stages[-1](nc, x_all, A, None)


def lay_out(inputs):
    import numpy as np

    a = {k: np.asarray(v) for k, v in inputs.items()}

    def rows(w):
        return np.ascontiguousarray(w.reshape(-1, P, w.shape[-1]).transpose(1, 0, 2))

    out = {"x": a["x"]}
    out["ctx_t"] = np.ascontiguousarray(a["ctx_1024"].reshape(B, S, DC, P).transpose(0, 3, 2, 1))
    mask = a["mask_SxS2_bk1"]
    out["mask"] = np.ascontiguousarray(np.stack([rows(mask), rows(np.ascontiguousarray(mask.T))], axis=1))
    turned = lambda w: w.reshape(-1, 2, 8, DH0).transpose(0, 1, 3, 2).reshape(-1, D)
    out["L0_wq"] = rows(turned(a["L0_xattn_Wq"].T))
    out["L0_wk"] = rows(turned(a["L0_xattn_Wk"].T))
    wv = np.zeros((D, H0, SLOT), np.float32)
    wv[:, :, :DH0] = a["L0_xattn_Wv"].T.reshape(D, H0, DH0)
    out["L0_wv"] = rows(wv.reshape(D, H0 * SLOT))
    bv = np.zeros((H0, SLOT), np.float32)
    bv[:, :DH0] = a["L0_xattn_bv"].reshape(H0, DH0)
    bv[:, DH0] = 1.0
    out["L0_bv"] = bv.reshape(-1)
    wo = np.zeros((H0, SLOT, D), np.float32)
    wo[:, :DH0, :] = a["L0_xattn_Wo"].T.reshape(H0, DH0, D)
    out["L0_wo"] = rows(wo.reshape(H0 * SLOT, D))
    out["L0_bo"] = a["L0_xattn_bo"]
    out["L0_bqk"] = np.ascontiguousarray(
        np.stack([turned(a["L0_xattn_bq"]).reshape(2, P), turned(a["L0_xattn_bk"]).reshape(2, P)]).transpose(2, 0, 1))
    out["L0_wr"] = rows(a["L0_ffn_Wr"])
    out["L0_br"] = a["L0_ffn_br"]
    out["L0_w1"] = np.ascontiguousarray(a["L0_ffn_W1"].reshape(E, DC, P, FF).transpose(0, 2, 1, 3))
    out["L0_b1"] = np.ascontiguousarray(a["L0_ffn_b1"].reshape(E, FC, P).transpose(0, 2, 1))
    out["L0_w2"] = np.ascontiguousarray(a["L0_ffn_W2"].reshape(E, FC, P, D).transpose(0, 2, 1, 3))
    out["L0_b2"] = np.ascontiguousarray(np.broadcast_to(a["L0_ffn_b2"][:, None, :], (E, P, D)))
    paired = lambda w: w.reshape(-1, PAIRS, 2, DK).transpose(0, 1, 3, 2).reshape(-1, H1 * DK)
    for k in "qk":
        out["L1_w" + k] = rows(paired(a[f"L1_xattn_w{k}_w"]))
    out["L1_wv"] = rows(a["L1_xattn_wv_w"])
    out["L1_wo"] = rows(a["L1_xattn_wo_w"])
    out["L1_bv"], out["L1_bo"] = a["L1_xattn_wv_b"], a["L1_xattn_wo_b"]
    out["L1_bqk"] = np.ascontiguousarray(
        np.stack([paired(a["L1_xattn_wq_b"]).reshape(PAIRS, P),
                  paired(a["L1_xattn_wk_b"]).reshape(PAIRS, P)]).transpose(2, 0, 1))
    out["L1_mk"] = np.ascontiguousarray(
        paired(a["L1_xattn_mk"][0]).reshape(MEM, PAIRS, P).transpose(2, 1, 0)).reshape(P, PAIRS * MEM)
    out["L1_mv"] = a["L1_xattn_mv"].reshape(MEM, H1 * DK)
    out["f1_q"] = np.ascontiguousarray(
        a["L1_ffn_qweights"].reshape(NLIN, D, DC, P).transpose(3, 0, 2, 1))
    out["f1_scale"] = np.ascontiguousarray(
        np.repeat(a["L1_ffn_scales"], GROUP, axis=2).reshape(NLIN, D, DC, P).transpose(3, 0, 2, 1))
    out["f1_la"] = np.ascontiguousarray(a["L1_ffn_lora_a"].transpose(1, 0, 2))
    out["f1_lb"] = np.ascontiguousarray(a["L1_ffn_lora_b"].transpose(2, 0, 1))
    out["f1_bias"] = a["L1_ffn_biases"].reshape(-1)
    for k in ("gamma", "beta"):
        out["f1_" + k] = np.ascontiguousarray(a["L1_ffn_ln_" + k].reshape(NLIN // 2, DC, P).transpose(2, 0, 1))
    return out


STAGES = (attention0, mixture, attention1, feed_forward1)


def program(nc, arrays):
    A = {k: nc.dram_tensor("in_" + k, v.shape, U8 if v.dtype == bool else mybir.dt.from_np(v.dtype),
                              kind="ExternalInput").ap()
         for k, v in arrays.items()}
    A["out"] = nc.dram_tensor("out", [B, S, D], F32, kind="ExternalOutput").ap()
    for name in ("x_slots", "y_slots"):
        A[name] = nc.dram_tensor(name, [TILES * CT, D], F32, kind="Internal").ap()
    build(nc, A, STAGES)


def kernel(**inputs):
    import concourse.bacc as bacc
    from concourse.bass_utils import run_bass_kernel_spmd

    arrays = lay_out(inputs)
    nc = bacc.Bacc("TRN2", target_bir_lowering=False, num_devices=1)
    program(nc, arrays)
    result = run_bass_kernel_spmd(nc, [{"in_" + k: v for k, v in arrays.items()}], core_ids=[0])
    return result.results[0]["out"]
```
